# Optimizing a Trainium2 kernel written in Bass

```python
import numpy as np
import jax
import jax.numpy as jnp

def _softmax(x, axis=-1):
    return jax.nn.softmax(x, axis=axis)

def _gelu(x):
    return jax.nn.gelu(x, approximate=True)

def _silu(x):
    return jax.nn.silu(x)

def _sigmoid(x):
    return jax.nn.sigmoid(x)

def _layernorm(x, axis=-1, eps=1e-05):
    m = jnp.mean(x, axis=axis, keepdims=True)
    v = jnp.var(x, axis=axis, keepdims=True)
    return (x - m) / jnp.sqrt(v + eps)

def _scatter_add(tgt, idx, src, axis=0):
    return tgt.at[idx].add(src)

def _segment_sum(src, seg, n):
    return jax.ops.segment_sum(src, seg, n)
kernel_name = 'mk_gnn_resnorm_d4_gnn_r32_b99d51'

def setup_inputs(seed: int=0):
    np.random.seed(seed)
    _w = jnp.asarray

    def _rec_inputs():
        import jax
        import jax.numpy as jnp
        _gk = jax.random.key(seed)
        x = -0.0005121 + 1.001 * jax.random.normal(jax.random.fold_in(_gk, 1), (50000, 64), jnp.float32)
        src = jax.random.randint(jax.random.fold_in(_gk, 2), (50000,), 0, 50000, jnp.int32)
        dst = jax.random.randint(jax.random.fold_in(_gk, 3), (50000,), 0, 50000, jnp.int32)
        _o = jnp.argsort(dst, stable=True)
        src = src[_o]
        dst = dst[_o]
        edge_attr_2 = jax.random.uniform(jax.random.fold_in(_gk, 13), (50000, 2), jnp.float32, 0.0, 0.999999)
        edge_attr_64 = 0.000189758 + 1.00013 * jax.random.normal(jax.random.fold_in(_gk, 14), (50000, 64), jnp.float32)
        edge_weight = jax.random.uniform(jax.random.fold_in(_gk, 16), (50000,), jnp.float32, 0.0, 0.2)
        return (x, src, dst, edge_attr_2, edge_attr_64, edge_weight)
    x, src, dst, edge_attr_2, edge_attr_64, edge_weight = _rec_inputs()

    def _L0_gnn_setup():
        import jax, jax.numpy as jnp
        import numpy as np
        N_NODES = 50000
        N_EDGES = 25000
        D_NODE = 64
        HID = 64
        N_TGT = 64

        def _init_linear(key, fan_in, fan_out):
            kw, kb = jax.random.split(key)
            bound = 1.0 / np.sqrt(fan_in)
            W = jax.random.uniform(kw, (fan_in, fan_out), minval=-bound, maxval=bound, dtype=jnp.float32)
            b = jax.random.uniform(kb, (fan_out,), minval=-bound, maxval=bound, dtype=jnp.float32)
            return (W, b)
        key = jax.random.key(seed)
        ks = jax.random.split(key, 8)
        x = jax.random.normal(ks[0], (N_NODES, D_NODE), dtype=jnp.float32)
        edge_index = jax.random.randint(ks[1], (2, N_EDGES), 0, N_NODES, dtype=jnp.int64)
        edge_attr = jax.random.normal(ks[2], (N_EDGES, HID), dtype=jnp.float32)
        u = jax.random.normal(ks[3], (1, 16), dtype=jnp.float32)
        batch = jnp.zeros((N_NODES,), dtype=jnp.int64)
        W1a, b1a = _init_linear(ks[4], D_NODE + HID, HID)
        W1b, b1b = _init_linear(ks[5], HID, HID)
        W2a, b2a = _init_linear(ks[6], D_NODE + HID, HID)
        W2b, b2b = _init_linear(ks[7], HID, N_TGT)
        return {'x': x, 'edge_index': edge_index, 'edge_attr': edge_attr, 'u': u, 'batch': batch, 'W1a': W1a, 'b1a': b1a, 'W1b': W1b, 'b1b': b1b, 'W2a': W2a, 'b2a': b2a, 'W2b': W2b, 'b2b': b2b}
    _L0_gnn_all = _L0_gnn_setup()
    _L0_gnn_in = {k: v for k, v in _L0_gnn_all.items() if k in ('u', 'W1a', 'b1a', 'W1b', 'b1b', 'W2a', 'b2a', 'W2b', 'b2b')}
    del _L0_gnn_all

    def _L1_gnn_setup():
        import jax, jax.numpy as jnp
        import numpy as np
        K = 5

        def _spline_basis(pseudo):
            v = pseudo * (K - 1)
            lo = jnp.floor(v)
            frac = v - lo
            lo = lo.astype(jnp.int32)
            b = jnp.stack([1.0 - frac, frac], axis=-1)
            idx = jnp.clip(lo[..., None] + jnp.arange(2, dtype=jnp.int32), 0, K - 1)
            basis = b[:, 0, :, None] * b[:, 1, None, :]
            wi = idx[:, 0, :, None] + K * idx[:, 1, None, :]
            E = pseudo.shape[0]
            return (basis.reshape(E, 4), wi.reshape(E, 4))

        def _spline_conv(x, src, dst, pseudo, W, root, bias, num_nodes):
            basis, wi = _spline_basis(pseudo)
            xW = jnp.einsum('ni,kio->nko', x, W)
            gathered = xW[src[:, None], wi]
            msg = jnp.einsum('es,eso->eo', basis, gathered)
            agg = jax.ops.segment_max(msg, dst, num_segments=num_nodes)
            agg = jnp.where(jnp.isneginf(agg), 0.0, agg)
            return agg + x @ root + bias
        key = jax.random.key(seed)
        ks = jax.random.split(key, 12)
        N, E, C = (50000, 25000, 64)
        s = 1.0 / np.sqrt(C)
        return {'x': jax.random.normal(ks[0], (N, C), jnp.float32), 'edge_index': jax.random.randint(ks[1], (2, E), 0, N, jnp.int32), 'edge_attr': jax.random.uniform(ks[2], (E, 2), jnp.float32), 'W1': jax.random.normal(ks[3], (25, C, C), jnp.float32) * s, 'root1': jax.random.normal(ks[4], (C, C), jnp.float32) * s, 'b1': jnp.zeros((C,), jnp.float32), 'W2': jax.random.normal(ks[5], (25, C, C), jnp.float32) * s, 'root2': jax.random.normal(ks[6], (C, C), jnp.float32) * s, 'b2': jnp.zeros((C,), jnp.float32), 'final_w': jax.random.normal(ks[7], (3 * C, C), jnp.float32) / np.sqrt(3 * C), 'final_b': jnp.zeros((C,), jnp.float32)}
    _L1_gnn_all = _L1_gnn_setup()
    _L1_gnn_in = {k: v for k, v in _L1_gnn_all.items() if k in ('W1', 'root1', 'b1', 'W2', 'root2', 'b2', 'final_w', 'final_b')}
    del _L1_gnn_all

    def _L2_gnn_setup():
        import jax, jax.numpy as jnp
        import numpy as np
        N = 3125
        D = 64
        E = 31250
        L = 10
        ALPHA = 0.3
        EPS = 1e-08
        key = jax.random.key(seed)
        k1, k2, k3, k4 = jax.random.split(key, 4)
        edge_src = jax.random.randint(k1, (E,), 0, N)
        edge_dst = jax.random.randint(k2, (E,), 0, N)
        edge_vals = jax.random.uniform(k3, (E,), dtype=jnp.float32) * 0.2
        X = jax.random.normal(k4, (N, D), dtype=jnp.float32)
        l_idx = jnp.arange(L + 1, dtype=jnp.float32)
        manifold_weights = ALPHA * (1.0 - ALPHA) ** (l_idx * 1.5)
        return {'X': X, 'edge_vals': edge_vals, 'manifold_weights': manifold_weights, 'edge_src': edge_src, 'edge_dst': edge_dst}
    _L2_gnn_all = _L2_gnn_setup()
    _L2_gnn_in = {k: v for k, v in _L2_gnn_all.items() if k in ('manifold_weights',)}
    del _L2_gnn_all

    def _L3_gnn_setup():
        import jax, jax.numpy as jnp
        import numpy as np
        N_NODES = 6250
        EMBED_DIM = 64
        N_EDGES = 156250

        def _lightgcn_forward(x, edge_index):
            n = x.shape[0]
            loop = jnp.arange(n, dtype=edge_index.dtype)
            row = jnp.concatenate([edge_index[0], loop])
            col = jnp.concatenate([edge_index[1], loop])
            w = jnp.ones(row.shape[0], dtype=x.dtype)
            deg = jax.ops.segment_sum(w, row, num_segments=n)
            inv_deg = 1.0 / (deg + 1e-08)
            w = w * inv_deg[row]
            deg2 = jax.ops.segment_sum(w, row, num_segments=n)
            inv_sqrt = jnp.where(deg2 > 0, jax.lax.rsqrt(deg2 + 1e-08), 0.0)
            w = inv_sqrt[row] * w * inv_sqrt[col]
            h = jax.ops.segment_sum(w[:, None] * x[col], row, num_segments=n)
            return h
        key = jax.random.key(seed)
        k1, k2 = jax.random.split(key)
        x = jax.random.normal(k1, (N_NODES, EMBED_DIM), dtype=jnp.float32)
        edge_index = jax.random.randint(k2, (2, N_EDGES), 0, N_NODES, dtype=jnp.int64)
        return {'x': x, 'edge_index': edge_index}
    _L3_gnn_all = _L3_gnn_setup()
    _L3_gnn_in = {k: v for k, v in _L3_gnn_all.items() if k in ()}
    del _L3_gnn_all
    return {'x': x, 'src': src, 'dst': dst, 'edge_attr_2': edge_attr_2, 'edge_attr_64': edge_attr_64, 'edge_weight': edge_weight, 'L0_gnn_u': _L0_gnn_in['u'], 'L0_gnn_W1a': _L0_gnn_in['W1a'], 'L0_gnn_b1a': _L0_gnn_in['b1a'], 'L0_gnn_W1b': _L0_gnn_in['W1b'], 'L0_gnn_b1b': _L0_gnn_in['b1b'], 'L0_gnn_W2a': _L0_gnn_in['W2a'], 'L0_gnn_b2a': _L0_gnn_in['b2a'], 'L0_gnn_W2b': _L0_gnn_in['W2b'], 'L0_gnn_b2b': _L0_gnn_in['b2b'], 'L1_gnn_W1': _L1_gnn_in['W1'], 'L1_gnn_root1': _L1_gnn_in['root1'], 'L1_gnn_b1': _L1_gnn_in['b1'], 'L1_gnn_W2': _L1_gnn_in['W2'], 'L1_gnn_root2': _L1_gnn_in['root2'], 'L1_gnn_b2': _L1_gnn_in['b2'], 'L1_gnn_final_w': _L1_gnn_in['final_w'], 'L1_gnn_final_b': _L1_gnn_in['final_b'], 'L2_gnn_manifold_weights': _L2_gnn_in['manifold_weights']}

def reference(x, src, dst, edge_attr_2, edge_attr_64, edge_weight, L0_gnn_u, L0_gnn_W1a, L0_gnn_b1a, L0_gnn_W1b, L0_gnn_b1b, L0_gnn_W2a, L0_gnn_b2a, L0_gnn_W2b, L0_gnn_b2b, L1_gnn_W1, L1_gnn_root1, L1_gnn_b1, L1_gnn_W2, L1_gnn_root2, L1_gnn_b2, L1_gnn_final_w, L1_gnn_final_b, L2_gnn_manifold_weights):
    import jax
    import jax.numpy as jnp

    def _L0_gnn_ref(x, edge_index, edge_attr, u, batch, W1a, b1a, W1b, b1b, W2a, b2a, W2b, b2b):
        import jax, jax.numpy as jnp
        import numpy as np
        N_NODES = 50000
        N_EDGES = 25000
        D_NODE = 64
        HID = 64
        N_TGT = 64

        def _init_linear(key, fan_in, fan_out):
            kw, kb = jax.random.split(key)
            bound = 1.0 / np.sqrt(fan_in)
            W = jax.random.uniform(kw, (fan_in, fan_out), minval=-bound, maxval=bound, dtype=jnp.float32)
            b = jax.random.uniform(kb, (fan_out,), minval=-bound, maxval=bound, dtype=jnp.float32)
            return (W, b)
        row, col = (edge_index[0], edge_index[1])
        msg = jnp.concatenate([x[col], edge_attr], axis=1)
        msg = jnp.maximum(msg @ W1a + b1a, 0.0) @ W1b + b1b
        summed = jax.ops.segment_sum(msg, row, num_segments=x.shape[0])
        counts = jax.ops.segment_sum(jnp.ones((row.shape[0],), msg.dtype), row, num_segments=x.shape[0])
        agg = summed / jnp.maximum(counts, 1.0)[:, None]
        h = jnp.concatenate([x, agg], axis=1)
        out = jnp.maximum(h @ W2a + b2a, 0.0) @ W2b + b2b
        return out

    def _L1_gnn_ref(x, edge_index, edge_attr, W1, root1, b1, W2, root2, b2, final_w, final_b):
        import jax, jax.numpy as jnp
        import numpy as np
        K = 5

        def _spline_basis(pseudo):
            v = pseudo * (K - 1)
            lo = jnp.floor(v)
            frac = v - lo
            lo = lo.astype(jnp.int32)
            b = jnp.stack([1.0 - frac, frac], axis=-1)
            idx = jnp.clip(lo[..., None] + jnp.arange(2, dtype=jnp.int32), 0, K - 1)
            basis = b[:, 0, :, None] * b[:, 1, None, :]
            wi = idx[:, 0, :, None] + K * idx[:, 1, None, :]
            E = pseudo.shape[0]
            return (basis.reshape(E, 4), wi.reshape(E, 4))

        def _spline_conv(x, src, dst, pseudo, W, root, bias, num_nodes):
            basis, wi = _spline_basis(pseudo)
            xW = jnp.einsum('ni,kio->nko', x, W)
            gathered = xW[src[:, None], wi]
            msg = jnp.einsum('es,eso->eo', basis, gathered)
            agg = jax.ops.segment_max(msg, dst, num_segments=num_nodes)
            agg = jnp.where(jnp.isneginf(agg), 0.0, agg)
            return agg + x @ root + bias
        N = x.shape[0]
        src, dst = (edge_index[0], edge_index[1])
        x1 = jax.nn.relu(_spline_conv(x, src, dst, edge_attr, W1, root1, b1, N))
        x2 = jax.nn.relu(_spline_conv(x1, src, dst, edge_attr, W2, root2, b2, N))
        h = jnp.concatenate([x, x1, x2], axis=-1)
        return h @ final_w + final_b

    def _L2_gnn_ref(X, edge_vals, manifold_weights, edge_src, edge_dst):
        import jax, jax.numpy as jnp
        import numpy as np
        N = 3125
        D = 64
        E = 31250
        L = 10
        ALPHA = 0.3
        EPS = 1e-08
        n = X.shape[0]

        def spmm(H):
            return jax.ops.segment_sum(edge_vals[:, None] * H[edge_src], edge_dst, num_segments=n)
        H = X
        Z = manifold_weights[0] * H
        for l in range(1, L + 1):
            H = spmm(H)
            Hn = jnp.linalg.norm(H, axis=1, keepdims=True)
            H = H / (Hn + EPS) * jnp.tanh(Hn + EPS)
            Z = Z + manifold_weights[l] * H
        return Z

    def _L3_gnn_ref(x, edge_index):
        import jax, jax.numpy as jnp
        import numpy as np
        N_NODES = 6250
        EMBED_DIM = 64
        N_EDGES = 156250

        def _lightgcn_forward(x, edge_index):
            n = x.shape[0]
            loop = jnp.arange(n, dtype=edge_index.dtype)
            row = jnp.concatenate([edge_index[0], loop])
            col = jnp.concatenate([edge_index[1], loop])
            w = jnp.ones(row.shape[0], dtype=x.dtype)
            deg = jax.ops.segment_sum(w, row, num_segments=n)
            inv_deg = 1.0 / (deg + 1e-08)
            w = w * inv_deg[row]
            deg2 = jax.ops.segment_sum(w, row, num_segments=n)
            inv_sqrt = jnp.where(deg2 > 0, jax.lax.rsqrt(deg2 + 1e-08), 0.0)
            w = inv_sqrt[row] * w * inv_sqrt[col]
            h = jax.ops.segment_sum(w[:, None] * x[col], row, num_segments=n)
            return h
        return _lightgcn_forward(x, edge_index)
    edge_index = jnp.stack([src, dst])
    batch0 = jnp.zeros((50000,), jnp.int32)
    x = _layernorm(x + _L0_gnn_ref(x, edge_index, edge_attr_64, L0_gnn_u, batch0, L0_gnn_W1a, L0_gnn_b1a, L0_gnn_W1b, L0_gnn_b1b, L0_gnn_W2a, L0_gnn_b2a, L0_gnn_W2b, L0_gnn_b2b), axis=-1)
    x = _layernorm(x + _L1_gnn_ref(x, edge_index, edge_attr_2, L1_gnn_W1, L1_gnn_root1, L1_gnn_b1, L1_gnn_W2, L1_gnn_root2, L1_gnn_b2, L1_gnn_final_w, L1_gnn_final_b), axis=-1)
    x = _layernorm(x + _L2_gnn_ref(x, edge_weight, L2_gnn_manifold_weights, src, dst), axis=-1)
    x = _layernorm(x + _L3_gnn_ref(x, edge_index), axis=-1)
    return x

_drawn_inputs = setup_inputs


def setup_inputs(seed=0):
    import zlib

    import numpy as np

    out = dict(_drawn_inputs(seed))
    spreads = {'L1_gnn_b1': (0.0, 0.1), 'L1_gnn_b2': (0.0, 0.1), 'L1_gnn_final_b': (0.0, 0.1)}
    factors = {'edge_attr_64': 3.715,
     'edge_weight': 32.415,
     'L0_gnn_W1a': 2.828,
     'L0_gnn_b1a': 26.686,
     'L0_gnn_b1b': 6.063,
     'L2_gnn_manifold_weights': 8.0}
    for name, (base, spread) in spreads.items():
        noise = np.random.default_rng([zlib.crc32(name.encode()), seed]).standard_normal(out[name].shape)
        drawn = base * np.exp(spread * noise) if base else spread * noise
        out[name] = jnp.asarray(drawn.astype(out[name].dtype))
    for name, factor in factors.items():
        out[name] = (out[name] * factor).astype(out[name].dtype)
    return out
```

```python
import concourse.bass as bass
from concourse import mybir
from contextlib import ExitStack

F32 = mybir.dt.float32
F16 = mybir.dt.float16
I32 = mybir.dt.int32
ALU = mybir.AluOpType
ACT = mybir.ActivationFunctionType
AX = mybir.AxisListType

P = 128
N = 50000
D = 64
T = 7
BLK = P * T
NB = 56
H = NB // 2
NP = NB * BLK
CO = NP // P
LO = 512
HI = NP // LO
RS = NP + 1
ZROW = NP
KS = 5
NL = 10
EPS_LN = 1e-5
EPS = 1e-8
NEG = -3.0e38
RSQRT_SEED = 0x5F3759DF
UN = 8
G = UN // 2
NU = CO // UN
assert NP >= N and HI * LO == NP and CO % UN == 0


def ge(eng, sem, value):
    if isinstance(value, int) and value <= 0:
        return
    eng.wait_ge(sem, value)


def rsem(eng, sem, value, go):
    if isinstance(value, int) and value <= 0:
        return
    eng.wait_ge(sem, value)
    eng.sem_inc(go, 1)


class Order:

    def __init__(self, eng, sem):
        self.eng, self.sem, self.n = eng, sem, 0

    def did(self, ins):
        ins.then_inc(self.sem, 1)
        self.n += 1

    def done(self):
        if self.n:
            self.eng.wait_ge(self.sem, self.n)

    def restart(self):
        self.done()
        self.eng.sem_inc(self.sem, -self.n)
        self.n = 0


def steps(eng, body, last=H):
    body(0)
    with eng.Fori(1, last) as i:
        body(i)


def bc(ap, shape):
    return ap.to_broadcast(shape)


def program(nc, A, out):
    ctx = ExitStack()

    def sb(name, shape, dt=F32, c=ctx):
        return c.enter_context(nc.sbuf_tensor(name, shape, dt))

    def ps(name, shape, dt=F32, c=ctx):
        return c.enter_context(nc.psum_tensor(name, shape, dt))

    lent = []

    def sem(name):
        lent.append(nc.alloc_semaphore(name=name))
        return lent[-1]

    def sem2(name, keep=False):
        return [(kept if keep else sem)(f"{name}{u}") for u in range(2)]

    def kept(name):
        return ctx.enter_context(nc.semaphore(name))

    def end_phase():
        for s in lent:
            nc.gpsimd.sem_clear(s)
        nc.all_engine_barrier()
        for s in lent:
            nc.release_semaphore(s)
        lent.clear()

    def dram(name, shape, dt=F32):
        return nc.dram_tensor(name, shape, dt, kind="Internal").ap()

    def flat(ap):
        return ap.rearrange("(p c) -> p c", c=CO)

    def blocks(ap):
        if len(ap.shape) == 1:
            return ap.rearrange("(b p t) -> b p t", p=P, t=T)
        return ap.rearrange("(b p t) w -> b p t w", p=P, t=T)

    with ctx:
        pos_s = dram("pos_s", [NP], I32)
        pos_d = dram("pos_d", [NP], I32)
        last_s = dram("last_s", [NP], I32)
        last_d = dram("last_d", [NP], I32)
        last_d_f = dram("last_d_f", [NP])
        cnt_s = dram("cnt_s", [NP])
        r_rows = dram("r_rows", [NP, D + 2])
        rec_d = dram("rec_d", [NP, 5])
        key_sh = dram("key_sh", [2, NP + P])
        same_s = dram("same_s", [NP])
        same_d = dram("same_d", [NP])
        cut_d = dram("cut_d", [NP])
        src_d = dram("src_d", [NP], I32)
        wgt_d = dram("wgt_d", [NP])
        coef_d = dram("coef_d", [NP, 2 * KS])
        dst_s = dram("dst_s", [NP], I32)
        q_tab = dram("q_tab", [2, NP], I32)
        sum_s = dram("sum_s", [RS, D])
        x1_rows = dram("x1_rows", [NP, D + 1])
        mx_rows = dram("mx_rows", [RS, D])
        y1_rows = dram("y1_rows", [NP, D])
        x2_rows = dram("x2_rows", [NP, D])
        h_tab = [dram(f"h_tab{k}", [RS, D]) for k in range(2)]
        z_rows = dram("z_rows", [RS, D])
        x3_rows = dram("x3_rows", [NP, D])
        y3_rows = dram("y3_rows", [NP, D])
        nscale = dram("nscale", [2, NP])

        ident = sb("ident", [P, P])
        ident16 = sb("ident16", [P, P], F16)
        below = sb("below", [P, P])
        above = sb("above", [P, P])
        iota_i = sb("iota_i", [P, LO], I32)
        diag_i = sb("diag_i", [P, P], I32)
        iota_lo = sb("iota_lo", [P, LO], F16)
        zrow = sb("zrow", [P, 3 * (D + 2)])
        W1a = sb("W1a", [P, D])
        Wcat = sb("Wcat", [P, D])
        W1bT = sb("W1bT", [D, D])
        W1b = sb("W1b", [D, D + 1])
        W2lo = sb("W2lo", [D, D])
        b1bT = sb("b1bT", [D, P])
        W2b = sb("W2b", [D, D])
        root1 = sb("root1", [D, D])
        R2F = sb("R2F", [P, 2 * D])
        F2 = sb("F2", [D, D])
        spl = [sb(f"spl{n}", [P, 3, KS * D]) for n in range(2)]
        biasB = sb("biasB", [P, 7, D])
        B1A, B2A, B2B, BV, SB1, SB2, FB = range(7)
        mwB = sb("mwB", [P, NL + 1])
        mwl = sb("mwl", [P, 1])

        def bias(k):
            return biasB[:, k:k + 1, :].to_broadcast([P, T, D])

        s_boot = sem("constants_loaded")
        s_zero = sem("zero_rows_stored")
        s_pool = sem("iotas_made")
        s_vo = kept("vector_order")
        s_go = kept("waits_passed")
        s_tr = sem("setup_transposed")
        s_cp = sem("setup_copied")
        s_mm = sem("setup_multiplied")

        nload = [0]
        with nc.Block(no_gpsimd_drain=True) as block, ExitStack() as c:
            pset = ps("pset", [P, 512], F32, c)
            wl = []

            @block.sync
            def _(sp):
                def ld(dst, src):
                    sp.dma_start(dst, src).then_inc(s_boot, 16)
                    nload[0] += 16

                def zero(dst, src):
                    sp.dma_start(dst, src).then_inc(s_zero, 16)
                ld(W1a[:, :], A["W1a"])
                ld(Wcat[0:D, :], A["W2a"][0:D, :])
                ld(W2lo[:, :], A["W2a"][D:2 * D, :])
                ld(W1b[:, 0:D], A["W1b"])
                ld(W1b[:, D:D + 1], A["b1b"].rearrange("(a b) -> a b", b=1))
                ld(W2b[:, :], A["W2b"])
                ld(root1[:, :], A["root1"])
                ld(R2F[D:P, 0:D], A["root2"])
                ld(R2F[:, D:2 * D], A["final_w"][0:2 * D, :])
                ld(F2[:, :], A["final_w"][2 * D:3 * D, :])
                for n in range(2):
                    w = A[f"W{n + 1}"].rearrange("(j i) c o -> (i c) j o", i=KS)
                    for k in range(3):
                        rows = min(P, KS * D - P * k)
                        ld(spl[n][0:rows, k, :].rearrange("p (j o) -> p j o", j=KS), w[P * k:P * k + rows])
                for k, name in ((B1A, "b1a"), (B2A, "b2a"), (B2B, "b2b"), (SB1, "sb1"), (SB2, "sb2"), (FB, "final_b")):
                    ld(biasB[:, k, :], A[name].rearrange("(a n) -> a n", a=1).to_broadcast([P, D]))
                ld(mwB[:, :], A["mw"].rearrange("(a n) -> a n", a=1).to_broadcast([P, NL + 1]))
                sp.wait_ge(s_cp, 1)
                zero(sum_s[ZROW:ZROW + 1, :], zrow[0:1, 0:D])
                zero(mx_rows[ZROW:ZROW + 1, :], zrow[0:1, 0:D])
                zero(z_rows[ZROW:ZROW + 1, :], zrow[0:1, 0:D])
                for k in range(2):
                    zero(h_tab[k][ZROW:ZROW + 1, :], zrow[0:1, 0:D])
                for k in range(2):
                    zero(key_sh[k:k + 1, 0:1], zrow[0:1, 2 * D:2 * D + 1])
                sp.wait_ge(s_boot, nload[0])
                sp.wait_ge(s_zero, 7 * 16)

            @block.gpsimd
            def _(pool):
                pool.iota(iota_i[:, :], pattern=[[1, LO]], base=0, channel_multiplier=0).then_inc(s_pool, 1)
                pool.iota(diag_i[:, :], pattern=[[1, P]], base=0, channel_multiplier=-1).then_inc(s_pool, 1)

            @block.vector
            def _(dve):
                v = nc.vector
                o = Order(dve, s_vo)
                o.did(v.memset(zrow[:, :], 0.0))
                o.done()
                o.did(v.memset(zrow[:, 2 * D:2 * D + 1], -1.0))
                o.did(v.memset(R2F[0:D, 0:D], 0.0))
                o.done()
                dve.sem_inc(s_cp, 1)
                dve.wait_ge(s_pool, 2)
                o.did(v.tensor_copy(iota_lo[:, :], iota_i[:, :]))
                o.did(v.tensor_scalar(ident[:, :], diag_i[:, :], 0.0, None, ALU.is_equal))
                o.did(v.tensor_scalar(ident16[:, :], diag_i[:, :], 0.0, None, ALU.is_equal))
                o.did(v.tensor_scalar(below[:, :], diag_i[:, :], 0.0, None, ALU.is_lt))
                o.did(v.tensor_scalar(above[:, :], diag_i[:, :], 0.0, None, ALU.is_gt))
                o.restart()
                dve.sem_inc(s_cp, 1)
                dve.wait_ge(s_tr, 1)
                o.did(v.tensor_copy(W1bT[:, :], pset[0:D, 0:D]))
                o.did(v.tensor_copy(b1bT[:, :], W1b[:, D:D + 1].to_broadcast([D, P])))
                o.restart()
                dve.sem_inc(s_cp, 1)
                dve.wait_ge(s_mm, 1)
                o.did(v.tensor_copy(Wcat[D:P, :], pset[0:D, 64:128]))
                o.did(v.tensor_copy(biasB[:, BV, :], pset[:, 128:192]))
                o.restart()

            @block.tensor
            def _(pe):
                pe.wait_ge(s_boot, nload[0])
                pe.wait_ge(s_cp, 2)
                nc.tensor.transpose(pset[0:D, 0:D], W1b[:, 0:D], ident[0:D, 0:D]).then_inc(s_tr, 1)
                pe.wait_ge(s_cp, 3)
                nc.tensor.matmul(pset[0:D, 64:128], W1bT[:, :], W2lo[:, :], start=True, stop=True)
                nc.tensor.matmul(pset[:, 128:192], b1bT[:, :], W2lo[:, :], start=True, stop=True).then_inc(s_mm, 1)

        end_phase()

        def sort_by(name, key_in, pos, last, last_f, count):
            with ExitStack() as c:
                def cs(nm, shape, dt=F32):
                    return sb(f"{name}_{nm}", shape, dt, c)

                key_i = cs("key_i", [P, CO], I32)
                dig_i = cs("dig_i", [P, CO], I32)
                key_f = cs("key_f", [P, CO])
                hi_f = cs("hi_f", [P, CO])
                lo_f = cs("lo_f", [P, CO])
                pos_i = cs("pos_i", [P, CO], I32)
                oh_hi = cs("oh_hi", [P, 2 * G, HI], F16)
                oh_lo = cs("oh_lo", [P, 2 * G, LO], F16)
                hist = cs("hist", [HI, LO])
                ends = cs("ends", [HI, LO])
                start = cs("start", [HI, LO])
                base = cs("base", [HI, 1])
                last_t = cs("last_t", [HI, LO])
                last_i = cs("last_i", [HI, LO], I32)
                tab = cs("tab", [HI, 2, LO])
                hiT = cs("hiT", [HI, 2, G, P])
                keyB = cs("keyB", [P, 2, G, P])
                junk = cs("junk", [P, 2, UN, LO])
                rank = cs("rank", [P, 2, UN])
                pC = [ps(f"{name}_pC{k}", [HI, LO], F32, c) for k in range(2)]
                pL = [ps(f"{name}_pL{k}", [P, LO], F32, c) for k in range(2)]
                pH = ps(f"{name}_pH", [HI, 2, G, P], F16, c)
                pK = [ps(f"{name}_pK{k}", [P, G, P], F32, c) for k in range(2)]
                pB = pL[0]

                def ssem(nm):
                    return sem(f"{name}_{nm}")
                s_key, s_dig, s_oh, s_cnt = ssem("key_loaded"), ssem("digits"), ssem("hist_onehots"), ssem("hist_counted")
                s_row, s_base, s_st, s_init = ssem("row_totals"), ssem("bases"), ssem("starts"), ssem("table_init")
                s_oh2, s_T, s_bcst, s_tab, s_hT = ssem("onehots"), ssem("transposed"), ssem("key_spread"), ssem("table_copied"), ssem("hiT_copied")
                s_upd, s_look, s_rank, s_eq = ssem("table_updated"), ssem("looked_up"), ssem("ranked"), ssem("compared")
                s_pos, s_st2, s_out = ssem("pos_done"), ssem("last_done"), ssem("stored")

                with nc.Block(no_gpsimd_drain=True) as block:
                    @block.sync
                    def _(sp):
                        sp.dma_start(key_i[:, :], flat(key_in)).then_inc(s_key, 16)
                        sp.wait_ge(s_st2, 1)
                        node = "(h l) -> h l"
                        sp.dma_start(last.rearrange(node, l=LO), last_i[:, :]).then_inc(s_out, 16)
                        n = 16
                        if last_f is not None:
                            sp.dma_start(last_f.rearrange(node, l=LO), last_t[:, :]).then_inc(s_out, 16)
                            n += 16
                        if count is not None:
                            sp.dma_start(count.rearrange(node, l=LO), hist[:, :]).then_inc(s_out, 16)
                            n += 16
                        sp.wait_ge(s_pos, 1)
                        sp.dma_start(flat(pos), pos_i[:, :]).then_inc(s_out, 16)
                        sp.wait_ge(s_out, n + 16)

                    @block.vector
                    def _(dve):
                        v = nc.vector
                        o = Order(dve, s_vo)
                        dve.wait_ge(s_key, 16)
                        o.did(v.tensor_copy(key_f[:, :], key_i[:, :]))
                        o.did(v.tensor_scalar(dig_i[:, :], key_i[:, :], 9, None, ALU.arith_shift_right))
                        o.done()
                        o.did(v.tensor_copy(hi_f[:, :], dig_i[:, :]))
                        o.did(v.scalar_tensor_tensor(out=lo_f[:, :], in0=dig_i[:, :], scalar=-float(LO), in1=key_f[:, :],
                                                     op0=ALU.mult, op1=ALU.add))
                        o.restart()
                        dve.sem_inc(s_dig, 1)

                        def onehots(n, k, s):
                            v.tensor_scalar(oh_hi[:, k, :], iota_lo[:, 0:HI], hi_f[:, bass.ds(n, 1)], None,
                                            ALU.is_equal).then_inc(s, 1)
                            v.tensor_scalar(oh_lo[:, k, :], iota_lo[:, :], lo_f[:, bass.ds(n, 1)], None,
                                            ALU.is_equal).then_inc(s, 1)

                        def hist_step(i):
                            for k in range(UN):
                                n = i * UN + k
                                if not isinstance(n, int):
                                    dve.wait_ge(s_cnt, n - UN + 1)
                                onehots(n, k, s_oh)
                        steps(dve, hist_step, NU)

                        dve.wait_ge(s_cnt, CO + 1)
                        o.did(v.tensor_copy(hist[:, :], pC[0][:, :]))
                        o.done()
                        o.did(v.tensor_tensor_scan(ends[:, :], ones[0:HI, :], hist[:, :], 0.0, op0=ALU.mult, op1=ALU.add))
                        o.done()
                        dve.sem_inc(s_row, 1)
                        dve.wait_ge(s_base, 1)
                        o.did(v.tensor_copy(base[:, :], pB[0:HI, 0:1]))
                        o.done()
                        o.did(v.tensor_scalar(ends[:, :], ends[:, :], base[:, :], None, ALU.add))
                        o.done()
                        o.did(v.tensor_tensor(start[:, :], ends[:, :], hist[:, :], ALU.subtract))
                        o.did(v.tensor_scalar(last_t[:, :], ends[:, :], -1.0 - ZROW, None, ALU.add))
                        o.done()
                        o.did(v.tensor_scalar(junk[0:HI, 0, 0, :], hist[:, :], 0.5, None, ALU.is_gt))
                        o.done()
                        o.did(v.tensor_tensor(last_t[:, :], last_t[:, :], junk[0:HI, 0, 0, :], ALU.mult))
                        o.done()
                        o.did(v.tensor_scalar(last_t[:, :], last_t[:, :], float(ZROW), None, ALU.add))
                        o.done()
                        o.did(v.tensor_copy(last_i[:, :], last_t[:, :]))
                        o.did(v.tensor_copy(tab[:, 0, :], start[:, :]))
                        o.restart()
                        dve.sem_inc(s_st, 1)
                        dve.sem_inc(s_st2, 1)

                        def group(i, u):
                            for k in range(G):
                                n = (i * 2 + u) * G + k
                                dve.wait_ge(s_T, 2 * (i * 2 + u) + 2)
                                v.scalar_tensor_tensor(out=junk[:, 0, u * G + k, 0:(k + 1) * P],
                                                       in0=pK[u][:, 0:k + 1, :].rearrange("p k f -> p (k f)"),
                                                       scalar=key_f[:, bass.ds(n, 1)], in1=before[:, (G - 1 - k) * P:],
                                                       op0=ALU.is_equal, op1=ALU.mult,
                                                       accum_out=rank[:, 0, u * G + k:u * G + k + 1]).then_inc(s_eq, 1)
                                dve.wait_ge(s_look, n + 1)
                                v.scalar_tensor_tensor(out=junk[:, 1, u * G + k, :], in0=pL[k % 2][:, :], scalar=1.0,
                                                       in1=oh_lo[:, u * G + k, :], op0=ALU.mult, op1=ALU.mult,
                                                       accum_out=rank[:, 1, u * G + k:u * G + k + 1]).then_inc(s_rank, 1)

                        def group_onehots(i, u):
                            if not isinstance(i, int):
                                dve.wait_ge(s_upd, 2 * i + u - 1)
                            for k in range(G):
                                onehots((i * 2 + u) * G + k, u * G + k, s_oh2)

                        def sort_step(i):
                            group_onehots(i, 0)
                            group_onehots(i, 1)
                            group(i, 0)
                            group(i, 1)
                            dve.wait_ge(s_rank, (i + 1) * UN)
                            dve.wait_ge(s_eq, (i + 1) * UN)
                            o.did(v.tensor_tensor(pos_i[:, bass.ds(i * UN, UN)], rank[:, 0, :], rank[:, 1, :], ALU.add))
                            o.restart()
                        steps(dve, sort_step, NU)
                        dve.sem_inc(s_pos, 1)

                    @block.scalar
                    def _(act):
                        a = nc.scalar
                        act.wait_ge(s_dig, 1)

                        def sort_step(i):
                            for u in range(2):
                                g = i * 2 + u
                                if not isinstance(i, int):
                                    act.wait_ge(s_T, 2 * g - 2)
                                a.activation(keyB[:, u, :, :],
                                             key_f[:, bass.ds(g * G, G)].rearrange("p (k a) -> p k a", a=1)
                                             .to_broadcast([P, G, P]), ACT.Copy).then_inc(s_bcst, 1)
                                act.wait_ge(s_T, 2 * g + 2)
                                if not isinstance(i, int):
                                    act.wait_ge(s_look, (g - 1) * G)
                                a.activation(hiT[:, u, :, :], pH[:, u, :, :], ACT.Copy).then_inc(s_hT, 1)
                                act.wait_ge(s_upd, g + 1)
                                if not (isinstance(i, int) and u == 0):
                                    act.wait_ge(s_look, g * G)
                                a.activation(tab[:, 1 - u, :], pC[u][:, :], ACT.Copy).then_inc(s_tab, 1)
                        steps(act, sort_step, NU)

                    @block.tensor
                    def _(pe):
                        t = nc.tensor
                        t.matmul(pC[0][:, :], zero16[:, 0:HI], iota_lo[:, :], start=True, stop=False)

                        def hist_step(i):
                            for k in range(UN):
                                pe.wait_ge(s_oh, 2 * (i * UN + k) + 2)
                                t.matmul(pC[0][:, :], oh_hi[:, k, :], oh_lo[:, k, :], start=False,
                                         stop=False).then_inc(s_cnt, 1)
                        steps(pe, hist_step, NU)
                        t.matmul(pC[0][:, :], zero16[:, 0:HI], iota_lo[:, :], start=False, stop=True).then_inc(s_cnt, 1)
                        pe.wait_ge(s_row, 1)
                        t.matmul(pB[0:HI, 0:1], above[0:HI, 0:HI], ends[:, LO - 1:LO], start=True, stop=True).then_inc(s_base, 1)
                        pe.wait_ge(s_st, 1)

                        def sort_step(i):
                            for u in range(2):
                                g = i * 2 + u
                                pe.wait_ge(s_oh2, 2 * (g + 1) * G)
                                if not isinstance(i, int):
                                    pe.wait_ge(s_hT, g - 1)
                                    pe.wait_ge(s_eq, (g - 1) * G)
                                for k in range(G):
                                    last_t_ = t.transpose(pH[:, u, k, :], oh_hi[:, u * G + k, :], ident16[:, :])
                                last_t_.then_inc(s_T, 1)
                                pe.wait_ge(s_bcst, g + 1)
                                for k in range(G):
                                    last_t_ = t.transpose(pK[u][:, k, :], keyB[:, u, k, :], ident[:, :])
                                last_t_.then_inc(s_T, 1)
                                if not (isinstance(i, int) and u == 0):
                                    pe.wait_ge(s_tab, g)
                                t.matmul(pC[u][:, :], ident[0:HI, 0:HI], tab[:, u, :], start=True, stop=False)
                                for k in range(G):
                                    m = t.matmul(pC[u][:, :], oh_hi[:, u * G + k, :], oh_lo[:, u * G + k, :],
                                                 start=False, stop=(k == G - 1))
                                m.then_inc(s_upd, 1)
                                pe.wait_ge(s_hT, g + 1)
                                for k in range(G):
                                    n = g * G + k
                                    if not (isinstance(i, int) and u == 0 and k < 2):
                                        pe.wait_ge(s_rank, n - 1)
                                    t.matmul(pL[k % 2][:, :], hiT[:, u, k, :], tab[:, u, :], start=True,
                                             stop=True).then_inc(s_look, 1)
                        steps(pe, sort_step, NU)
            end_phase()

        with ExitStack() as c:
            ones = sb("ones", [P, LO], F32, c)
            zero16 = sb("zero16", [P, P], F16, c)
            before = sb("before", [P, G * P], F32, c)
            with nc.Block(no_gpsimd_drain=True) as block:
                @block.vector
                def _(dve):
                    o = Order(dve, s_vo)
                    o.did(nc.vector.memset(ones[:, :], 1.0))
                    o.did(nc.vector.memset(zero16[:, :], 0.0))
                    o.did(nc.vector.memset(before[:, 0:(G - 1) * P], 1.0))
                    o.did(nc.vector.tensor_copy(before[:, (G - 1) * P:], below[:, :]))
                    o.restart()
            sort_by("bysrc", A["src"], pos_s, last_s, None, cnt_s)
            sort_by("bydst", A["dst"], pos_d, last_d, last_d_f, None)

        class Shifted:

            def __init__(self, table, base):
                self.table, self.base = table, base

            def __getitem__(self, b):
                return self.table[b + self.base]

        def cols(ap, w):
            return ap.rearrange("p (t a) -> p t a", a=1).to_broadcast([P, ap.shape[1], w])

        def rsqrt(o, dst, src, scr):
            v = nc.vector
            o.did(v.tensor_scalar(scr.bitcast(I32), src.bitcast(I32), 1, None, ALU.arith_shift_right))
            o.done()
            o.did(v.tensor_scalar(dst.bitcast(I32), scr.bitcast(I32), -1.0, float(RSQRT_SEED), ALU.mult, ALU.add))
            for _ in range(3):
                o.done()
                o.did(v.tensor_tensor(scr, src, dst, ALU.mult))
                o.done()
                o.did(v.tensor_tensor(scr, scr, dst, ALU.mult))
                o.done()
                o.did(v.tensor_scalar(scr, scr, -0.5, 1.5, ALU.mult, ALU.add))
                o.done()
                o.did(v.tensor_tensor(dst, dst, scr, ALU.mult))
            o.done()

        def layernorm(o, y, sq, st, dst):
            v = nc.vector
            o.did(v.tensor_reduce(st[:, 0, :], y, AX.X, ALU.add))
            o.done()
            o.did(v.tensor_scalar(st[:, 0, :], st[:, 0, :], -1.0 / D, None, ALU.mult))
            o.done()
            o.did(v.tensor_tensor(y, y, cols(st[:, 0, :], D), ALU.add))
            o.done()
            o.did(v.tensor_tensor(sq, y, y, ALU.mult))
            o.done()
            o.did(v.tensor_reduce(st[:, 1, :], sq, AX.X, ALU.add))
            o.done()
            o.did(v.tensor_scalar(st[:, 1, :], st[:, 1, :], 1.0 / D, EPS_LN, ALU.mult, ALU.add))
            o.done()
            rsqrt(o, st[:, 2, :], st[:, 1, :], st[:, 3, :])
            return v.tensor_tensor(dst, y, cols(st[:, 2, :], D), ALU.mult)

        def gather(pool, table, idx, dst, s):
            for t in range(T):
                pool.indirect_dma_start(out=dst[:, t, :], out_offset=None, in_=table,
                                        in_offset=bass.IndirectOffsetOnAxis(ap=idx[:, t:t + 1], axis=0)).then_inc(s, 16)

        def scatter(pool, table, idx, src, s):
            for t in range(T):
                pool.indirect_dma_start(out=table, out_offset=bass.IndirectOffsetOnAxis(ap=idx[:, t:t + 1], axis=0),
                                        in_=src[:, t, :], in_offset=None).then_inc(s, 16)

        def before_b(i, u):
            return (i, 0) if u == 1 else (i - 1, 1)

        with ExitStack() as c:
            di = [sb(f"m_dst{u}", [P, T], I32, c) for u in range(2)]
            si = [sb(f"m_src{u}", [P, T], I32, c) for u in range(2)]
            pi_s = [sb(f"m_pos_s{u}", [P, T], I32, c) for u in range(2)]
            pi_d = [sb(f"m_pos_d{u}", [P, T], I32, c) for u in range(2)]
            ea = [sb(f"m_ea{u}", [P, T, 2], F32, c) for u in range(2)]
            ew = [sb(f"m_ew{u}", [P, T], F32, c) for u in range(2)]
            hb = [sb(f"m_hb{u}", [P, T, 2 * D], F32, c) for u in range(2)]
            ht = sb("m_ht", [P, T * P], F32, c)
            tmp = [sb(f"m_tmp{u}", [P, T, D], F32, c) for u in range(2)]
            rr = [sb(f"m_rr{u}", [P, T, D + 2], F32, c) for u in range(2)]
            rec = [sb(f"m_rec{u}", [P, T, 5], F32, c) for u in range(2)]
            pT = ps("m_pT", [P, 8 * P], F32, c)
            pU = [ps(f"m_pU{u}", [P, T, D], F32, c) for u in range(2)]
            s_in1, s_in2 = sem2("m_gather_inputs"), sem2("m_scatter_inputs")
            s_g, s_sc = sem2("m_gathered", keep=True), sem2("m_scattered", keep=True)
            s_T, s_ev, s_mm = sem("m_transposed"), sem("m_copied"), sem("m_multiplied")
            s_r, s_cp2, s_add = sem("m_rows_ready"), sem("m_records_ready"), sem("m_biased")
            dstb, srcb, posb, posdb = blocks(A["dst"]), blocks(A["src"]), blocks(pos_s), blocks(pos_d)
            eab, ea64b, ewb = blocks(A["ea2"]), blocks(A["ea64"]), blocks(A["ew"])
            with nc.Block(no_gpsimd_drain=True) as block:
                @block.sync
                def _(sp):
                    def load1(b, u):
                        sp.dma_start(di[u][:, :], dstb[b]).then_inc(s_in1[u], 16)
                        sp.dma_start(hb[u][:, :, D:2 * D], ea64b[b]).then_inc(s_in1[u], 16)

                    def load2(b, u):
                        sp.dma_start(si[u][:, :], srcb[b]).then_inc(s_in2[u], 16)
                        sp.dma_start(pi_s[u][:, :], posb[b]).then_inc(s_in2[u], 16)
                        sp.dma_start(pi_d[u][:, :], posdb[b]).then_inc(s_in2[u], 16)
                        sp.dma_start(ea[u][:, :, :], eab[b]).then_inc(s_in2[u], 16)
                        sp.dma_start(ew[u][:, :], ewb[b]).then_inc(s_in2[u], 16)
                    for u in range(2):
                        load1(u, u)
                        load2(u, u)
                    with sp.Fori(0, H - 1) as i:
                        for u in range(2):
                            b = 2 * i + u
                            sp.wait_ge(s_T, b + 1)
                            sp.wait_ge(s_cp2, b + 1)
                            load1(b + 2, u)
                            sp.wait_ge(s_sc[u], 2 * T * 16 * (i + 1))
                            load2(b + 2, u)

                @block.gpsimd
                def _(pool):
                    def scat(i, u):
                        rsem(pool, s_r, 2 * i + u + 1, s_go)
                        rsem(pool, s_cp2, 2 * i + u + 1, s_go)
                        scatter(pool, r_rows[:, :], pi_s[u], rr[u], s_sc[u])
                        scatter(pool, rec_d[:, :], pi_d[u], rec[u], s_sc[u])

                    def step(i):
                        for u in range(2):
                            rsem(pool, s_in1[u], 32 * (i + 1), s_go)
                            rsem(pool, s_T, 2 * i + u - 1, s_go)
                            gather(pool, A["x"][:, :], di[u], hb[u][:, :, 0:D], s_g[u])
                            if not (isinstance(i, int) and u == 0):
                                scat(*before_b(i, u))
                    steps(pool, step)
                    scat(H - 1, 1)
                    for u in range(2):
                        pool.wait_ge(s_sc[u], 2 * T * 16 * H)

                @block.tensor
                def _(pe):
                    def step(i):
                        for u in range(2):
                            b = 2 * i + u
                            pe.wait_ge(s_g[u], T * 16 * (i + 1))
                            pe.wait_ge(s_in1[u], 32 * (i + 1))
                            ge(pe, s_ev, b)
                            for t in range(T):
                                x = nc.tensor.transpose(pT[:, t * P:(t + 1) * P], hb[u][:, t, :], ident[:, :])
                            x.then_inc(s_T, 1)
                            pe.wait_ge(s_ev, b + 1)
                            ge(pe, s_add, b - 1)
                            for t in range(T):
                                x = nc.tensor.matmul(pU[u][:, t, :], ht[:, t * P:(t + 1) * P], W1a[:, :], start=True, stop=True)
                            x.then_inc(s_mm, 1)
                    steps(pe, step)

                @block.scalar
                def _(act):
                    a = nc.scalar

                    def step(i):
                        for u in range(2):
                            b = 2 * i + u
                            act.wait_ge(s_T, b + 1)
                            ge(act, s_mm, b)
                            a.activation(ht[:, :], pT[:, 0:T * P], ACT.Copy).then_inc(s_ev, 1)
                            act.wait_ge(s_in2[u], 5 * 16 * (i + 1))
                            ge(act, s_sc[u], 2 * T * 16 * i)
                            a.activation(rec[u][:, :, 0:1], si[u].rearrange("p (t a) -> p t a", a=1), ACT.Copy)
                            a.activation(rec[u][:, :, 1:3], ea[u][:, :, :], ACT.Copy)
                            a.activation(rec[u][:, :, 3:4], ew[u].rearrange("p (t a) -> p t a", a=1), ACT.Copy)
                            a.activation(rec[u][:, :, 4:5], di[u].rearrange("p (t a) -> p t a", a=1), ACT.Copy)
                            a.activation(rr[u][:, :, D:D + 1], di[u].rearrange("p (t a) -> p t a", a=1), ACT.Copy)
                            a.activation(rr[u][:, :, D + 1:D + 2], si[u].rearrange("p (t a) -> p t a", a=1),
                                         ACT.Copy).then_inc(s_cp2, 1)
                    steps(act, step)

                @block.vector
                def _(dve):
                    v = nc.vector
                    o = Order(dve, s_vo)

                    def step(i):
                        for u in range(2):
                            b = 2 * i + u
                            dve.wait_ge(s_mm, b + 1)
                            v.tensor_tensor(tmp[u][:, :, :], pU[u][:, :, :], bias(B1A), ALU.add).then_inc(s_add, 1)
                            dve.wait_ge(s_add, b + 1)
                            ge(dve, s_sc[u], 2 * T * 16 * i)
                            v.tensor_scalar(rr[u][:, :, 0:D], tmp[u][:, :, :], 0.0, None, ALU.max).then_inc(s_r, 1)
                            dve.wait_ge(s_r, b + 1)
                    steps(dve, step)

        end_phase()

        with ExitStack() as c:
            def ft(nm, w=None, dt=F32):
                return sb(f"f_{nm}", [P, CO] if w is None else [P, CO, w], dt, c)
            recs, ids = ft("recs", 5), ft("ids", 2)
            kd, ks, pd, pks = ft("kd"), ft("ks"), ft("pd"), ft("pks")
            srci, dsti = ft("srci", None, I32), ft("dsti", None, I32)
            wt, coef, t1, t2 = ft("wt"), ft("coef", 2 * KS), ft("t1"), ft("t2")
            smd, sms, cut = ft("smd"), ft("sms"), ft("cut")
            cn, deg, inv, isq = ft("cn"), ft("deg"), ft("inv"), ft("isq")
            s_ld, s_k, s_ld2, s_fin, s_w = sem("f_loaded"), sem("f_keys"), sem("f_loaded2"), sem("f_done"), sem("f_stored")
            s_kw = sem("f_keys_stored")
            with nc.Block(no_gpsimd_drain=True) as block:
                @block.sync
                def _(sp):
                    sp.dma_start(recs[:, :, :], rec_d[0:NP, :].rearrange("(p c) w -> p c w", c=CO)).then_inc(s_ld, 16)
                    sp.dma_start(ids[:, :, :], r_rows[0:NP, D:D + 2].rearrange("(p c) w -> p c w", c=CO)).then_inc(s_ld, 16)
                    sp.dma_start(cn[:, :], flat(cnt_s)).then_inc(s_ld, 16)
                    sp.wait_ge(s_k, 1)
                    sp.dma_start(flat(key_sh[0, 1:NP + 1]), kd[:, :]).then_inc(s_kw, 16)
                    sp.dma_start(flat(key_sh[1, 1:NP + 1]), ks[:, :]).then_inc(s_kw, 16)
                    sp.wait_ge(s_kw, 32)
                    sp.dma_start(pd[:, :], flat(key_sh[0, 0:NP])).then_inc(s_ld2, 16)
                    sp.dma_start(pks[:, :], flat(key_sh[1, 0:NP])).then_inc(s_ld2, 16)
                    sp.wait_ge(s_fin, 1)
                    n = 0
                    for dst, src in ((same_s, sms), (same_d, smd), (cut_d, cut), (src_d, srci), (q_tab[0], srci),
                                     (dst_s, dsti), (wgt_d, wt), (nscale[0], isq), (nscale[1], inv)):
                        sp.dma_start(flat(dst), src[:, :]).then_inc(s_w, 16)
                        n += 16
                    sp.dma_start(coef_d.rearrange("(p c) w -> p c w", c=CO), coef[:, :, :]).then_inc(s_w, 16)
                    sp.wait_ge(s_w, n + 16)

                @block.vector
                def _(dve):
                    v = nc.vector
                    o = Order(dve, s_vo)
                    dve.wait_ge(s_ld, 48)

                    def col(tile, k):
                        return tile[:, :, k:k + 1].rearrange("p c a -> p (c a)")
                    o.did(v.tensor_copy(kd[:, :], col(recs, 4)))
                    o.did(v.tensor_copy(ks[:, :], col(ids, 1)))
                    o.done()
                    dve.sem_inc(s_k, 1)
                    o.did(v.tensor_copy(srci[:, :], col(recs, 0)))
                    o.did(v.tensor_copy(dsti[:, :], col(ids, 0)))
                    o.did(v.tensor_copy(wt[:, :], col(recs, 3)))
                    for d in range(2):
                        for k in range(KS):
                            o.done()
                            o.did(v.tensor_scalar(t1[:, :], col(recs, 1 + d), -float(KS - 1), k + 1.0, ALU.mult, ALU.add))
                            o.did(v.tensor_scalar(t2[:, :], col(recs, 1 + d), float(KS - 1), 1.0 - k, ALU.mult, ALU.add))
                            o.done()
                            o.did(v.tensor_tensor(t1[:, :], t1[:, :], t2[:, :], ALU.min))
                            o.done()
                            o.did(v.tensor_scalar(col(coef, d * KS + k), t1[:, :], 0.0, None, ALU.max))
                    o.did(v.tensor_scalar(deg[:, :], cn[:, :], 1.0, None, ALU.add))
                    o.done()
                    o.did(v.tensor_scalar(t2[:, :], deg[:, :], EPS, None, ALU.add))
                    o.done()
                    o.did(v.reciprocal(inv[:, :], t2[:, :]))
                    o.done()
                    o.did(v.tensor_tensor(deg[:, :], deg[:, :], inv[:, :], ALU.mult))
                    o.done()
                    o.did(v.tensor_scalar(cn[:, :], deg[:, :], 0.0, None, ALU.is_gt))
                    o.did(v.tensor_scalar(deg[:, :], deg[:, :], EPS, None, ALU.add))
                    o.done()
                    rsqrt(o, isq[:, :], deg[:, :], t2[:, :])
                    o.did(v.tensor_tensor(isq[:, :], isq[:, :], cn[:, :], ALU.mult))
                    o.done()
                    o.did(v.tensor_tensor(inv[:, :], isq[:, :], inv[:, :], ALU.mult))
                    dve.wait_ge(s_ld2, 32)
                    o.did(v.tensor_tensor(smd[:, :], kd[:, :], pd[:, :], ALU.is_equal))
                    o.did(v.tensor_tensor(sms[:, :], ks[:, :], pks[:, :], ALU.is_equal))
                    o.done()
                    o.did(v.tensor_scalar(cut[:, :], smd[:, :], -1.0, -NEG, ALU.add, ALU.mult))
                    o.restart()
                    dve.sem_inc(s_fin, 1)

        end_phase()

        def edge_pass(name, kind, table, width, index, flags, into, sems, splw=None, rnd=None):
            i0 = 0 if rnd is None else rnd * H
            conv, rd, plain = kind == "conv", kind == "round", kind == "plain"
            with ExitStack() as c:
                def two(nm, shape, dt=F32):
                    return [sb(f"{name}_{nm}{u}", shape, dt, c) for u in range(2)]
                S = sems
                s_ix, s_fl, s_w, s_g, s_st = S["ix"], S["fl"], S["w"], S["g"], S["st"]
                s_T, s_ev, s_scan, s_bk, s_rows, s_mul = S["T"], S["ev"], S["scan"], S["bk"], S["rows"], S["mul"]
                ix = two("ix", [P, T], I32)
                g = two("g", [P, T, width])
                fl = two("fl", [D, BLK])
                sT = two("sT", [D, BLK])
                sO = two("sO", [D, BLK])
                rows = two("rows", [P, T, D])
                pT = ps(f"{name}_pT", [D, 8 * P], F32, c)
                pB = [ps(f"{name}_pB{u}", [P, T, D], F32, c) for u in range(1 if conv else 2)]
                pB = pB * 2 if conv else pB
                msg = g if kind in ("plain", "sum") else two("msg", [P, T, D])
                if conv:
                    co = two("co", [P, T, 2 * KS])
                    z = two("z", [P, T, KS, D])
                    zT = two("zT", [P, 3, P])
                    cmb = two("cmb", [P, KS, D])
                    qf = two("q", [P, T], I32)
                    pZ = [ps(f"{name}_pZ{u}", [P, 3, P], F32, c) for u in range(2)]
                    pU = [ps(f"{name}_pU{u}", [P, KS, D], F32, c) for u in range(2)]
                    s_qst = S["qst"]
                    s_z, s_zT, s_ze, s_pu, s_comb, s_q = S["z"], S["zT"], S["ze"], S["pu"], S["comb"], S["q"]
                if rd:
                    wt_ = two("w", [P, T])
                    sq = two("sq", [P, T, D])
                    st = two("st", [P, 5, T])
                    s_sq, s_nrm, s_th = S["sq"], S["nrm"], S["th"]
                flb = flags.rearrange("(b a n) -> b a n", a=1, n=BLK)
                write_q = conv and width > D

                def ready_rows(eng, ci, u):
                    if plain:
                        eng.wait_ge(s_ix[u], 16 * (ci + 1))
                    else:
                        eng.wait_ge(s_g[u], T * 16 * (ci + 1))

                with nc.Block(no_gpsimd_drain=True) as block:
                    @block.sync
                    def _(sp):
                        def load_ix(b, u):
                            if plain:
                                sp.dma_start(g[u][:, :, :], blocks(table[0:NP, :])[b]).then_inc(s_ix[u], 16)
                            else:
                                sp.dma_start(ix[u][:, :], index[b]).then_inc(s_ix[u], 16)

                        def load_fl(b, u):
                            sp.dma_start(fl[u][:, :], flb[b].to_broadcast([D, BLK])).then_inc(s_fl[u], 16)

                        def load_w(b, u):
                            if conv:
                                sp.dma_start(co[u][:, :, :], blocks(coef_d)[b]).then_inc(s_w[u], 16)
                            if rd:
                                sp.dma_start(wt_[u][:, :], blocks(wgt_d)[b]).then_inc(s_w[u], 16)

                        def store(i, u):
                            b = 2 * i + u
                            sp.wait_ge(s_rows, b + 2 * i0 + 1)
                            sp.dma_start(into(b), rows[u][:, :, :]).then_inc(s_st[u], 16)
                        def store_q(b, u):
                            sp.wait_ge(s_q, b + 1)
                            sp.dma_start(blocks(q_tab[1])[b], qf[u][:, :]).then_inc(s_qst[u], 16)

                        for u in range(2):
                            load_ix(u, u)
                            load_w(u, u)
                            load_fl(u, u)
                        with sp.Fori(0, H - 1) as i:
                            for u in range(2):
                                b = 2 * i + u
                                bb = b + 2 * i0
                                if plain:
                                    sp.wait_ge(s_T, bb + 1)
                                else:
                                    sp.wait_ge(s_g[u], T * 16 * (i + i0 + 1))
                                load_ix(b + 2, u)
                                if write_q:
                                    store_q(b, u)
                                if conv or rd:
                                    sp.wait_ge(s_mul, bb + 1)
                                    load_w(b + 2, u)
                                sp.wait_ge(s_scan, bb + 1)
                                load_fl(b + 2, u)
                                if not conv:
                                    store(i, u)
                        if write_q:
                            for u in range(2):
                                store_q(2 * (H - 1) + u, u)
                            for u in range(2):
                                sp.wait_ge(s_qst[u], 16 * H)
                        if not conv:
                            store(H - 1, 0)
                            store(H - 1, 1)
                        for u in range(2):
                            sp.wait_ge(s_st[u], 16 * (H + i0))
                        sp.sem_inc(s_go, 1)

                    if not plain:
                        @block.gpsimd
                        def _(pool):
                            def step(i):
                                for u in range(2):
                                    rsem(pool, s_ix[u], 16 * (i + i0 + 1), s_go)
                                    if not isinstance(i, int):
                                        rsem(pool, s_mul if (rd or conv) else s_T, 2 * (i + i0) + u - 1, s_go)
                                    gather(pool, table, ix[u], g[u], s_g[u])
                            steps(pool, step)

                    @block.tensor
                    def _(pe):
                        t_ = nc.tensor

                        def to_cols(i, u):
                            b = 2 * (i + i0) + u
                            if kind in ("plain", "sum"):
                                ready_rows(pe, i + i0, u)
                            else:
                                pe.wait_ge(s_mul, (b + 1) if rd else (b + 1))
                            if not (isinstance(i, int) and u == 0):
                                ge(pe, s_ev, b)
                            pe.sem_inc(s_go, 1)
                            for t in range(T):
                                x = t_.transpose(pT[:, t * P:(t + 1) * P], msg[u][:, t, 0:D], ident[:, :])
                            x.then_inc(s_T, 1)

                        def to_rows(i, u):
                            b = 2 * (i + i0) + u
                            pe.wait_ge(s_scan, b + 1)
                            if conv:
                                ge(pe, s_rows, b)
                            elif not isinstance(i, int):
                                pe.wait_ge(s_rows, b - 1)
                            pe.sem_inc(s_go, 1)
                            v3 = sO[u].rearrange("f (p t) -> f t p", t=T)
                            for t in range(T):
                                x = t_.transpose(pB[u][:, t, :], v3[:, t, :], ident[0:D, 0:D])
                            x.then_inc(s_bk, 1)

                        def spread(i, u, t):
                            n = T * (2 * i + u) + t
                            par = (u + t) % 2
                            if t == 0:
                                pe.wait_ge(s_z, 2 * i + u + 1)
                            ge(pe, s_ze, 2 * (n - 1))
                            zr = z[u].rearrange("p t i o -> p t (i o)")
                            for k in range(3):
                                w = min(P, KS * D - k * P)
                                x = t_.transpose(pZ[par][0:w, k, :], zr[:, t, k * P:k * P + w], ident[:, :])
                            x.then_inc(s_zT, 1)

                        def kernelmul(i, u, t):
                            n = T * (2 * i + u) + t
                            par = (u + t) % 2
                            pe.wait_ge(s_ze, 2 * (n + 1))
                            ge(pe, s_comb, n - 1)
                            for k in range(3):
                                w = min(P, KS * D - k * P)
                                x = t_.matmul(pU[par].rearrange("p j o -> p (j o)"), zT[par][0:w, k, :], splw[0:w, k, :],
                                              start=(k == 0), stop=(k == 2))
                            x.then_inc(s_pu, 1)

                        def step(i):
                            for u in range(2):
                                if conv:
                                    first = isinstance(i, int) and u == 0
                                    spread(i, u, 0)
                                    for t in range(1, T):
                                        spread(i, u, t)
                                        kernelmul(i, u, t - 1)
                                        if t == 2 and not first:
                                            to_cols(*before_b(i, u))
                                        if t == 4 and not isinstance(i, int):
                                            to_rows(i - 1, u)
                                    kernelmul(i, u, T - 1)
                                else:
                                    to_cols(i, u)
                                    to_rows(i, u)
                        steps(pe, step)
                        if conv:
                            to_cols(H - 1, 1)
                            to_rows(H - 1, 0)
                            to_rows(H - 1, 1)

                    @block.scalar
                    def _(act):
                        a = nc.scalar

                        def copy_cols(i, u):
                            b = 2 * (i + i0) + u
                            act.wait_ge(s_T, b + 1)
                            if not isinstance(i, int):
                                act.wait_ge(s_scan, b - 1)
                            elif conv:
                                ge(act, s_scan, b - 1)
                            a.activation(sT[u].rearrange("f (p t) -> f t p", t=T),
                                         pT[:, 0:T * P].rearrange("f (t p) -> f t p", t=T), ACT.Copy).then_inc(s_ev, 1)

                        def copy_rows(i, u):
                            b = 2 * (i + i0) + u
                            act.wait_ge(s_bk, b + 1)
                            ge(act, s_st[u], 16 * i)
                            a.activation(rows[u][:, :, :], pB[u][:, :, :], ACT.Copy).then_inc(s_rows, 1)
                            if conv:
                                act.wait_ge(s_rows, b + 1)
                                act.dma_start(into(2 * i + u), rows[u][:, :, :]).then_inc(s_st[u], 16)

                        def copy_spread(i, u, t):
                            n = T * (2 * i + u) + t
                            par = (u + t) % 2
                            act.wait_ge(s_zT, n + 1)
                            ge(act, s_pu, n - 1)
                            a.activation(zT[par][:, 0:2, :], pZ[par][:, 0:2, :], ACT.Copy).then_inc(s_ze, 1)
                            a.activation(zT[par][0:D, 2, :], pZ[par][0:D, 2, :], ACT.Copy).then_inc(s_ze, 1)

                        def step(i):
                            for u in range(2):
                                b = 2 * (i + i0) + u
                                if conv:
                                    for t in range(T):
                                        copy_spread(i, u, t)
                                        if t == 2 and not (isinstance(i, int) and u == 0):
                                            copy_cols(*before_b(i, u))
                                        if t == 4 and not isinstance(i, int):
                                            copy_rows(i - 1, u)
                                else:
                                    copy_cols(i, u)
                                    if rd:
                                        act.wait_ge(s_bk, b + 1)
                                        if not isinstance(i, int):
                                            act.wait_ge(s_nrm, b - 1)
                                        a.activation(sq[u][:, :, :], pB[u][:, :, :], ACT.Square).then_inc(s_sq, 1)
                                        act.wait_ge(s_nrm, b + 1)
                                        a.activation(st[u][:, 3, :], st[u][:, 2, :], ACT.Tanh).then_inc(s_th, 1)
                                    else:
                                        copy_rows(i, u)
                        steps(act, step)
                        if conv:
                            copy_cols(H - 1, 1)
                            copy_rows(H - 1, 0)
                            copy_rows(H - 1, 1)

                    @block.vector
                    def _(dve):
                        v = nc.vector
                        o = Order(dve, s_vo)

                        def run_over(i, u):
                            b = 2 * (i + i0) + u
                            dve.wait_ge(s_ev, b + 1)
                            dve.wait_ge(s_fl[u], 16 * (i + i0 + 1))
                            if not isinstance(i, int) or conv:
                                ge(dve, s_bk, b - 1)
                            first = isinstance(i, int) and i == 0 and u == 0
                            if not first:
                                dve.wait_ge(s_scan, b)
                            v.tensor_tensor_scan(sO[u][:, :], fl[u][:, :], sT[u][:, :],
                                                 (NEG if conv else 0.0) if first else sO[1 - u][:, BLK - 1:BLK],
                                                 op0=ALU.add if conv else ALU.mult,
                                                 op1=ALU.max if conv else ALU.add).then_inc(s_scan, 1)

                        def scale(i, u):
                            b = 2 * i + u
                            ready_rows(dve, i, u)
                            dve.wait_ge(s_w[u], 16 * (i + 1))
                            ge(dve, s_zT, T * (b - 1))
                            for k in range(KS):
                                x = v.tensor_tensor(z[u][:, :, k, :], g[u][:, :, 0:D],
                                                    co[u][:, :, k:k + 1].to_broadcast([P, T, D]), ALU.mult)
                                x.then_inc(s_z5, 1)
                            dve.wait_ge(s_z5, KS * (b + 1))
                            dve.sem_inc(s_z, 1)
                            if write_q:
                                ge(dve, s_qst[u], 16 * i)
                                o.did(v.tensor_copy(qf[u].rearrange("p (t a) -> p t a", a=1), g[u][:, :, D:D + 1]))
                                o.done()
                                dve.sem_inc(s_q, 1)

                        def combine(i, u, t):
                            n = T * (2 * i + u) + t
                            par = (u + t) % 2
                            dve.wait_ge(s_pu, n + 1)
                            ge(dve, s_cred, n - 1)
                            v.tensor_tensor(cmb[par][:, :, :], pU[par][:, :, :],
                                            co[u][:, t, KS:2 * KS].rearrange("p (j a) -> p j a", a=1)
                                            .to_broadcast([P, KS, D]), ALU.mult).then_inc(s_comb, 1)
                            dve.wait_ge(s_comb, n + 1)
                            if t == 0:
                                ge(dve, s_T, 2 * i + u - 1)
                            v.tensor_reduce(msg[u][:, t, :], cmb[par].rearrange("p j o -> p o j"), AX.X,
                                            ALU.add).then_inc(s_cred, 1)

                        def norm(i, u):
                            b = 2 * (i + i0) + u
                            dve.wait_ge(s_sq, b + 1)
                            o.did(v.tensor_reduce(st[u][:, 0, :], sq[u][:, :, :], AX.X, ALU.add))
                            o.done()
                            rsqrt(o, st[u][:, 1, :], st[u][:, 0, :], st[u][:, 2, :])
                            o.did(v.tensor_tensor(st[u][:, 1, :], st[u][:, 0, :], st[u][:, 1, :], ALU.mult))
                            o.done()
                            v.tensor_scalar(st[u][:, 2, :], st[u][:, 1, :], EPS, None, ALU.add).then_inc(s_nrm, 1)
                            dve.wait_ge(s_nrm, b + 1)
                            o.did(v.reciprocal(st[u][:, 0, :], st[u][:, 2, :]))
                            o.done()
                            dve.wait_ge(s_th, b + 1)
                            o.did(v.tensor_tensor(st[u][:, 4, :], st[u][:, 0, :], st[u][:, 3, :], ALU.mult))
                            o.done()
                            if not (isinstance(i, int) and i == 0):
                                dve.wait_ge(s_st[u], 16 * (i + i0))
                            v.tensor_tensor(rows[u][:, :, :], pB[u][:, :, :], cols(st[u][:, 4, :], D), ALU.mult).then_inc(s_rows, 1)
                            dve.wait_ge(s_rows, b + 1)
                            zb = Z[:, bass.ds((2 * i + u) * T * D, T * D)]
                            o.did(v.scalar_tensor_tensor(out=zb, in0=rows[u].rearrange("p t w -> p (t w)"), scalar=mwl[:, :],
                                                         in1=zb, op0=ALU.mult, op1=ALU.add))

                        if rd:
                            o.did(v.tensor_copy(mwl[:, :], mwB[:, bass.ds(rnd + 1, 1)]))
                            o.restart()
                        if conv:
                            s_z5, s_cred = S["z5"], S["cred"]
                            scale(0, 0)

                        def step(i):
                            for u in range(2):
                                b = 2 * (i + i0) + u
                                first = isinstance(i, int) and u == 0
                                if conv:
                                    last = False
                                    if u == 0:
                                        scale(i, 1)
                                    else:
                                        scale(i + 1, 0)
                                    for t in range(T):
                                        combine(i, u, t)
                                        if t == 4 and not first:
                                            run_over(*before_b(i, u))
                                    dve.wait_ge(s_cred, T * (b + 1))
                                    dve.sem_inc(s_mul, 1)
                                else:
                                    if rd:
                                        ready_rows(dve, i + i0, u)
                                        dve.wait_ge(s_w[u], 16 * (i + i0 + 1))
                                        if not isinstance(i, int):
                                            dve.wait_ge(s_T, b - 1)
                                        v.tensor_tensor(msg[u][:, :, :], g[u][:, :, :], cols(wt_[u][:, :], D),
                                                        ALU.mult).then_inc(s_mul, 1)
                                        if not first:
                                            norm(*before_b(i, u))
                                    run_over(i, u)
                            if rd or write_q:
                                o.restart()
                        if conv:
                            steps(dve, step, H - 1)
                            for u in range(2):
                                if u == 0:
                                    scale(H - 1, 1)
                                for t in range(T):
                                    combine(H - 1, u, t)
                                    if t == 4:
                                        run_over(*before_b(H - 1, u))
                                dve.wait_ge(s_cred, T * (2 * (H - 1) + u + 1))
                                dve.sem_inc(s_mul, 1)
                            run_over(H - 1, 1)
                            if write_q:
                                o.restart()
                        else:
                            steps(dve, step)
                            if rd:
                                norm(H - 1, 1)
                                o.restart()

        def edge_semaphores(name, kind):
            S = {k: sem2(f"{name}_{k}_") for k in ("ix", "fl", "w", "st")}
            S["g"] = sem2(f"{name}_g_", keep=True)
            S.update({k: sem(f"{name}_{k}") for k in ("T", "ev", "scan", "bk", "rows", "mul")})
            if kind == "conv":
                S.update({k: sem(f"{name}_{k}") for k in ("z", "zT", "ze", "pu", "comb", "q", "z5", "cred")})
                S["qst"] = sem2(f"{name}_qst_")
            if kind == "round":
                S.update({k: sem(f"{name}_{k}") for k in ("sq", "nrm", "th")})
            return S
        def node_pass(name, table, index, loads, into):
            mats = name in ("net0", "conv1", "conv2")
            second = name in ("net0", "conv2")
            with ExitStack() as c:
                def two(nm, shape, dt=F32):
                    return [sb(f"n_{name}_{nm}{u}", shape, dt, c) for u in range(2)]
                s_ix, s_in, s_st = [sem2(f"n_{name}_{x}") for x in ("index", "inputs", "stored")]
                s_g = sem2(f"n_{name}_node_gathered", keep=True)
                s_s1, s_T1, s_e1, s_m1, s_used, s_s2, s_T2, s_e2, s_m2, s_fin = [
                    sem(f"n_{name}_{x}") for x in ("stage1", "transposed1", "copied1", "multiplied1", "rows_used", "stage2",
                                                 "transposed2", "copied2", "multiplied2", "finished")]
                ix = two("ix", [P, T], I32)
                ga = two("ga", [P, T, D])
                buf = {"o": two("o", [P, T, D + 1 if name == "net0" else D])}
                widths = {"hb": 2 * D, "xr": D, "yr": D}
                for k in sorted({x[0] for x in loads}):
                    buf[k] = two(k, [P, T, widths[k]] if k in widths else [P, T])
                if name == "z":
                    buf["o2"] = two("o2", [P, T, D])
                t1, t2, y = two("t1", [P, T, D]), two("t2", [P, T, D]), two("y", [P, T, D])
                st = two("st", [P, 4, T])
                k1 = 2 * D if name != "conv1" else D
                n1 = 2 * D if name == "conv2" else D
                if mats:
                    x1T = sb(f"n_{name}_x1T", [k1, T * P], F32, c)
                    pT = ps(f"n_{name}_pT", [P, 8 * P], F32, c)
                    pU = [ps(f"n_{name}_pU{u}", [P, 8, n1], F32, c) for u in range(2)]
                if second:
                    x2T = sb(f"n_{name}_x2T", [D, T * P], F32, c)
                    pV = ps(f"n_{name}_pV", [P, T, D], F32, c)

                with nc.Block(no_gpsimd_drain=True) as block:
                    @block.sync
                    def _(sp):
                        def load_in(b, u):
                            for k, src, cut in loads:
                                dst = buf[k][u]
                                dst = dst[:, :] if cut is None else dst[:, :, cut]
                                sp.dma_start(dst, src(b)).then_inc(s_in[u], 16)

                        def store(b, u):
                            sp.wait_ge(s_fin, b + 1)
                            for k, dst in into:
                                sp.dma_start(dst(b), buf[k][u][:, :, :]).then_inc(s_st[u], 16)
                        for u in range(2):
                            sp.dma_start(ix[u][:, :], index[u]).then_inc(s_ix[u], 16)
                            load_in(u, u)
                        with sp.Fori(0, H - 1) as i:
                            for u in range(2):
                                b = 2 * i + u
                                sp.wait_ge(s_g[u], T * 16 * (i + 1))
                                sp.dma_start(ix[u][:, :], index[b + 2]).then_inc(s_ix[u], 16)
                                store(b, u)
                                load_in(b + 2, u)
                        for u in range(2):
                            store(2 * (H - 1) + u, u)
                        for u in range(2):
                            sp.wait_ge(s_st[u], 16 * len(into) * H)

                    @block.gpsimd
                    def _(pool):
                        def step(i):
                            for u in range(2):
                                rsem(pool, s_ix[u], 16 * (i + 1), s_go)
                                rsem(pool, s_used, 2 * i + u - 1, s_go)
                                gather(pool, table, ix[u], ga[u], s_g[u])
                        steps(pool, step)

                    if mats:
                        w1, w2 = {"net0": (Wcat, W2b), "conv1": (root1, None), "conv2": (R2F, F2)}[name]

                        @block.tensor
                        def _(pe):
                            t_ = nc.tensor

                            def step(i):
                                for u in range(2):
                                    b = 2 * i + u
                                    pe.wait_ge(s_in[u], 16 * len(loads) * (i + 1))
                                    if name == "net0":
                                        pe.wait_ge(s_s1, b + 1)
                                    ge(pe, s_e2 if second else s_e1, b)
                                    pe.sem_inc(s_go, 1)
                                    src = buf["hb"][u] if "hb" in buf else buf["xr"][u]
                                    for t in range(T):
                                        x = t_.transpose(pT[0:k1, t * P:(t + 1) * P], src[:, t, 0:k1], ident[:, :])
                                    x.then_inc(s_T1, 1)
                                    pe.wait_ge(s_e1, b + 1)
                                    ge(pe, s_fin, b - 1)
                                    for t in range(T):
                                        x = t_.matmul(pU[u][:, t, :], x1T[:, t * P:(t + 1) * P], w1[:, :], start=True, stop=True)
                                    x.then_inc(s_m1, 1)
                                    if second:
                                        pe.wait_ge(s_s2, b + 1)
                                        pe.sem_inc(s_go, 1)
                                        for t in range(T):
                                            x = t_.transpose(pT[0:D, t * P:(t + 1) * P], t2[u][:, t, :], ident[:, :])
                                        x.then_inc(s_T2, 1)
                                        pe.wait_ge(s_e2, b + 1)
                                        ge(pe, s_fin, b)
                                        for t in range(T):
                                            x = t_.matmul(pV[:, t, :], x2T[:, t * P:(t + 1) * P], w2[:, :], start=True, stop=True)
                                        x.then_inc(s_m2, 1)
                            steps(pe, step)

                        @block.scalar
                        def _(act):
                            def step(i):
                                for u in range(2):
                                    b = 2 * i + u
                                    act.wait_ge(s_T1, b + 1)
                                    ge(act, s_m1, b)
                                    nc.scalar.activation(x1T[:, :], pT[0:k1, 0:T * P], ACT.Copy).then_inc(s_e1, 1)
                                    if second:
                                        act.wait_ge(s_T2, b + 1)
                                        ge(act, s_m2, b)
                                        nc.scalar.activation(x2T[:, :], pT[0:D, 0:T * P], ACT.Copy).then_inc(s_e2, 1)
                            steps(act, step)

                    @block.vector
                    def _(dve):
                        v = nc.vector
                        o = Order(dve, s_vo)

                        def arrived(i, u):
                            dve.wait_ge(s_g[u], T * 16 * (i + 1))
                            dve.wait_ge(s_in[u], 16 * len(loads) * (i + 1))

                        def out_free(i, u):
                            ge(dve, s_st[u], 16 * len(into) * i)

                        def stage1(i, u):
                            b = 2 * i + u
                            arrived(i, u)
                            cn, sc = buf["cnt"][u], st[u]
                            o.done()
                            o.did(v.tensor_scalar(sc[:, 0, :], cn[:, :], 1.0, None, ALU.max))
                            o.done()
                            o.did(v.reciprocal(sc[:, 1, :], sc[:, 0, :]))
                            o.done()
                            o.did(v.tensor_tensor(buf["hb"][u][:, :, D:2 * D], ga[u][:, :, :], cols(sc[:, 1, :], D), ALU.mult))
                            o.done()
                            dve.sem_inc(s_s1, 1)
                            dve.sem_inc(s_used, 1)

                        def stage2(i, u):
                            b = 2 * i + u
                            arrived(i, u)
                            o.done()
                            if name == "net0":
                                o.did(v.tensor_scalar(st[u][:, 0, :], buf["cnt"][u][:, :], 1.0, None, ALU.min))
                                o.done()
                                o.did(v.tensor_tensor(t1[u][:, :, :], bias(BV), cols(st[u][:, 0, :], D), ALU.mult))
                                o.done()
                                o.did(v.tensor_tensor(t1[u][:, :, :], t1[u][:, :, :], bias(B2A), ALU.add))
                            else:
                                o.did(v.tensor_tensor(t1[u][:, :, :], ga[u][:, :, :], bias(SB1 if name == "conv1" else SB2), ALU.add))
                            o.done()
                            if name != "net0":
                                dve.sem_inc(s_used, 1)
                            dve.wait_ge(s_m1, b + 1)
                            o.did(v.tensor_tensor(t1[u][:, :, :], t1[u][:, :, :], pU[u][:, 0:T, 0:D], ALU.add))
                            o.done()
                            if name == "conv1":
                                out_free(i, u)
                                v.tensor_scalar(buf["o"][u][:, :, :], t1[u][:, :, :], 0.0, None, ALU.max).then_inc(s_fin, 1)
                            else:
                                o.did(v.tensor_scalar(t2[u][:, :, :], t1[u][:, :, :], 0.0, None, ALU.max))
                                o.done()
                                dve.sem_inc(s_s2, 1)

                        def stage3(i, u):
                            b = 2 * i + u
                            yy = y[u][:, :, :]
                            o.done()
                            if second:
                                dve.wait_ge(s_m2, b + 1)
                                if name == "net0":
                                    o.did(v.tensor_tensor(yy, buf["hb"][u][:, :, 0:D], pV[:, :, :], ALU.add))
                                else:
                                    o.did(v.tensor_tensor(yy, buf["hb"][u][:, :, 0:D], pU[u][:, 0:T, D:2 * D], ALU.add))
                                    o.done()
                                    o.did(v.tensor_tensor(yy, yy, pV[:, :, :], ALU.add))
                                o.done()
                                o.did(v.tensor_tensor(yy, yy, bias(B2B if name == "net0" else FB), ALU.add))
                            elif name == "z":
                                arrived(i, u)
                                xr = buf["xr"][u].rearrange("p t w -> p (t w)")
                                o.did(v.scalar_tensor_tensor(out=y[u].rearrange("p t w -> p (t w)"), in0=xr, scalar=mwB[:, 0:1],
                                                             in1=ga[u].rearrange("p t w -> p (t w)"), op0=ALU.mult, op1=ALU.add))
                                o.done()
                                dve.sem_inc(s_used, 1)
                                o.did(v.tensor_tensor(yy, yy, buf["xr"][u][:, :, :], ALU.add))
                            else:
                                arrived(i, u)
                                o.did(v.tensor_tensor(yy, ga[u][:, :, :], buf["yr"][u][:, :, :], ALU.add))
                                o.done()
                                dve.sem_inc(s_used, 1)
                                o.did(v.tensor_tensor(yy, yy, cols(buf["sc"][u][:, :], D), ALU.mult))
                                o.done()
                                o.did(v.tensor_tensor(yy, yy, buf["xr"][u][:, :, :], ALU.add))
                            o.done()
                            out_free(i, u)
                            last = layernorm(o, yy, t1[u][:, :, :], st[u], buf["o"][u][:, :, 0:D])
                            if name == "net0":
                                o.did(last)
                                o.did(v.tensor_copy(buf["o"][u][:, :, D:D + 1], buf["ldf"][u].rearrange("p (t a) -> p t a", a=1)))
                                o.done()
                                dve.sem_inc(s_fin, 1)
                            elif name == "z":
                                o.did(last)
                                o.done()
                                o.did(v.tensor_tensor(buf["o2"][u][:, :, :], buf["o"][u][:, :, :], cols(buf["sc"][u][:, :], D), ALU.mult))
                                o.done()
                                dve.sem_inc(s_fin, 1)
                            else:
                                o.did(last)
                                o.done()
                                dve.sem_inc(s_fin, 1)

                        def step(i):
                            for u in range(2):
                                if name == "net0":
                                    stage1(i, u)
                                if second and not (isinstance(i, int) and u == 0):
                                    stage3(*before_b(i, u))
                                if mats:
                                    stage2(i, u)
                                if not mats:
                                    stage3(i, u)
                            o.restart()
                        steps(dve, step)
                        if second:
                            stage3(H - 1, 1)
                            o.restart()
            end_phase()

        idx_src_d, idx_dst_s = blocks(src_d), blocks(dst_s)
        lst_s, lst_d = blocks(last_s), blocks(last_d)
        all_c, left = slice(0, D), slice(0, D)
        edge_pass("sum0", "plain", r_rows, D + 2, None, same_s, lambda b: blocks(sum_s[0:NP, :])[b],
                  edge_semaphores("sum0", "plain"))
        end_phase()
        node_pass("net0", sum_s[:, :], lst_s,
                  [("hb", lambda b: blocks(A["x"])[b], slice(0, D)), ("cnt", lambda b: blocks(cnt_s)[b], None),
                   ("ldf", lambda b: blocks(last_d_f)[b], None)],
                  [("o", lambda b: blocks(x1_rows)[b])])
        edge_pass("conv1", "conv", x1_rows[:, :], D + 1, idx_src_d, cut_d, lambda b: blocks(mx_rows[0:NP, :])[b],
                  edge_semaphores("conv1", "conv"), splw=spl[0])
        end_phase()
        node_pass("conv1", mx_rows[:, :], lst_d, [("xr", lambda b: blocks(x1_rows)[b][:, :, 0:D], slice(0, D))],
                  [("o", lambda b: blocks(y1_rows)[b])])
        edge_pass("conv2", "conv", y1_rows[:, :], D, idx_src_d, cut_d, lambda b: blocks(mx_rows[0:NP, :])[b],
                  edge_semaphores("conv2", "conv"), splw=spl[1])
        end_phase()
        node_pass("conv2", mx_rows[:, :], lst_d,
                  [("hb", lambda b: blocks(x1_rows)[b][:, :, 0:D], slice(0, D)), ("hb", lambda b: blocks(y1_rows)[b], slice(D, 2 * D))],
                  [("o", lambda b: blocks(h_tab[0][0:NP, :])[b]), ("o", lambda b: blocks(x2_rows)[b])])

        with ExitStack() as c:
            Z = sb("Z", [P, NB * T * D], F32, c)
            s_zz = sem("z_stored")
            with nc.Block(no_gpsimd_drain=True) as block:
                @block.vector
                def _(dve):
                    o = Order(dve, s_vo)
                    o.did(nc.vector.memset(Z[:, :], 0.0))
                    o.restart()

            q_blocks = blocks(q_tab.rearrange("k n -> (k n)"))
            round_sems = edge_semaphores("round", "round")
            with nc.Fori(0, NL // 2) as pair:
                for half in range(2):
                    r = pair * 2 + half
                    later = (pair + NL - 1) // NL if half == 0 else 1
                    edge_pass(f"round{half}", "round", h_tab[half][:, :], D, Shifted(q_blocks, later * NB), same_d,
                              lambda b: blocks(h_tab[1 - half][0:NP, :])[b], round_sems, rnd=r)
            with nc.Block(no_gpsimd_drain=True) as block:
                @block.sync
                def _(sp):
                    sp.dma_start(z_rows[0:NP, :].rearrange("(b p t) w -> p b (t w)", p=P, t=T),
                                 Z[:, :].rearrange("p (b n) -> p b n", b=NB)).then_inc(s_zz, 16)
                    sp.wait_ge(s_zz, 16)
        end_phase()
        node_pass("z", z_rows[:, :], lst_d,
                  [("xr", lambda b: blocks(x2_rows)[b], slice(0, D)), ("sc", lambda b: blocks(nscale[0])[b], None)],
                  [("o", lambda b: blocks(x3_rows)[b]), ("o2", lambda b: blocks(y3_rows)[b])])
        edge_pass("sum3", "sum", y3_rows[:, :], D, idx_dst_s, same_s, lambda b: blocks(sum_s[0:NP, :])[b],
                  edge_semaphores("sum3", "sum"))
        end_phase()
        node_pass("out", sum_s[:, :], lst_s,
                  [("xr", lambda b: blocks(x3_rows)[b], slice(0, D)), ("yr", lambda b: blocks(y3_rows)[b], slice(0, D)),
                   ("sc", lambda b: blocks(nscale[1])[b], None)],
                  [("o", lambda b: blocks(out)[b])])


_INS = {'x': 'x', 'src': 'src', 'dst': 'dst', 'edge_attr_2': 'ea2', 'edge_attr_64': 'ea64', 'edge_weight': 'ew',
        'L0_gnn_W1a': 'W1a', 'L0_gnn_b1a': 'b1a', 'L0_gnn_W1b': 'W1b', 'L0_gnn_b1b': 'b1b', 'L0_gnn_W2a': 'W2a',
        'L0_gnn_b2a': 'b2a', 'L0_gnn_W2b': 'W2b', 'L0_gnn_b2b': 'b2b', 'L1_gnn_W1': 'W1', 'L1_gnn_root1': 'root1',
        'L1_gnn_b1': 'sb1', 'L1_gnn_W2': 'W2', 'L1_gnn_root2': 'root2', 'L1_gnn_b2': 'sb2',
        'L1_gnn_final_w': 'final_w', 'L1_gnn_final_b': 'final_b', 'L2_gnn_manifold_weights': 'mw'}


def kernel(**inputs):
    import numpy as _np
    import concourse.bacc as _bacc
    from concourse import mybir as _mybir
    from concourse.bass_utils import run_bass_kernel_spmd as _run

    nc = _bacc.Bacc("TRN2", target_bir_lowering=False, num_devices=1)
    arrays, args = {}, {}
    for name, short in _INS.items():
        a = _np.ascontiguousarray(inputs[name])
        if a.shape[0] == N:
            pad = _np.full((NP,) + a.shape[1:], N if a.dtype.kind in "iu" else 0, a.dtype)
            pad[:N] = a
            a = pad
        arrays[f"in_{short}"] = a
        args[short] = nc.dram_tensor(f"in_{short}", a.shape, _mybir.dt.from_np(a.dtype), kind="ExternalInput").ap()
    out = nc.dram_tensor("out_0", (NP, D), F32, kind="ExternalOutput").ap()
    program(nc, args, out)
    r = _run(nc, [arrays], core_ids=[0])
    return r.results[0]["out_0"][:N]
```

```python
import concourse.bass as bass
from concourse import mybir
from contextlib import ExitStack

F32 = mybir.dt.float32
F16 = mybir.dt.float16
I32 = mybir.dt.int32
ALU = mybir.AluOpType
ACT = mybir.ActivationFunctionType
AX = mybir.AxisListType

P = 128
N = 50000
D = 64
T = 7
BLK = P * T
NB = 56
H = NB // 2
NP = NB * BLK
TR = 14
TN = 2 * T
CO = NP // P
LO = 512
HI = NP // LO
RS = NP + 1
ZROW = NP
KS = 5
NL = 10
EPS_LN = 1e-5
EPS = 1e-8
NEG = -3.0e38
RSQRT_SEED = 0x5F3759DF
UN = 8
G = UN // 2
NU = CO // UN
assert NP >= N and HI * LO == NP and CO % UN == 0


def ge(eng, sem, value):
    if isinstance(value, int) and value <= 0:
        return
    eng.wait_ge(sem, value)


def rsem(eng, sem, value, go):
    if isinstance(value, int) and value <= 0:
        return
    eng.wait_ge(sem, value)
    eng.sem_inc(go, 1)


class Order:

    def __init__(self, eng, sem):
        self.eng, self.sem, self.n = eng, sem, 0

    def did(self, ins):
        ins.then_inc(self.sem, 1)
        self.n += 1

    def done(self):
        if self.n:
            self.eng.wait_ge(self.sem, self.n)

    def restart(self):
        if not self.n:
            return
        self.done()
        self.eng.sem_inc(self.sem, -self.n)
        self.n = 0


def steps(eng, body, last=H):
    body(0)
    with eng.Fori(1, last) as i:
        body(i)


def bc(ap, shape):
    return ap.to_broadcast(shape)


def program(nc, A, out):
    ctx = ExitStack()

    def sb(name, shape, dt=F32, c=ctx):
        return c.enter_context(nc.sbuf_tensor(name, shape, dt))

    def ps(name, shape, dt=F32, c=ctx):
        return c.enter_context(nc.psum_tensor(name, shape, dt))

    lent = []

    def sem(name):
        lent.append(nc.alloc_semaphore(name=name))
        return lent[-1]

    def sem2(name, keep=False):
        return [(kept if keep else sem)(f"{name}{u}") for u in range(2)]

    def kept(name):
        return ctx.enter_context(nc.semaphore(name))

    def end_phase():
        for s in lent:
            nc.gpsimd.sem_clear(s)
        nc.all_engine_barrier()
        for s in lent:
            nc.release_semaphore(s)
        lent.clear()

    def dram(name, shape, dt=F32):
        return nc.dram_tensor(name, shape, dt, kind="Internal").ap()

    def flat(ap):
        return ap.rearrange("(p c) -> p c", c=CO)

    def blocks(ap, T=T):
        if len(ap.shape) == 1:
            return ap.rearrange("(b p t) -> b p t", p=P, t=T)
        return ap.rearrange("(b p t) w -> b p t w", p=P, t=T)

    with ctx:
        pos_s = dram("pos_s", [NP], I32)
        pos_d = dram("pos_d", [NP], I32)
        last_s = dram("last_s", [NP], I32)
        last_d = dram("last_d", [NP], I32)
        last_d_f = dram("last_d_f", [NP])
        cnt_s = dram("cnt_s", [NP])
        r_rows = dram("r_rows", [NP, D + 2])
        rec_d = dram("rec_d", [NP, 5])
        key_sh = dram("key_sh", [2, NP + P])
        same_s = dram("same_s", [NP])
        same_d = dram("same_d", [NP])
        cut_d = dram("cut_d", [NP])
        src_d = dram("src_d", [NP], I32)
        wgt_d = dram("wgt_d", [NP])
        coef_d = [dram(f"coef_d{k}", [NP, KS]) for k in range(2)]
        dst_s = dram("dst_s", [NP], I32)
        q_tab = dram("q_tab", [2, NP], I32)
        sum_s = dram("sum_s", [RS, D])
        x1_rows = dram("x1_rows", [NP, D + 1])
        mx_rows = dram("mx_rows", [RS, D])
        y1_rows = dram("y1_rows", [NP, D])
        x2_rows = dram("x2_rows", [NP, D])
        h_tab = [dram(f"h_tab{k}", [RS, D]) for k in range(2)]
        z_rows = dram("z_rows", [RS, D])
        x3_rows = dram("x3_rows", [NP, D])
        y3_rows = dram("y3_rows", [NP, D])
        has_s = dram("has_s", [NP])
        nscale = dram("nscale", [2, NP])

        ident = sb("ident", [P, P])
        ident16 = sb("ident16", [P, P], F16)
        below = sb("below", [P, P])
        above = sb("above", [P, P])
        iota_i = sb("iota_i", [P, LO], I32)
        diag_i = sb("diag_i", [P, P], I32)
        iota_lo = sb("iota_lo", [P, LO], F16)
        zrow = sb("zrow", [P, 3 * (D + 2)])
        W1a = sb("W1a", [P, D])
        Wcat = sb("Wcat", [P, D])
        W1bT = sb("W1bT", [D, D])
        W1b = sb("W1b", [D, D + 1])
        W2lo = sb("W2lo", [D, D])
        b1bT = sb("b1bT", [D, P])
        W2b = sb("W2b", [D + 1, D])
        root1 = sb("root1", [D + 1, D])
        R2F = sb("R2F", [P, 2 * D])
        F2 = sb("F2", [D + 1, D])
        spl = [sb(f"spl{n}", [P, 3, KS * D]) for n in range(2)]
        b2a_rows = sb("b2a_rows", [1, T, D])
        sb2_row = sb("sb2_row", [1, D])
        ones_row = sb("ones_row", [1, P])
        bv = sb("bv", [1, D])
        biasB = sb("biasB", [P, 1, D])
        mwB = sb("mwB", [P, NL + 1])
        mwl = sb("mwl", [P, 1])

        s_boot = sem("constants_loaded")
        s_zero = sem("zero_rows_stored")
        s_pool = sem("iotas_made")
        s_vo = kept("vector_order")
        s_go = kept("waits_passed")
        s_tr = sem("setup_transposed")
        s_cp = sem("setup_copied")
        s_mm = sem("setup_multiplied")

        nload = [0]
        with nc.Block(no_gpsimd_drain=True) as block, ExitStack() as c:
            pset = ps("pset", [P, 512], F32, c)

            @block.sync
            def _(sp):
                def ld(dst, src):
                    sp.dma_start(dst, src).then_inc(s_boot, 16)
                    nload[0] += 16

                def zero(dst, src):
                    sp.dma_start(dst, src).then_inc(s_zero, 16)
                ld(W1a[:, :], A["W1a"])
                ld(Wcat[0:D, :], A["W2a"][0:D, :])
                ld(W2lo[:, :], A["W2a"][D:2 * D, :])
                ld(W1b[:, 0:D], A["W1b"])
                ld(W1b[:, D:D + 1], A["b1b"].rearrange("(a b) -> a b", b=1))
                ld(W2b[0:D, :], A["W2b"])
                ld(root1[0:D, :], A["root1"])
                ld(R2F[D:P, 0:D], A["root2"])
                ld(R2F[:, D:2 * D], A["final_w"][0:2 * D, :])
                ld(F2[0:D, :], A["final_w"][2 * D:3 * D, :])
                for n in range(2):
                    w = A[f"W{n + 1}"].rearrange("(j i) c o -> (i c) j o", i=KS)
                    for k in range(3):
                        rows = min(P, KS * D - P * k)
                        ld(spl[n][0:rows, k, :].rearrange("p (j o) -> p j o", j=KS), w[P * k:P * k + rows])
                ld(b2a_rows[:, :, :], A["b2a"].rearrange("(a b n) -> a b n", a=1, b=1).to_broadcast([1, T, D]))
                for row, name in ((sb2_row[:, :], "sb2"), (W2b[D:D + 1, :], "b2b"), (root1[D:D + 1, :], "sb1"),
                                  (F2[D:D + 1, :], "final_b")):
                    ld(row, A[name].rearrange("(a n) -> a n", a=1))
                ld(biasB[:, 0, :], A["b1a"].rearrange("(a n) -> a n", a=1).to_broadcast([P, D]))
                ld(mwB[:, :], A["mw"].rearrange("(a n) -> a n", a=1).to_broadcast([P, NL + 1]))
                sp.wait_ge(s_cp, 1)
                zero(sum_s[ZROW:ZROW + 1, :], zrow[0:1, 0:D])
                zero(mx_rows[ZROW:ZROW + 1, :], zrow[0:1, 0:D])
                zero(z_rows[ZROW:ZROW + 1, :], zrow[0:1, 0:D])
                for k in range(2):
                    zero(h_tab[k][ZROW:ZROW + 1, :], zrow[0:1, 0:D])
                for k in range(2):
                    zero(key_sh[k:k + 1, 0:1], zrow[0:1, 2 * D:2 * D + 1])
                sp.wait_ge(s_boot, nload[0])
                sp.wait_ge(s_zero, 7 * 16)

            @block.gpsimd
            def _(pool):
                pool.iota(iota_i[:, :], pattern=[[1, LO]], base=0, channel_multiplier=0).then_inc(s_pool, 1)
                pool.iota(diag_i[:, :], pattern=[[1, P]], base=0, channel_multiplier=-1).then_inc(s_pool, 1)

            @block.vector
            def _(dve):
                v = nc.vector
                o = Order(dve, s_vo)
                o.did(v.memset(zrow[:, :], 0.0))
                o.done()
                o.did(v.memset(zrow[:, 2 * D:2 * D + 1], -1.0))
                o.did(v.memset(R2F[0:D, 0:D], 0.0))
                o.did(v.memset(ones_row[:, :], 1.0))
                o.done()
                dve.sem_inc(s_cp, 1)
                dve.wait_ge(s_pool, 2)
                o.did(v.tensor_copy(iota_lo[:, :], iota_i[:, :]))
                o.did(v.tensor_scalar(ident[:, :], diag_i[:, :], 0.0, None, ALU.is_equal))
                o.did(v.tensor_scalar(ident16[:, :], diag_i[:, :], 0.0, None, ALU.is_equal))
                o.did(v.tensor_scalar(below[:, :], diag_i[:, :], 0.0, None, ALU.is_lt))
                o.did(v.tensor_scalar(above[:, :], diag_i[:, :], 0.0, None, ALU.is_gt))
                o.restart()
                dve.sem_inc(s_cp, 1)
                dve.wait_ge(s_tr, 1)
                o.did(v.tensor_copy(W1bT[:, :], pset[0:D, 0:D]))
                o.did(v.tensor_copy(b1bT[:, :], W1b[:, D:D + 1].to_broadcast([D, P])))
                o.restart()
                dve.sem_inc(s_cp, 1)
                dve.wait_ge(s_mm, 1)
                o.did(v.tensor_copy(Wcat[D:P, :], pset[0:D, 64:128]))
                o.did(v.tensor_copy(bv[:, :], pset[0:1, 128:192]))
                o.restart()
                dve.sem_inc(s_cp, 1)

            @block.tensor
            def _(pe):
                pe.wait_ge(s_boot, nload[0])
                pe.wait_ge(s_cp, 2)
                nc.tensor.transpose(pset[0:D, 0:D], W1b[:, 0:D], ident[0:D, 0:D]).then_inc(s_tr, 1)
                pe.wait_ge(s_cp, 3)
                nc.tensor.matmul(pset[0:D, 64:128], W1bT[:, :], W2lo[:, :], start=True, stop=True)
                nc.tensor.matmul(pset[:, 128:192], b1bT[:, :], W2lo[:, :], start=True, stop=True).then_inc(s_mm, 1)

        end_phase()

        def sort_by(name, key_in, pos, last, last_f, count):
            with ExitStack() as c:
                def cs(nm, shape, dt=F32):
                    return sb(f"{name}_{nm}", shape, dt, c)

                key_i = cs("key_i", [P, CO], I32)
                dig_i = cs("dig_i", [P, CO], I32)
                key_f = cs("key_f", [P, CO])
                hi_f = cs("hi_f", [P, CO])
                lo_f = cs("lo_f", [P, CO])
                pos_i = cs("pos_i", [P, CO], I32)
                oh_hi = cs("oh_hi", [P, 2 * G, HI], F16)
                oh_lo = cs("oh_lo", [P, 2 * G, LO], F16)
                hist = cs("hist", [HI, LO])
                ends = cs("ends", [HI, LO])
                start = cs("start", [HI, LO])
                base = cs("base", [HI, 1])
                last_t = cs("last_t", [HI, LO])
                last_i = cs("last_i", [HI, LO], I32)
                tab = cs("tab", [HI, 2, LO])
                hiT = cs("hiT", [HI, 2, G, P])
                keyB = cs("keyB", [P, 2, G, P])
                junk = cs("junk", [P, 2, UN, LO])
                rank = cs("rank", [P, 2, UN])
                pC = [ps(f"{name}_pC{k}", [HI, LO], F32, c) for k in range(2)]
                pL = [ps(f"{name}_pL{k}", [P, LO], F32, c) for k in range(2)]
                pH = ps(f"{name}_pH", [HI, 2, G, P], F16, c)
                pK = [ps(f"{name}_pK{k}", [P, G, P], F32, c) for k in range(2)]
                pB = pL[0]

                def ssem(nm):
                    return sem(f"{name}_{nm}")
                s_key, s_dig, s_oh, s_cnt = ssem("key_loaded"), ssem("digits"), ssem("hist_onehots"), ssem("hist_counted")
                s_row, s_base, s_st, s_init = ssem("row_totals"), ssem("bases"), ssem("starts"), ssem("table_init")
                s_oh2, s_T, s_bcst, s_tab, s_hT = ssem("onehots"), ssem("transposed"), ssem("key_spread"), ssem("table_copied"), ssem("hiT_copied")
                s_upd, s_look, s_rank, s_eq = ssem("table_updated"), ssem("looked_up"), ssem("ranked"), ssem("compared")
                s_pos, s_st2, s_out = ssem("pos_done"), ssem("last_done"), ssem("stored")

                with nc.Block(no_gpsimd_drain=True) as block:
                    @block.sync
                    def _(sp):
                        sp.dma_start(key_i[:, :], flat(key_in)).then_inc(s_key, 16)
                        sp.wait_ge(s_st2, 1)
                        node = "(h l) -> h l"
                        sp.dma_start(last.rearrange(node, l=LO), last_i[:, :]).then_inc(s_out, 16)
                        n = 16
                        if last_f is not None:
                            sp.dma_start(last_f.rearrange(node, l=LO), last_t[:, :]).then_inc(s_out, 16)
                            n += 16
                        if count is not None:
                            sp.dma_start(count.rearrange(node, l=LO), hist[:, :]).then_inc(s_out, 16)
                            n += 16
                        sp.wait_ge(s_pos, 1)
                        sp.dma_start(flat(pos), pos_i[:, :]).then_inc(s_out, 16)
                        sp.wait_ge(s_out, n + 16)

                    @block.vector
                    def _(dve):
                        v = nc.vector
                        o = Order(dve, s_vo)
                        dve.wait_ge(s_key, 16)
                        o.did(v.tensor_copy(key_f[:, :], key_i[:, :]))
                        o.did(v.tensor_scalar(dig_i[:, :], key_i[:, :], 9, None, ALU.arith_shift_right))
                        o.done()
                        o.did(v.tensor_copy(hi_f[:, :], dig_i[:, :]))
                        o.did(v.scalar_tensor_tensor(out=lo_f[:, :], in0=dig_i[:, :], scalar=-float(LO), in1=key_f[:, :],
                                                     op0=ALU.mult, op1=ALU.add))
                        o.restart()
                        dve.sem_inc(s_dig, 1)

                        def onehots(n, k, s):
                            v.tensor_scalar(oh_hi[:, k, :], iota_lo[:, 0:HI], hi_f[:, bass.ds(n, 1)], None,
                                            ALU.is_equal).then_inc(s, 1)
                            v.tensor_scalar(oh_lo[:, k, :], iota_lo[:, :], lo_f[:, bass.ds(n, 1)], None,
                                            ALU.is_equal).then_inc(s, 1)

                        def hist_step(i):
                            for k in range(UN):
                                n = i * UN + k
                                if not isinstance(n, int):
                                    dve.wait_ge(s_cnt, n - UN + 1)
                                onehots(n, k, s_oh)
                        steps(dve, hist_step, NU)

                        dve.wait_ge(s_cnt, CO + 1)
                        o.did(v.tensor_copy(hist[:, :], pC[0][:, :]))
                        o.done()
                        o.did(v.tensor_tensor_scan(ends[:, :], ones[0:HI, :], hist[:, :], 0.0, op0=ALU.mult, op1=ALU.add))
                        o.done()
                        dve.sem_inc(s_row, 1)
                        dve.wait_ge(s_base, 1)
                        o.did(v.tensor_copy(base[:, :], pB[0:HI, 0:1]))
                        o.done()
                        o.did(v.tensor_scalar(ends[:, :], ends[:, :], base[:, :], None, ALU.add))
                        o.done()
                        o.did(v.tensor_tensor(start[:, :], ends[:, :], hist[:, :], ALU.subtract))
                        o.did(v.tensor_scalar(last_t[:, :], ends[:, :], -1.0 - ZROW, None, ALU.add))
                        o.done()
                        o.did(v.tensor_scalar(junk[0:HI, 0, 0, :], hist[:, :], 0.5, None, ALU.is_gt))
                        o.done()
                        o.did(v.tensor_tensor(last_t[:, :], last_t[:, :], junk[0:HI, 0, 0, :], ALU.mult))
                        o.done()
                        o.did(v.tensor_scalar(last_t[:, :], last_t[:, :], float(ZROW), None, ALU.add))
                        o.done()
                        o.did(v.tensor_copy(last_i[:, :], last_t[:, :]))
                        o.did(v.tensor_copy(tab[:, 0, :], start[:, :]))
                        o.restart()
                        dve.sem_inc(s_st, 1)
                        dve.sem_inc(s_st2, 1)

                        def group(i, u):
                            for k in range(G):
                                n = (i * 2 + u) * G + k
                                dve.wait_ge(s_T, 2 * (i * 2 + u) + 2)
                                v.scalar_tensor_tensor(out=junk[:, 0, u * G + k, 0:(k + 1) * P],
                                                       in0=pK[u][:, 0:k + 1, :].rearrange("p k f -> p (k f)"),
                                                       scalar=key_f[:, bass.ds(n, 1)], in1=before[:, (G - 1 - k) * P:],
                                                       op0=ALU.is_equal, op1=ALU.mult,
                                                       accum_out=rank[:, 0, u * G + k:u * G + k + 1]).then_inc(s_eq, 1)
                                dve.wait_ge(s_look, n + 1)
                                v.scalar_tensor_tensor(out=junk[:, 1, u * G + k, :], in0=pL[k % 2][:, :], scalar=1.0,
                                                       in1=oh_lo[:, u * G + k, :], op0=ALU.mult, op1=ALU.mult,
                                                       accum_out=rank[:, 1, u * G + k:u * G + k + 1]).then_inc(s_rank, 1)

                        def group_onehots(i, u):
                            g = i * 2 + u
                            ge(dve, s_upd, g - 1)
                            ge(dve, s_rank, (g - 1) * G)
                            for k in range(G):
                                onehots(g * G + k, u * G + k, s_oh2)

                        def sort_step(i, more=True):
                            group_onehots(i, 1)
                            group(i, 0)
                            if more:
                                group_onehots(i + 1, 0)
                            group(i, 1)
                            dve.wait_ge(s_rank, (i + 1) * UN)
                            dve.wait_ge(s_eq, (i + 1) * UN)
                            o.did(v.tensor_tensor(pos_i[:, bass.ds(i * UN, UN)], rank[:, 0, :], rank[:, 1, :], ALU.add))
                            o.restart()
                        group_onehots(0, 0)
                        steps(dve, sort_step, NU - 1)
                        sort_step(NU - 1, more=False)
                        dve.sem_inc(s_pos, 1)

                    @block.scalar
                    def _(act):
                        a = nc.scalar
                        act.wait_ge(s_dig, 1)

                        def sort_step(i):
                            for u in range(2):
                                g = i * 2 + u
                                if not isinstance(i, int):
                                    act.wait_ge(s_T, 2 * g - 2)
                                a.activation(keyB[:, u, :, :],
                                             key_f[:, bass.ds(g * G, G)].rearrange("p (k a) -> p k a", a=1)
                                             .to_broadcast([P, G, P]), ACT.Copy).then_inc(s_bcst, 1)
                                act.wait_ge(s_T, 2 * g + 2)
                                if not isinstance(i, int):
                                    act.wait_ge(s_look, (g - 1) * G)
                                a.activation(hiT[:, u, :, :], pH[:, u, :, :], ACT.Copy).then_inc(s_hT, 1)
                                act.wait_ge(s_upd, g + 1)
                                if not (isinstance(i, int) and u == 0):
                                    act.wait_ge(s_look, g * G)
                                a.activation(tab[:, 1 - u, :], pC[u][:, :], ACT.Copy).then_inc(s_tab, 1)
                        steps(act, sort_step, NU)

                    @block.tensor
                    def _(pe):
                        t = nc.tensor
                        t.matmul(pC[0][:, :], zero16[:, 0:HI], iota_lo[:, :], start=True, stop=False)

                        def hist_step(i):
                            for k in range(UN):
                                pe.wait_ge(s_oh, 2 * (i * UN + k) + 2)
                                t.matmul(pC[0][:, :], oh_hi[:, k, :], oh_lo[:, k, :], start=False,
                                         stop=False).then_inc(s_cnt, 1)
                        steps(pe, hist_step, NU)
                        t.matmul(pC[0][:, :], zero16[:, 0:HI], iota_lo[:, :], start=False, stop=True).then_inc(s_cnt, 1)
                        pe.wait_ge(s_row, 1)
                        t.matmul(pB[0:HI, 0:1], above[0:HI, 0:HI], ends[:, LO - 1:LO], start=True, stop=True).then_inc(s_base, 1)
                        pe.wait_ge(s_st, 1)

                        def sort_step(i):
                            for u in range(2):
                                g = i * 2 + u
                                pe.wait_ge(s_oh2, 2 * (g + 1) * G)
                                if not isinstance(i, int):
                                    pe.wait_ge(s_hT, g - 1)
                                    pe.wait_ge(s_eq, (g - 1) * G)
                                for k in range(G):
                                    last_t_ = t.transpose(pH[:, u, k, :], oh_hi[:, u * G + k, :], ident16[:, :])
                                last_t_.then_inc(s_T, 1)
                                pe.wait_ge(s_bcst, g + 1)
                                for k in range(G):
                                    last_t_ = t.transpose(pK[u][:, k, :], keyB[:, u, k, :], ident[:, :])
                                last_t_.then_inc(s_T, 1)
                                if not (isinstance(i, int) and u == 0):
                                    pe.wait_ge(s_tab, g)
                                t.matmul(pC[u][:, :], ident[0:HI, 0:HI], tab[:, u, :], start=True, stop=False)
                                for k in range(G):
                                    m = t.matmul(pC[u][:, :], oh_hi[:, u * G + k, :], oh_lo[:, u * G + k, :],
                                                 start=False, stop=(k == G - 1))
                                m.then_inc(s_upd, 1)
                                pe.wait_ge(s_hT, g + 1)
                                for k in range(G):
                                    n = g * G + k
                                    if not (isinstance(i, int) and u == 0 and k < 2):
                                        pe.wait_ge(s_rank, n - 1)
                                    t.matmul(pL[k % 2][:, :], hiT[:, u, k, :], tab[:, u, :], start=True,
                                             stop=True).then_inc(s_look, 1)
                        steps(pe, sort_step, NU)
            end_phase()

        with ExitStack() as c:
            ones = sb("ones", [P, LO], F32, c)
            zero16 = sb("zero16", [P, P], F16, c)
            before = sb("before", [P, G * P], F32, c)
            with nc.Block(no_gpsimd_drain=True) as block:
                @block.vector
                def _(dve):
                    o = Order(dve, s_vo)
                    o.did(nc.vector.memset(ones[:, :], 1.0))
                    o.did(nc.vector.memset(zero16[:, :], 0.0))
                    o.did(nc.vector.memset(before[:, 0:(G - 1) * P], 1.0))
                    o.did(nc.vector.tensor_copy(before[:, (G - 1) * P:], below[:, :]))
                    o.restart()
            sort_by("bysrc", A["src"], pos_s, last_s, None, cnt_s)
            sort_by("bydst", A["dst"], pos_d, last_d, last_d_f, None)

        class Shifted:

            def __init__(self, table, base):
                self.table, self.base = table, base

            def __getitem__(self, b):
                return self.table[b + self.base]

        def cols(ap, w):
            return ap.rearrange("p (t a) -> p t a", a=1).to_broadcast([P, ap.shape[1], w])

        def rsqrt(o, dst, src, scr):
            v = nc.vector
            o.did(v.tensor_scalar(scr.bitcast(I32), src.bitcast(I32), 1, None, ALU.arith_shift_right))
            o.done()
            o.did(v.tensor_scalar(dst.bitcast(I32), scr.bitcast(I32), -1.0, float(RSQRT_SEED), ALU.mult, ALU.add))
            o.did(v.tensor_scalar(src, src, -0.5, None, ALU.mult))
            for _ in range(3):
                o.done()
                o.did(v.tensor_tensor(scr, src, dst, ALU.mult))
                o.done()
                o.did(v.tensor_tensor(scr, scr, dst, ALU.mult))
                o.done()
                o.did(v.scalar_tensor_tensor(out=dst, in0=scr, scalar=1.5, in1=dst, op0=ALU.add, op1=ALU.mult))
            o.done()

        def layernorm_start(o, y, sq, st):
            v = nc.vector
            o.did(v.tensor_reduce(st[:, 0, :], y, AX.X, ALU.add))
            o.done()
            o.did(v.tensor_scalar(st[:, 0, :], st[:, 0, :], -1.0 / D, None, ALU.mult))
            o.done()
            o.did(v.tensor_tensor(y, y, cols(st[:, 0, :], D), ALU.add))
            o.done()
            o.did(v.tensor_tensor(sq, y, y, ALU.mult))
            o.done()
            o.did(v.tensor_reduce(st[:, 1, :], sq, AX.X, ALU.add))

        def layernorm_end(o, y, st, dst):
            v = nc.vector
            o.done()
            o.did(v.tensor_scalar(st[:, 1, :], st[:, 1, :], 1.0 / D, EPS_LN, ALU.mult, ALU.add))
            o.done()
            rsqrt(o, st[:, 2, :], st[:, 1, :], st[:, 3, :])
            return v.tensor_tensor(dst, y, cols(st[:, 2, :], D), ALU.mult)

        def gather(pool, table, idx, dst, s):
            for t in range(idx.shape[1]):
                pool.indirect_dma_start(out=dst[:, t, :], out_offset=None, in_=table,
                                        in_offset=bass.IndirectOffsetOnAxis(ap=idx[:, t:t + 1], axis=0)).then_inc(s, 16)

        def scatter(pool, table, idx, src, s):
            for t in range(T):
                pool.indirect_dma_start(out=table, out_offset=bass.IndirectOffsetOnAxis(ap=idx[:, t:t + 1], axis=0),
                                        in_=src[:, t, :], in_offset=None).then_inc(s, 16)

        def before_h(i, u, h):
            return (i, u, 0) if h == 1 else (*before_b(i, u), 1)

        def before_b(i, u):
            return (i, 0) if u == 1 else (i - 1, 1)

        with ExitStack() as c:
            di = [sb(f"m_dst{u}", [P, T], I32, c) for u in range(2)]
            si = [sb(f"m_src{u}", [P, T], I32, c) for u in range(2)]
            pi_s = [sb(f"m_pos_s{u}", [P, T], I32, c) for u in range(2)]
            pi_d = [sb(f"m_pos_d{u}", [P, T], I32, c) for u in range(2)]
            ea = [sb(f"m_ea{u}", [P, T, 2], F32, c) for u in range(2)]
            ew = [sb(f"m_ew{u}", [P, T], F32, c) for u in range(2)]
            hb = [sb(f"m_hb{u}", [P, T, 2 * D], F32, c) for u in range(2)]
            ht = sb("m_ht", [P, T * P], F32, c)
            tmp = [sb(f"m_tmp{u}", [P, T, D], F32, c) for u in range(2)]
            rr = [sb(f"m_rr{u}", [P, T, D + 2], F32, c) for u in range(2)]
            rec = [sb(f"m_rec{u}", [P, T, 5], F32, c) for u in range(2)]
            pT = ps("m_pT", [P, 8 * P], F32, c)
            pU = [ps(f"m_pU{u}", [P, T, D], F32, c) for u in range(2)]
            s_in1, s_in2 = sem2("m_gather_inputs"), sem2("m_scatter_inputs")
            s_g, s_sc = sem2("m_gathered", keep=True), sem2("m_scattered", keep=True)
            s_T, s_ev, s_mm = sem("m_transposed"), sem("m_copied"), sem("m_multiplied")
            s_r, s_cp2, s_add = sem("m_rows_ready"), sem("m_records_ready"), sem("m_biased")
            dstb, srcb, posb, posdb = blocks(A["dst"]), blocks(A["src"]), blocks(pos_s), blocks(pos_d)
            eab, ea64b, ewb = blocks(A["ea2"]), blocks(A["ea64"]), blocks(A["ew"])
            with nc.Block(no_gpsimd_drain=True) as block:
                @block.sync
                def _(sp):
                    def load1(b, u):
                        sp.dma_start(di[u][:, :], dstb[b]).then_inc(s_in1[u], 16)
                        sp.dma_start(hb[u][:, :, D:2 * D], ea64b[b]).then_inc(s_in1[u], 16)

                    def load2(b, u):
                        sp.dma_start(si[u][:, :], srcb[b]).then_inc(s_in2[u], 16)
                        sp.dma_start(pi_s[u][:, :], posb[b]).then_inc(s_in2[u], 16)
                        sp.dma_start(pi_d[u][:, :], posdb[b]).then_inc(s_in2[u], 16)
                        sp.dma_start(ea[u][:, :, :], eab[b]).then_inc(s_in2[u], 16)
                        sp.dma_start(ew[u][:, :], ewb[b]).then_inc(s_in2[u], 16)
                    for u in range(2):
                        load1(u, u)
                        load2(u, u)
                    with sp.Fori(0, H - 1) as i:
                        for u in range(2):
                            b = 2 * i + u
                            sp.wait_ge(s_T, b + 1)
                            sp.wait_ge(s_cp2, b + 1)
                            load1(b + 2, u)
                            sp.wait_ge(s_sc[u], 2 * T * 16 * (i + 1))
                            load2(b + 2, u)

                @block.gpsimd
                def _(pool):
                    def scat(i, u):
                        rsem(pool, s_r, 2 * i + u + 1, s_go)
                        rsem(pool, s_cp2, 2 * i + u + 1, s_go)
                        scatter(pool, r_rows[:, :], pi_s[u], rr[u], s_sc[u])
                        scatter(pool, rec_d[:, :], pi_d[u], rec[u], s_sc[u])

                    def step(i):
                        for u in range(2):
                            rsem(pool, s_in1[u], 32 * (i + 1), s_go)
                            rsem(pool, s_T, 2 * i + u - 1, s_go)
                            gather(pool, A["x"][:, :], di[u], hb[u][:, :, 0:D], s_g[u])
                            if not (isinstance(i, int) and u == 0):
                                scat(*before_b(i, u))
                    steps(pool, step)
                    scat(H - 1, 1)
                    for u in range(2):
                        pool.wait_ge(s_sc[u], 2 * T * 16 * H)

                @block.tensor
                def _(pe):
                    def step(i):
                        for u in range(2):
                            b = 2 * i + u
                            pe.wait_ge(s_g[u], T * 16 * (i + 1))
                            pe.wait_ge(s_in1[u], 32 * (i + 1))
                            ge(pe, s_ev, b)
                            for t in range(T):
                                x = nc.tensor.transpose(pT[:, t * P:(t + 1) * P], hb[u][:, t, :], ident[:, :])
                            x.then_inc(s_T, 1)
                            pe.wait_ge(s_ev, b + 1)
                            ge(pe, s_add, b - 1)
                            for t in range(T):
                                x = nc.tensor.matmul(pU[u][:, t, :], ht[:, t * P:(t + 1) * P], W1a[:, :], start=True, stop=True)
                            x.then_inc(s_mm, 1)
                    steps(pe, step)

                @block.scalar
                def _(act):
                    a = nc.scalar

                    def step(i):
                        for u in range(2):
                            b = 2 * i + u
                            act.wait_ge(s_T, b + 1)
                            ge(act, s_mm, b)
                            a.activation(ht[:, :], pT[:, 0:T * P], ACT.Copy).then_inc(s_ev, 1)
                            act.wait_ge(s_in2[u], 5 * 16 * (i + 1))
                            ge(act, s_sc[u], 2 * T * 16 * i)
                            a.activation(rec[u][:, :, 0:1], si[u].rearrange("p (t a) -> p t a", a=1), ACT.Copy)
                            a.activation(rec[u][:, :, 1:3], ea[u][:, :, :], ACT.Copy)
                            a.activation(rec[u][:, :, 3:4], ew[u].rearrange("p (t a) -> p t a", a=1), ACT.Copy)
                            a.activation(rec[u][:, :, 4:5], di[u].rearrange("p (t a) -> p t a", a=1), ACT.Copy)
                            a.activation(rr[u][:, :, D:D + 1], di[u].rearrange("p (t a) -> p t a", a=1), ACT.Copy)
                            a.activation(rr[u][:, :, D + 1:D + 2], si[u].rearrange("p (t a) -> p t a", a=1),
                                         ACT.Copy).then_inc(s_cp2, 1)
                    steps(act, step)

                @block.vector
                def _(dve):
                    v = nc.vector
                    o = Order(dve, s_vo)

                    def step(i):
                        for u in range(2):
                            b = 2 * i + u
                            dve.wait_ge(s_mm, b + 1)
                            v.tensor_tensor(tmp[u][:, :, :], pU[u][:, :, :], biasB[:, 0:1, :].to_broadcast([P, T, D]), ALU.add).then_inc(s_add, 1)
                            dve.wait_ge(s_add, b + 1)
                            ge(dve, s_sc[u], 2 * T * 16 * i)
                            v.tensor_scalar(rr[u][:, :, 0:D], tmp[u][:, :, :], 0.0, None, ALU.max).then_inc(s_r, 1)
                            dve.wait_ge(s_r, b + 1)
                    steps(dve, step)

        end_phase()

        with ExitStack() as c:
            def ft(nm, w=None, dt=F32):
                return sb(f"f_{nm}", [P, CO] if w is None else [P, CO, w], dt, c)
            recs, ids = ft("recs", 5), ft("ids", 2)
            kd, ks, pd, pks = ft("kd"), ft("ks"), ft("pd"), ft("pks")
            srci, dsti = ft("srci", None, I32), ft("dsti", None, I32)
            wt, coef, t1, t2 = ft("wt"), [ft(f"coef{k}", KS) for k in range(2)], ft("t1"), ft("t2")
            smd, sms, cut = ft("smd"), ft("sms"), ft("cut")
            cn, deg, inv, isq, has = ft("cn"), ft("deg"), ft("inv"), ft("isq"), ft("has")
            s_ld, s_k, s_ld2, s_fin, s_w = sem("f_loaded"), sem("f_keys"), sem("f_loaded2"), sem("f_done"), sem("f_stored")
            s_kw = sem("f_keys_stored")
            with nc.Block(no_gpsimd_drain=True) as block:
                @block.sync
                def _(sp):
                    sp.dma_start(recs[:, :, :], rec_d[0:NP, :].rearrange("(p c) w -> p c w", c=CO)).then_inc(s_ld, 16)
                    sp.dma_start(ids[:, :, :], r_rows[0:NP, D:D + 2].rearrange("(p c) w -> p c w", c=CO)).then_inc(s_ld, 16)
                    sp.dma_start(cn[:, :], flat(cnt_s)).then_inc(s_ld, 16)
                    sp.wait_ge(s_k, 1)
                    sp.dma_start(flat(key_sh[0, 1:NP + 1]), kd[:, :]).then_inc(s_kw, 16)
                    sp.dma_start(flat(key_sh[1, 1:NP + 1]), ks[:, :]).then_inc(s_kw, 16)
                    sp.wait_ge(s_kw, 32)
                    sp.dma_start(pd[:, :], flat(key_sh[0, 0:NP])).then_inc(s_ld2, 16)
                    sp.dma_start(pks[:, :], flat(key_sh[1, 0:NP])).then_inc(s_ld2, 16)
                    sp.wait_ge(s_fin, 1)
                    n = 0
                    for dst, src in ((same_s, sms), (same_d, smd), (cut_d, cut), (src_d, srci), (q_tab[0], srci),
                                     (dst_s, dsti), (wgt_d, wt), (has_s, has), (nscale[0], isq), (nscale[1], inv)):
                        sp.dma_start(flat(dst), src[:, :]).then_inc(s_w, 16)
                        n += 16
                    for k in range(2):
                        sp.dma_start(coef_d[k].rearrange("(p c) w -> p c w", c=CO), coef[k][:, :, :]).then_inc(s_w, 16)
                    sp.wait_ge(s_w, n + 2 * 16)

                @block.vector
                def _(dve):
                    v = nc.vector
                    o = Order(dve, s_vo)
                    dve.wait_ge(s_ld, 48)

                    def col(tile, k):
                        return tile[:, :, k:k + 1].rearrange("p c a -> p (c a)")
                    o.did(v.tensor_copy(kd[:, :], col(recs, 4)))
                    o.did(v.tensor_copy(ks[:, :], col(ids, 1)))
                    o.done()
                    dve.sem_inc(s_k, 1)
                    o.did(v.tensor_copy(srci[:, :], col(recs, 0)))
                    o.did(v.tensor_copy(dsti[:, :], col(ids, 0)))
                    o.did(v.tensor_copy(wt[:, :], col(recs, 3)))
                    for d in range(2):
                        for k in range(KS):
                            o.done()
                            o.did(v.tensor_scalar(t1[:, :], col(recs, 1 + d), -float(KS - 1), k + 1.0, ALU.mult, ALU.add))
                            o.did(v.tensor_scalar(t2[:, :], col(recs, 1 + d), float(KS - 1), 1.0 - k, ALU.mult, ALU.add))
                            o.done()
                            o.did(v.tensor_tensor(t1[:, :], t1[:, :], t2[:, :], ALU.min))
                            o.done()
                            o.did(v.tensor_scalar(col(coef[d], k), t1[:, :], 0.0, None, ALU.max))
                    o.did(v.tensor_scalar(has[:, :], cn[:, :], 1.0, None, ALU.min))
                    o.did(v.tensor_scalar(deg[:, :], cn[:, :], 1.0, None, ALU.add))
                    o.done()
                    o.did(v.tensor_scalar(t2[:, :], deg[:, :], EPS, None, ALU.add))
                    o.done()
                    o.did(v.reciprocal(inv[:, :], t2[:, :]))
                    o.done()
                    o.did(v.tensor_tensor(deg[:, :], deg[:, :], inv[:, :], ALU.mult))
                    o.done()
                    o.did(v.tensor_scalar(cn[:, :], deg[:, :], 0.0, None, ALU.is_gt))
                    o.did(v.tensor_scalar(deg[:, :], deg[:, :], EPS, None, ALU.add))
                    o.done()
                    rsqrt(o, isq[:, :], deg[:, :], t2[:, :])
                    o.did(v.tensor_tensor(isq[:, :], isq[:, :], cn[:, :], ALU.mult))
                    o.done()
                    o.did(v.tensor_tensor(inv[:, :], isq[:, :], inv[:, :], ALU.mult))
                    dve.wait_ge(s_ld2, 32)
                    o.did(v.tensor_tensor(smd[:, :], kd[:, :], pd[:, :], ALU.is_equal))
                    o.did(v.tensor_tensor(sms[:, :], ks[:, :], pks[:, :], ALU.is_equal))
                    o.done()
                    o.did(v.tensor_scalar(cut[:, :], smd[:, :], -1.0, -NEG, ALU.add, ALU.mult))
                    o.restart()
                    dve.sem_inc(s_fin, 1)

        end_phase()

        def edge_pass(name, kind, table, width, index, flags, into, sems, T=T, splw=None, rnd=None):
            BLK = P * T
            NB = NP // BLK
            H = NB // 2
            i0 = 0 if rnd is None else rnd * H
            conv, rd, plain = kind == "conv", kind == "round", kind == "plain"
            with ExitStack() as c:
                def two(nm, shape, dt=F32):
                    return [sb(f"{name}_{nm}{u}", shape, dt, c) for u in range(2)]
                S = sems
                s_ix, s_fl, s_w, s_g, s_st = S["ix"], S["fl"], S["w"], S["g"], S["st"]
                s_T, s_ev, s_scan, s_bk, s_rows, s_mul = S["T"], S["ev"], S["scan"], S["bk"], S["rows"], S["mul"]
                ix = two("ix", [P, T], I32)
                g = two("g", [P, T, width])
                fl = two("fl", [D, BLK])
                sT = two("sT", [D, BLK]) if not rd else [sb(f"{name}_sT", [D, BLK], F32, c)] * 2
                sO = two("sO", [D, BLK])
                rows = two("rows", [P, T, D])
                pT = ps(f"{name}_pT", [D, -(-T // 4) * 4 * P], F32, c)
                pB = [ps(f"{name}_pB{u}", [P, -(-T // 8) * 8, D], F32, c) for u in range(1 if conv else 2)]
                pB = pB * 2 if conv else pB
                msg = g if kind in ("plain", "sum") else two("msg", [P, T, D])
                if conv:
                    co1, co2 = two("co1_", [P, T, KS]), two("co2_", [P, T, KS])
                    z = two("z", [P, T, KS, D])
                    zT = two("zT", [P, 3, P])
                    cmb = two("cmb", [P, KS, D])
                    qf = two("q", [P, T], I32)
                    pZ = [ps(f"{name}_pZ{u}", [P, 3, P], F32, c) for u in range(2)]
                    pU = [ps(f"{name}_pU{u}", [P, KS, D], F32, c) for u in range(2)]
                    s_qst, s_wx = S["qst"], S["wx"]
                    s_z, s_zT, s_ze, s_pu, s_comb, s_q = S["z"], S["zT"], S["ze"], S["pu"], S["comb"], S["q"]
                if rd:
                    wt_ = two("w", [P, T])
                    sq = two("sq", [P, T, D])
                    st = two("st", [P, 5, T])
                    s_sq, s_nrm, s_th = S["sq"], S["nrm"], S["th"]
                flb = flags.rearrange("(b a n) -> b a n", a=1, n=BLK)
                write_q = conv and width > D

                def ready_rows(eng, ci, u):
                    if plain:
                        eng.wait_ge(s_ix[u], 16 * (ci + 1))
                    else:
                        eng.wait_ge(s_g[u], T * 16 * (ci + 1))

                with nc.Block(no_gpsimd_drain=True) as block:
                    @block.sync
                    def _(sp):
                        def load_ix(b, u):
                            if plain:
                                sp.dma_start(g[u][:, :, :], blocks(table[0:NP, :], T)[b]).then_inc(s_ix[u], 16)
                            else:
                                sp.dma_start(ix[u][:, :], index[b]).then_inc(s_ix[u], 16)

                        def load_fl(b, u):
                            sp.dma_start(fl[u][:, :], flb[b].to_broadcast([D, BLK])).then_inc(s_fl[u], 16)

                        def load_w(b, u):
                            if conv:
                                sp.dma_start(co2[u][:, :, :], blocks(coef_d[1], T)[b]).then_inc(s_w[u], 16)
                            if rd:
                                sp.dma_start(wt_[u][:, :], blocks(wgt_d, T)[b]).then_inc(s_w[u], 16)

                        def load_wx(b, u):
                            sp.dma_start(co1[u][:, :, :], blocks(coef_d[0], T)[b]).then_inc(s_wx[u], 16)

                        def store(i, u):
                            b = 2 * i + u
                            sp.wait_ge(s_rows, b + 2 * i0 + 1)
                            sp.dma_start(into(b), rows[u][:, :, :]).then_inc(s_st[u], 16)
                        def store_q(b, u):
                            sp.wait_ge(s_q, b + 1)
                            sp.dma_start(blocks(q_tab[1], T)[b], qf[u][:, :]).then_inc(s_qst[u], 16)

                        for u in range(2):
                            load_ix(u, u)
                            if conv:
                                load_wx(u, u)
                            load_w(u, u)
                            load_fl(u, u)
                        with sp.Fori(0, H - 1) as i:
                            for u in range(2):
                                b = 2 * i + u
                                bb = b + 2 * i0
                                if plain:
                                    sp.wait_ge(s_T, bb + 1)
                                else:
                                    sp.wait_ge(s_g[u], T * 16 * (i + i0 + 1))
                                load_ix(b + 2, u)
                                if write_q:
                                    store_q(b, u)
                                if conv:
                                    sp.wait_ge(s_z, KS * (b + 1))
                                    load_wx(b + 2, u)
                                if conv or rd:
                                    sp.wait_ge(s_mul, bb + 1)
                                    load_w(b + 2, u)
                                if not conv:
                                    sp.wait_ge(s_scan, bb + 1)
                                    load_fl(b + 2, u)
                                    store(i, u)
                        if write_q:
                            for u in range(2):
                                store_q(2 * (H - 1) + u, u)
                            for u in range(2):
                                sp.wait_ge(s_qst[u], 16 * H)
                        if not conv:
                            store(H - 1, 0)
                            store(H - 1, 1)
                        for u in range(2):
                            sp.wait_ge(s_st[u], 16 * (H + i0))
                        sp.sem_inc(s_go, 1)

                    if not plain:
                        @block.gpsimd
                        def _(pool):
                            def step(i):
                                for u in range(2):
                                    rsem(pool, s_ix[u], 16 * (i + i0 + 1), s_go)
                                    if not isinstance(i, int):
                                        if conv:
                                            rsem(pool, s_z, KS * (2 * i + u - 1), s_go)
                                            if write_q:
                                                rsem(pool, s_q, 2 * i + u - 1, s_go)
                                        else:
                                            rsem(pool, s_mul if rd else s_T, 2 * (i + i0) + u - 1, s_go)
                                    gather(pool, table, ix[u], g[u], s_g[u])
                            steps(pool, step, H)

                    @block.tensor
                    def _(pe):
                        t_ = nc.tensor

                        def to_cols(i, u):
                            b = 2 * (i + i0) + u
                            if kind in ("plain", "sum"):
                                ready_rows(pe, i + i0, u)
                            else:
                                pe.wait_ge(s_mul, (b + 1) if rd else (b + 1))
                            if not (isinstance(i, int) and u == 0):
                                ge(pe, s_ev, b)
                            pe.sem_inc(s_go, 1)
                            for t in range(T):
                                x = t_.transpose(pT[:, t * P:(t + 1) * P], msg[u][:, t, 0:D], ident[:, :])
                            x.then_inc(s_T, 1)

                        def to_rows(i, u):
                            b = 2 * (i + i0) + u
                            pe.wait_ge(s_scan, b + 1)
                            if conv:
                                ge(pe, s_rows, b)
                            elif not isinstance(i, int):
                                pe.wait_ge(s_rows, b - 1)
                            pe.sem_inc(s_go, 1)
                            v3 = sO[u].rearrange("f (p t) -> f t p", t=T)
                            for t in range(T):
                                x = t_.transpose(pB[u][:, t, :], v3[:, t, :], ident[0:D, 0:D])
                            x.then_inc(s_bk, 1)

                        def spread(i, u, t):
                            n = T * (2 * i + u) + t
                            par = (u + t) % 2
                            if t == 0:
                                pe.wait_ge(s_z, KS * (2 * i + u + 1))
                            ge(pe, s_ze, 2 * (n - 1))
                            zr = z[u].rearrange("p t i o -> p t (i o)")
                            for k in range(3):
                                w = min(P, KS * D - k * P)
                                x = t_.transpose(pZ[par][0:w, k, :], zr[:, t, k * P:k * P + w], ident[:, :])
                            x.then_inc(s_zT, 1)

                        def kernelmul(i, u, t):
                            n = T * (2 * i + u) + t
                            par = (u + t) % 2
                            pe.wait_ge(s_ze, 2 * (n + 1))
                            ge(pe, s_comb, n - 1)
                            for k in range(3):
                                w = min(P, KS * D - k * P)
                                x = t_.matmul(pU[par].rearrange("p j o -> p (j o)"), zT[par][0:w, k, :], splw[0:w, k, :],
                                              start=(k == 0), stop=(k == 2))
                            x.then_inc(s_pu, 1)

                        def step(i):
                            for u in range(2):
                                if conv:
                                    first = isinstance(i, int) and u == 0
                                    spread(i, u, 0)
                                    for t in range(1, T):
                                        spread(i, u, t)
                                        kernelmul(i, u, t - 1)
                                        if t == 2 and not first:
                                            to_cols(*before_b(i, u))
                                        if t == 4 and not isinstance(i, int):
                                            to_rows(i - 1, u)
                                    kernelmul(i, u, T - 1)
                                else:
                                    to_cols(i, u)
                                    to_rows(i, u)
                        steps(pe, step, H)
                        if conv:
                            to_cols(H - 1, 1)
                            to_rows(H - 1, 0)
                            to_rows(H - 1, 1)

                    @block.scalar
                    def _(act):
                        a = nc.scalar

                        def copy_cols(i, u):
                            b = 2 * (i + i0) + u
                            act.wait_ge(s_T, b + 1)
                            if rd:
                                if not (isinstance(i, int) and i == 0 and u == 0):
                                    act.wait_ge(s_scan, b)
                            elif not isinstance(i, int):
                                act.wait_ge(s_scan, b - 1)
                            elif conv:
                                ge(act, s_scan, b - 1)
                            a.activation(sT[u].rearrange("f (p t) -> f t p", t=T),
                                         pT[:, 0:T * P].rearrange("f (t p) -> f t p", t=T), ACT.Copy).then_inc(s_ev, 1)

                        def copy_rows(i, u, more=True):
                            b = 2 * (i + i0) + u
                            act.wait_ge(s_bk, b + 1)
                            ge(act, s_st[u], 16 * i)
                            a.activation(rows[u][:, :, :], pB[u][:, 0:T, :], ACT.Copy).then_inc(s_rows, 1)
                            if conv:
                                act.wait_ge(s_rows, b + 1)
                                act.dma_start(into(2 * i + u), rows[u][:, :, :]).then_inc(s_st[u], 16)
                                if more:
                                    act.wait_ge(s_scan, b + 1)
                                    act.dma_start(fl[u][:, :], flb[b + 2].to_broadcast([D, BLK])).then_inc(s_fl[u], 16)

                        def copy_spread(i, u, t):
                            n = T * (2 * i + u) + t
                            par = (u + t) % 2
                            act.wait_ge(s_zT, n + 1)
                            ge(act, s_pu, n - 1)
                            a.activation(zT[par][:, 0:2, :], pZ[par][:, 0:2, :], ACT.Copy).then_inc(s_ze, 1)
                            a.activation(zT[par][0:D, 2, :], pZ[par][0:D, 2, :], ACT.Copy).then_inc(s_ze, 1)

                        def step(i):
                            for u in range(2):
                                b = 2 * (i + i0) + u
                                if conv:
                                    for t in range(T):
                                        copy_spread(i, u, t)
                                        if t == 2 and not (isinstance(i, int) and u == 0):
                                            copy_cols(*before_b(i, u))
                                        if t == 4 and not isinstance(i, int):
                                            copy_rows(i - 1, u)
                                else:
                                    copy_cols(i, u)
                                    if rd:
                                        act.wait_ge(s_bk, b + 1)
                                        if not isinstance(i, int):
                                            act.wait_ge(s_nrm, b - 1)
                                        a.activation(sq[u][:, :, :], pB[u][:, 0:T, :], ACT.Square).then_inc(s_sq, 1)
                                        act.wait_ge(s_nrm, b + 1)
                                        a.activation(st[u][:, 3, :], st[u][:, 2, :], ACT.Tanh).then_inc(s_th, 1)
                                    else:
                                        copy_rows(i, u)
                        steps(act, step, H)
                        if conv:
                            copy_cols(H - 1, 1)
                            copy_rows(H - 1, 0, more=False)
                            copy_rows(H - 1, 1, more=False)

                    @block.vector
                    def _(dve):
                        v = nc.vector
                        o = Order(dve, s_vo)

                        def run_over(i, u):
                            b = 2 * (i + i0) + u
                            dve.wait_ge(s_ev, b + 1)
                            dve.wait_ge(s_fl[u], 16 * (i + i0 + 1))
                            if not isinstance(i, int) or conv:
                                ge(dve, s_bk, b - 1)
                            first = isinstance(i, int) and i == 0 and u == 0
                            if not first:
                                dve.wait_ge(s_scan, b)
                            v.tensor_tensor_scan(sO[u][:, :], fl[u][:, :], sT[u][:, :],
                                                 (NEG if conv else 0.0) if first else sO[1 - u][:, BLK - 1:BLK],
                                                 op0=ALU.add if conv else ALU.mult,
                                                 op1=ALU.max if conv else ALU.add).then_inc(s_scan, 1)

                        def scale(i, u, k):
                            if k == 0:
                                ready_rows(dve, i, u)
                                dve.wait_ge(s_wx[u], 16 * (i + 1))
                                ge(dve, s_zT, T * (2 * i + u - 1))
                            v.tensor_tensor(z[u][:, :, k, :], g[u][:, :, 0:D],
                                            co1[u][:, :, k:k + 1].to_broadcast([P, T, D]), ALU.mult).then_inc(s_z, 1)

                        def write_sources(i, u):
                            if write_q:
                                ge(dve, s_qst[u], 16 * i)
                                o.did(v.tensor_copy(qf[u].rearrange("p (t a) -> p t a", a=1), g[u][:, :, D:D + 1]))
                                o.done()
                                dve.sem_inc(s_q, 1)

                        def weigh(i, u, t):
                            n = T * (2 * i + u) + t
                            par = (u + t) % 2
                            if t == 0:
                                dve.wait_ge(s_w[u], 16 * (i + 1))
                            dve.wait_ge(s_pu, n + 1)
                            ge(dve, s_cred, n - 1)
                            v.tensor_tensor(cmb[par][:, :, :], pU[par][:, :, :],
                                            co2[u][:, t, :].rearrange("p (j a) -> p j a", a=1)
                                            .to_broadcast([P, KS, D]), ALU.mult).then_inc(s_comb, 1)

                        def sum_up(i, u, t):
                            n = T * (2 * i + u) + t
                            par = (u + t) % 2
                            dve.wait_ge(s_comb, n + 1)
                            if t == 0:
                                ge(dve, s_T, 2 * i + u - 1)
                            v.tensor_reduce(msg[u][:, t, :], cmb[par].rearrange("p j o -> p o j"), AX.X,
                                            ALU.add).then_inc(s_cred, 1)

                        def conv_block(i, u, scale_next, first=False):
                            for t in range(T):
                                weigh(i, u, t)
                                if t > 0:
                                    sum_up(i, u, t - 1)
                                if t < KS and scale_next is not None:
                                    scale(*scale_next, t)
                                if t == KS and not first:
                                    run_over(*before_b(i, u))
                            if write_q and scale_next is not None:
                                write_sources(*scale_next)
                            sum_up(i, u, T - 1)
                            dve.wait_ge(s_cred, T * (2 * i + u + 1))
                            dve.sem_inc(s_mul, 1)

                        def norm(i, u):
                            b = 2 * (i + i0) + u
                            dve.wait_ge(s_sq, b + 1)
                            o.did(v.tensor_reduce(st[u][:, 0, :], sq[u][:, :, :], AX.X, ALU.add))
                            o.done()
                            rsqrt(o, st[u][:, 1, :], st[u][:, 0, :], st[u][:, 2, :])
                            o.did(v.tensor_tensor(st[u][:, 1, :], st[u][:, 0, :], st[u][:, 1, :], ALU.mult))
                            o.done()
                            v.tensor_scalar(st[u][:, 2, :], st[u][:, 1, :], -2.0, EPS, ALU.mult, ALU.add).then_inc(s_nrm, 1)
                            dve.wait_ge(s_nrm, b + 1)
                            o.did(v.reciprocal(st[u][:, 0, :], st[u][:, 2, :]))
                            o.done()
                            dve.wait_ge(s_th, b + 1)
                            o.did(v.tensor_tensor(st[u][:, 4, :], st[u][:, 0, :], st[u][:, 3, :], ALU.mult))
                            o.done()
                            if not (isinstance(i, int) and i == 0):
                                dve.wait_ge(s_st[u], 16 * (i + i0))
                            v.tensor_tensor(rows[u][:, :, :], pB[u][:, 0:T, :], cols(st[u][:, 4, :], D), ALU.mult).then_inc(s_rows, 1)
                            dve.wait_ge(s_rows, b + 1)
                            zb = Z[:, bass.ds((2 * i + u) * T * D, T * D)]
                            o.did(v.scalar_tensor_tensor(out=zb, in0=rows[u].rearrange("p t w -> p (t w)"), scalar=mwl[:, :],
                                                         in1=zb, op0=ALU.mult, op1=ALU.add))

                        if rd:
                            o.did(v.tensor_copy(mwl[:, :], mwB[:, bass.ds(rnd + 1, 1)]))
                            o.restart()
                        if conv:
                            s_cred = S["cred"]
                            for k in range(KS):
                                scale(0, 0, k)
                            if write_q:
                                write_sources(0, 0)

                        def step(i):
                            for u in range(2):
                                b = 2 * (i + i0) + u
                                first = isinstance(i, int) and u == 0
                                if conv:
                                    conv_block(i, u, (i, 1) if u == 0 else (i + 1, 0), first)
                                else:
                                    if rd:
                                        ready_rows(dve, i + i0, u)
                                        dve.wait_ge(s_w[u], 16 * (i + i0 + 1))
                                        if not isinstance(i, int):
                                            dve.wait_ge(s_T, b - 1)
                                        v.tensor_tensor(msg[u][:, :, :], g[u][:, :, :], cols(wt_[u][:, :], D),
                                                        ALU.mult).then_inc(s_mul, 1)
                                        if not first:
                                            norm(*before_b(i, u))
                                    run_over(i, u)
                            if rd or write_q:
                                o.restart()
                        if conv:
                            steps(dve, step, H - 1)
                            conv_block(H - 1, 0, (H - 1, 1))
                            conv_block(H - 1, 1, None)
                            run_over(H - 1, 1)
                            if write_q:
                                o.restart()
                        else:
                            steps(dve, step, H)
                            if rd:
                                norm(H - 1, 1)
                                o.restart()

        def edge_semaphores(name, kind):
            S = {k: sem2(f"{name}_{k}_") for k in ("ix", "fl", "w", "st")}
            S["g"] = sem2(f"{name}_g_", keep=True)
            S.update({k: sem(f"{name}_{k}") for k in ("T", "ev", "scan", "bk", "rows", "mul")})
            if kind == "conv":
                S.update({k: sem(f"{name}_{k}") for k in ("z", "zT", "ze", "pu", "comb", "q", "cred")})
                S["qst"], S["wx"] = sem2(f"{name}_qst_"), sem2(f"{name}_wx_")
            if kind == "round":
                S.update({k: sem(f"{name}_{k}") for k in ("sq", "nrm", "th")})
            return S
        def node_pass(name, table, index, loads, into):
            mats = name in ("net0", "conv1", "conv2")
            second = name in ("net0", "conv2")
            BLKN = P * TN
            NBN = NP // BLKN
            HN = NBN // 2
            with ExitStack() as c:
                def two(nm, shape, dt=F32):
                    return [sb(f"n_{name}_{nm}{u}", shape, dt, c) for u in range(2)]
                s_ix, s_in, s_late, s_st = [sem2(f"n_{name}_{x}") for x in ("index", "inputs", "late_inputs", "stored")]
                s_g = sem2(f"n_{name}_gathered", keep=True)
                s_one = sem(f"n_{name}_ones")
                s_mean, s_T1, s_e1, s_m1, s_used, s_read1, s_r, s_T2, s_e2, s_m2, s_y, s_fin = [
                    sem(f"n_{name}_{x}") for x in ("means", "transposed1", "copied1", "multiplied1", "rows_used", "product1_used",
                                                   "relu", "transposed2", "copied2", "multiplied2", "summed", "finished")]
                ix = two("ix", [P, TN], I32)
                ga = two("ga", [P, TN, D])
                buf = {"o": two("o", [P, TN, D + 1 if name == "net0" else D])}
                widths = {"hb": 2 * D, "xr": D, "yr": D}
                early = [x for x in loads if x[0] not in ("y", "ldf")]
                late = [x for x in loads if x[0] in ("y", "ldf")]
                for k in sorted({x[0] for x in loads} - {"has", "y"}):
                    buf[k] = two(k, [P, TN, widths[k]] if k in widths else [P, TN])
                if name == "z":
                    buf["o2"] = two("o2", [P, TN, D])
                y = buf["y"] = two("y", [P, TN, D])
                sq = sb(f"n_{name}_sq", [P, TN, D], F32, c)
                st = sb(f"n_{name}_st", [P, 4, TN], F32, c)
                mean = sb(f"n_{name}_mean", [P, 2, TN], F32, c)
                k1 = 2 * D if name != "conv1" else D
                n1 = 2 * D if name == "conv2" else D
                if mats:
                    if name == "net0":
                        buf["has"] = two("has", [1, BLKN])
                    k1b = k1 + 1 if name == "conv1" else k1
                    x1T = sb(f"n_{name}_x1T", [k1b, 2, T * P], F32, c)
                    bufs = 1 if second else 2
                    pT = [ps(f"n_{name}_pT{h}", [P, 8 * P], F32, c) for h in range(bufs)] * (3 - bufs)
                    pU = [ps(f"n_{name}_pU{h}", [P, 8, n1], F32, c) for h in range(bufs)] * (3 - bufs)
                    w1, w2 = {"net0": (Wcat, W2b), "conv1": (root1, None), "conv2": (R2F, F2)}[name]
                    t2 = [sb(f"n_{name}_t2_{h}", [P, T, D], F32, c) for h in range(2)]
                if second:
                    x2T = sb(f"n_{name}_x2T", [D + 1, 2, T * P], F32, c)
                    pT2 = ps(f"n_{name}_pT2", [D, 8 * P], F32, c)
                    pU2 = [ps(f"n_{name}_pU2_{h}", [P, 8, D], F32, c) for h in range(2)]
                if name == "conv2":
                    t1 = [sb(f"n_{name}_t1_{h}", [P, T, D], F32, c) for h in range(2)]

                def half(h):
                    return slice(h * T, (h + 1) * T)

                with nc.Block(no_gpsimd_drain=True) as block:
                    @block.sync
                    def _(sp):
                        def load_in(b, u, which, s):
                            for k, src, cut in which:
                                dst = buf[k][u]
                                dst = dst[:, :] if len(dst.shape) == 2 else dst[:, :, cut or slice(0, D)]
                                sp.dma_start(dst, src(b)).then_inc(s[u], 16)

                        def store(b, u):
                            sp.wait_ge(s_fin, b + 1)
                            for k, dst in into:
                                sp.dma_start(dst(b), buf[k][u][:, :, :]).then_inc(s_st[u], 16)
                        for u in range(2):
                            sp.dma_start(ix[u][:, :], index[u]).then_inc(s_ix[u], 16)
                            load_in(u, u, early, s_in)
                            load_in(u, u, late, s_late)
                        with sp.Fori(0, HN - 1) as i:
                            for u in range(2):
                                b = 2 * i + u
                                if second:
                                    sp.wait_ge(s_m1, 2 * (b + 1))
                                    if name == "conv2":
                                        sp.wait_ge(s_read1, 2 * (b + 1))
                                    load_in(b + 2, u, early, s_in)
                                    store(b, u)
                                    load_in(b + 2, u, late, s_late)
                                else:
                                    sp.wait_ge(s_g[u], TN * 16 * (i + 1))
                                    sp.dma_start(ix[u][:, :], index[b + 2]).then_inc(s_ix[u], 16)
                                    store(b, u)
                                    load_in(b + 2, u, early, s_in)
                        for u in range(2):
                            store(2 * (HN - 1) + u, u)
                        for u in range(2):
                            sp.wait_ge(s_st[u], 16 * len(into) * HN)

                    @block.gpsimd
                    def _(pool):
                        def step(i):
                            for u in range(2):
                                rsem(pool, s_ix[u], 16 * (i + 1), s_go)
                                rsem(pool, s_used, 2 * i + u - 1, s_go)
                                gather(pool, table, ix[u], ga[u], s_g[u])
                        steps(pool, step, HN)

                    if mats:
                        @block.tensor
                        def _(pe):
                            t_ = nc.tensor
                            pe.wait_ge(s_one, 1)

                            def first(i, u, h):
                                n = 2 * (2 * i + u) + h
                                if h == 0:
                                    pe.wait_ge(s_in[u], 16 * len(early) * (i + 1))
                                    if name == "net0":
                                        pe.wait_ge(s_mean, 2 * i + u + 1)
                                ge(pe, s_e1, n if second else n - 1)
                                pe.sem_inc(s_go, 1)
                                src = buf["hb"][u] if "hb" in buf else buf["xr"][u]
                                for t in range(T):
                                    x = t_.transpose(pT[h][0:k1, t * P:(t + 1) * P], src[:, h * T + t, 0:k1], ident[:, :])
                                x.then_inc(s_T1, 1)

                            def product1(i, u, h):
                                n = 2 * (2 * i + u) + h
                                pe.wait_ge(s_e1, n + 1)
                                if second:
                                    ge(pe, s_r if name == "net0" else s_read1, n)
                                else:
                                    ge(pe, s_read1, n - 1)
                                if name == "net0":
                                    t_.matmul(pU[h][:, 0:T, :].rearrange("p t n -> p (t n)"), ones_row[0:1, :],
                                              b2a_rows.rearrange("a t n -> a (t n)"), start=True, stop=False)
                                    for t in range(T):
                                        t_.matmul(pU[h][:, t, :], x1T[:, h, t * P:(t + 1) * P], w1[:, :], start=False,
                                                  stop=False)
                                    ov = buf["has"][u].rearrange("a (p t) -> a t p", t=TN)
                                    for t in range(T):
                                        x = t_.matmul(pU[h][:, t, :], ov[:, h * T + t, :], bv[:, :], start=False, stop=(t == T - 1))
                                else:
                                    for t in range(T):
                                        x = t_.matmul(pU[h][:, t, :], x1T[:, h, t * P:(t + 1) * P], w1[:, :], start=True,
                                                      stop=name == "conv1")
                                        if name == "conv2":
                                            x = t_.matmul(pU[h][:, t, 0:D], ones_row[0:1, :], sb2_row[:, :], start=False,
                                                          stop=True)
                                x.then_inc(s_m1, 1)

                            def columns2(i, u, h):
                                n = 2 * (2 * i + u) + h
                                pe.wait_ge(s_r, n + 1)
                                ge(pe, s_e2, n)
                                pe.sem_inc(s_go, 1)
                                for t in range(T):
                                    x = t_.transpose(pT2[:, t * P:(t + 1) * P], t2[h][:, t, :], ident[:, :])
                                x.then_inc(s_T2, 1)

                            def product2(i, u, h):
                                n = 2 * (2 * i + u) + h
                                pe.wait_ge(s_e2, n + 1)
                                ge(pe, s_y, n - 1)
                                for t in range(T):
                                    x = t_.matmul(pU2[h][:, t, :], x2T[:, h, t * P:(t + 1) * P], w2[:, :],
                                                  start=True, stop=True)
                                x.then_inc(s_m2, 1)

                            def step(i):
                                for u in range(2):
                                    if not second:
                                        first(i, u, 0)
                                        first(i, u, 1)
                                        product1(i, u, 0)
                                        product1(i, u, 1)
                                        continue
                                    for h in range(2):
                                        start = isinstance(i, int) and u == 0 and h == 0
                                        first(i, u, h)
                                        if not start:
                                            columns2(*before_h(i, u, h))
                                        product1(i, u, h)
                                        if not start:
                                            product2(*before_h(i, u, h))
                            steps(pe, step, HN)
                            if second:
                                columns2(HN - 1, 1, 1)
                                product2(HN - 1, 1, 1)

                        @block.scalar
                        def _(act):
                            a = nc.scalar

                            def copy1(i, u, h):
                                n = 2 * (2 * i + u) + h
                                act.wait_ge(s_T1, n + 1)
                                ge(act, s_m1, n - 1)
                                a.activation(x1T[0:k1, h, :], pT[h][0:k1, 0:T * P], ACT.Copy).then_inc(s_e1, 1)

                            def hidden(i, u, h):
                                n = 2 * (2 * i + u) + h
                                act.wait_ge(s_m1 if name == "net0" else s_read1, n + 1)
                                ge(act, s_T2, n - 1)
                                a.activation(t2[h][:, :, :], pU[h][:, 0:T, 0:D] if name == "net0" else t1[h][:, :, :],
                                             ACT.Relu).then_inc(s_r, 1)

                            def copy2(i, u, h):
                                n = 2 * (2 * i + u) + h
                                act.wait_ge(s_T2, n + 1)
                                ge(act, s_m2, n - 1)
                                a.activation(x2T[0:D, h, :], pT2[:, 0:T * P], ACT.Copy).then_inc(s_e2, 1)

                            def step(i, more=True):
                                for u in range(2):
                                    if not second:
                                        copy1(i, u, 0)
                                        copy1(i, u, 1)
                                        for h in range(2):
                                            act.wait_ge(s_read1, 2 * (2 * i + u) + h + 1)
                                        ge(act, s_st[u], 16 * len(into) * i)
                                        a.activation(buf["o"][u][:, :, :], y[u][:, :, :], ACT.Relu).then_inc(s_fin, 1)
                                        continue
                                    if more:
                                        act.wait_ge(s_g[u], TN * 16 * (i + 1))
                                        act.dma_start(ix[u][:, :], index[2 * i + u + 2]).then_inc(s_ix[u], 16)
                                    for h in range(2):
                                        copy1(i, u, h)
                                        if not (isinstance(i, int) and i == 0 and u == 0 and h == 0):
                                            copy2(*before_h(i, u, h))
                                        hidden(i, u, h)
                            if second:
                                steps(act, step, HN - 1)
                                step(HN - 1, more=False)
                                copy2(HN - 1, 1, 1)
                            else:
                                steps(act, step, HN)

                    @block.vector
                    def _(dve):
                        v = nc.vector
                        o = Order(dve, s_vo)
                        if mats:
                            o.did(v.memset((x2T if second else x1T)[D:D + 1, :, :], 1.0))
                            o.restart()
                            dve.sem_inc(s_one, 1)

                        def arrived(i, u):
                            dve.wait_ge(s_g[u], TN * 16 * (i + 1))
                            dve.wait_ge(s_in[u], 16 * len(early) * (i + 1))

                        def means(i, u):
                            arrived(i, u)
                            cn = buf["cnt"][u]
                            o.done()
                            o.did(v.tensor_scalar(mean[:, 0, :], cn[:, :], 1.0, None, ALU.max))
                            o.done()
                            o.did(v.reciprocal(mean[:, 1, :], mean[:, 0, :]))
                            o.done()
                            v.tensor_tensor(buf["hb"][u][:, :, D:2 * D], ga[u][:, :, :], cols(mean[:, 1, :], D),
                                            ALU.mult).then_inc(s_mean, 1)
                            dve.wait_ge(s_mean, 2 * i + u + 1)
                            dve.sem_inc(s_used, 1)

                        def use1(i, u, h):
                            n = 2 * (2 * i + u) + h
                            if h == 0:
                                arrived(i, u)
                            dve.wait_ge(s_m1, n + 1)
                            if name == "conv1":
                                if h == 0:
                                    ge(dve, s_fin, 2 * i + u - 1)
                                v.tensor_tensor(y[u][:, half(h), :], ga[u][:, half(h), :], pU[h][:, 0:T, 0:D],
                                                ALU.add).then_inc(s_read1, 1)
                                dve.wait_ge(s_read1, n + 1)
                            else:
                                ge(dve, s_r, n - 1)
                                o.did(v.tensor_tensor(y[u][:, half(h), :], buf["hb"][u][:, half(h), 0:D], pU[h][:, 0:T, D:2 * D],
                                                      ALU.add))
                                v.tensor_tensor(t1[h][:, :, :], ga[u][:, half(h), :], pU[h][:, 0:T, 0:D],
                                                ALU.add).then_inc(s_read1, 1)
                                dve.wait_ge(s_read1, n + 1)
                            if h == 1:
                                dve.sem_inc(s_used, 1)

                        def use2(i, u, h):
                            n = 2 * (2 * i + u) + h
                            dve.wait_ge(s_m2, n + 1)
                            if late and h == 0:
                                dve.wait_ge(s_late[u], 16 * len(late) * (i + 1))
                            o.done()
                            v.tensor_tensor(y[u][:, half(h), :], y[u][:, half(h), :], pU2[h][:, 0:T, :],
                                            ALU.add).then_inc(s_y, 1)

                        def combine(i, u):
                            yy, xr, g_ = y[u][:, :, :], buf["xr"][u], ga[u]
                            arrived(i, u)
                            if name == "z":
                                o.did(v.scalar_tensor_tensor(out=y[u].rearrange("p t w -> p (t w)"),
                                                             in0=xr.rearrange("p t w -> p (t w)"), scalar=mwB[:, 0:1],
                                                             in1=g_.rearrange("p t w -> p (t w)"), op0=ALU.mult, op1=ALU.add))
                            else:
                                o.did(v.tensor_tensor(yy, g_[:, :, :], buf["yr"][u][:, :, :], ALU.add))
                                o.done()
                                o.did(v.tensor_tensor(yy, yy, cols(buf["sc"][u][:, :], D), ALU.mult))
                            o.done()
                            dve.sem_inc(s_used, 1)
                            o.did(v.tensor_tensor(yy, yy, xr[:, :, :], ALU.add))

                        def norm_start(i, u):
                            if second:
                                dve.wait_ge(s_y, 2 * (2 * i + u + 1))
                            o.done()
                            layernorm_start(o, y[u][:, :, :], sq[:, :, :], st)

                        def norm_end(i, u):
                            if not (isinstance(i, int) and i == 0):
                                dve.wait_ge(s_st[u], 16 * len(into) * i)
                            o.did(layernorm_end(o, y[u][:, :, :], st, buf["o"][u][:, :, 0:D]))
                            if name == "net0":
                                o.did(v.tensor_copy(buf["o"][u][:, :, D:D + 1], buf["ldf"][u].rearrange("p (t a) -> p t a", a=1)))
                            o.done()
                            if name == "z":
                                o.did(v.tensor_tensor(buf["o2"][u][:, :, :], buf["o"][u][:, :, :], cols(buf["sc"][u][:, :], D),
                                                      ALU.mult))
                                o.done()
                            dve.sem_inc(s_fin, 1)

                        def step(i, more=True):
                            for u in range(2):
                                first = isinstance(i, int) and i == 0 and u == 0
                                if name == "net0":
                                    if u == 0:
                                        means(i, 1)
                                    elif more:
                                        means(i + 1, 0)
                                    if not first:
                                        use2(*before_h(i, u, 0))
                                        norm_start(*before_b(i, u))
                                        norm_end(*before_b(i, u))
                                    use2(i, u, 0)
                                if name == "conv2":
                                    use1(i, u, 0)
                                    if not first:
                                        use2(*before_h(i, u, 0))
                                        norm_start(*before_b(i, u))
                                    use1(i, u, 1)
                                    if not first:
                                        norm_end(*before_b(i, u))
                                    use2(i, u, 0)
                                if name == "conv1":
                                    use1(i, u, 0)
                                    use1(i, u, 1)
                                if not mats:
                                    combine(i, u)
                                    norm_start(i, u)
                                    norm_end(i, u)
                            o.restart()
                        if second:
                            if name == "net0":
                                means(0, 0)
                            steps(dve, step, HN - 1)
                            step(HN - 1, more=False)
                            use2(HN - 1, 1, 1)
                            norm_start(HN - 1, 1)
                            norm_end(HN - 1, 1)
                            o.restart()
                        else:
                            steps(dve, step, HN)
            end_phase()

        idx_src_d, idx_dst_s = blocks(src_d), blocks(dst_s)
        edge_pass("sum0", "plain", r_rows, D + 2, None, same_s, lambda b: blocks(sum_s[0:NP, :])[b],
                  edge_semaphores("sum0", "plain"))
        end_phase()
        node_pass("net0", sum_s[:, :], blocks(last_s, TN),
                  [("hb", lambda b: blocks(A["x"], TN)[b], slice(0, D)), ("cnt", lambda b: blocks(cnt_s, TN)[b], None),
                   ("has", lambda b: has_s.rearrange("(b a n) -> b a n", a=1, n=P * TN)[b], None),
                   ("y", lambda b: blocks(A["x"], TN)[b], None), ("ldf", lambda b: blocks(last_d_f, TN)[b], None)],
                  [("o", lambda b: blocks(x1_rows, TN)[b])])
        edge_pass("conv1", "conv", x1_rows[:, :], D + 1, idx_src_d, cut_d, lambda b: blocks(mx_rows[0:NP, :])[b],
                  edge_semaphores("conv1", "conv"), splw=spl[0])
        end_phase()
        node_pass("conv1", mx_rows[:, :], blocks(last_d, TN), [("xr", lambda b: blocks(x1_rows, TN)[b][:, :, 0:D], slice(0, D))],
                  [("o", lambda b: blocks(y1_rows, TN)[b])])
        edge_pass("conv2", "conv", y1_rows[:, :], D, idx_src_d, cut_d, lambda b: blocks(mx_rows[0:NP, :])[b],
                  edge_semaphores("conv2", "conv"), splw=spl[1])
        end_phase()
        node_pass("conv2", mx_rows[:, :], blocks(last_d, TN),
                  [("hb", lambda b: blocks(x1_rows, TN)[b][:, :, 0:D], slice(0, D)), ("hb", lambda b: blocks(y1_rows, TN)[b], slice(D, 2 * D))],
                  [("o", lambda b: blocks(h_tab[0][0:NP, :], TN)[b]), ("o", lambda b: blocks(x2_rows, TN)[b])])

        with ExitStack() as c:
            Z = sb("Z", [P, CO * D], F32, c)
            s_zz = sem("z_stored")
            with nc.Block(no_gpsimd_drain=True) as block:
                @block.vector
                def _(dve):
                    o = Order(dve, s_vo)
                    o.did(nc.vector.memset(Z[:, :], 0.0))
                    o.restart()

            q_blocks = blocks(q_tab.rearrange("k n -> (k n)"), TR)
            round_sems = edge_semaphores("round", "round")
            with nc.Fori(0, NL // 2) as pair:
                for half in range(2):
                    r = pair * 2 + half
                    later = (pair + NL - 1) // NL if half == 0 else 1
                    edge_pass(f"round{half}", "round", h_tab[half][:, :], D, Shifted(q_blocks, later * (NP // (P * TR))),
                              same_d, lambda b: blocks(h_tab[1 - half][0:NP, :], TR)[b], round_sems, T=TR, rnd=r)
            with nc.Block(no_gpsimd_drain=True) as block:
                @block.sync
                def _(sp):
                    sp.dma_start(z_rows[0:NP, :].rearrange("(b p t) w -> p b (t w)", p=P, t=TR),
                                 Z[:, :].rearrange("p (b n) -> p b n", n=TR * D)).then_inc(s_zz, 16)
                    sp.wait_ge(s_zz, 16)
        end_phase()
        node_pass("z", z_rows[:, :], blocks(last_d, TN),
                  [("xr", lambda b: blocks(x2_rows, TN)[b], slice(0, D)), ("sc", lambda b: blocks(nscale[0], TN)[b], None)],
                  [("o", lambda b: blocks(x3_rows, TN)[b]), ("o2", lambda b: blocks(y3_rows, TN)[b])])
        edge_pass("sum3", "sum", y3_rows[:, :], D, idx_dst_s, same_s, lambda b: blocks(sum_s[0:NP, :])[b],
                  edge_semaphores("sum3", "sum"))
        end_phase()
        node_pass("out", sum_s[:, :], blocks(last_s, TN),
                  [("xr", lambda b: blocks(x3_rows, TN)[b], slice(0, D)), ("yr", lambda b: blocks(y3_rows, TN)[b], slice(0, D)),
                   ("sc", lambda b: blocks(nscale[1], TN)[b], None)],
                  [("o", lambda b: blocks(out, TN)[b])])


_INS = {'x': 'x', 'src': 'src', 'dst': 'dst', 'edge_attr_2': 'ea2', 'edge_attr_64': 'ea64', 'edge_weight': 'ew',
        'L0_gnn_W1a': 'W1a', 'L0_gnn_b1a': 'b1a', 'L0_gnn_W1b': 'W1b', 'L0_gnn_b1b': 'b1b', 'L0_gnn_W2a': 'W2a',
        'L0_gnn_b2a': 'b2a', 'L0_gnn_W2b': 'W2b', 'L0_gnn_b2b': 'b2b', 'L1_gnn_W1': 'W1', 'L1_gnn_root1': 'root1',
        'L1_gnn_b1': 'sb1', 'L1_gnn_W2': 'W2', 'L1_gnn_root2': 'root2', 'L1_gnn_b2': 'sb2',
        'L1_gnn_final_w': 'final_w', 'L1_gnn_final_b': 'final_b', 'L2_gnn_manifold_weights': 'mw'}


def kernel(**inputs):
    import numpy as _np
    import concourse.bacc as _bacc
    from concourse import mybir as _mybir
    from concourse.bass_utils import run_bass_kernel_spmd as _run

    nc = _bacc.Bacc("TRN2", target_bir_lowering=False, num_devices=1)
    arrays, args = {}, {}
    for name, short in _INS.items():
        a = _np.ascontiguousarray(inputs[name])
        if a.shape[0] == N:
            pad = _np.full((NP,) + a.shape[1:], N if a.dtype.kind in "iu" else 0, a.dtype)
            pad[:N] = a
            a = pad
        arrays[f"in_{short}"] = a
        args[short] = nc.dram_tensor(f"in_{short}", a.shape, _mybir.dt.from_np(a.dtype), kind="ExternalInput").ap()
    out = nc.dram_tensor("out_0", (NP, D), F32, kind="ExternalOutput").ap()
    program(nc, args, out)
    r = _run(nc, [arrays], core_ids=[0])
    return r.results[0]["out_0"][:N]
```

```python
import concourse.bass as bass
from concourse import mybir
from contextlib import ExitStack

F32 = mybir.dt.float32
F16 = mybir.dt.float16
I32 = mybir.dt.int32
ALU = mybir.AluOpType
ACT = mybir.ActivationFunctionType
AX = mybir.AxisListType

P = 128
N = 50000
D = 64
T = 7
BLK = P * T
NB = 56
H = NB // 2
NP = NB * BLK
TR = 14
TN = 2 * T
CO = NP // P
LO = 512
HI = NP // LO
RS = NP + 1
ZROW = NP
KS = 5
NL = 10
EPS_LN = 1e-5
EPS = 1e-8
NEG = -3.0e38
RSQRT_SEED = 0x5F3759DF
UN = 2 * T
G = 4
GROUPS = (4, 3, 4, 3)
FIRST = {-2: -7, -1: -3, 0: 0, 1: 4, 2: 7, 3: 11, 4: 14}
NU = CO // UN
assert NP >= N and HI * LO == NP and CO % UN == 0


def ge(eng, sem, value):
    if isinstance(value, int) and value <= 0:
        return
    eng.wait_ge(sem, value)


def rsem(eng, sem, value, go):
    if isinstance(value, int) and value <= 0:
        return
    eng.wait_ge(sem, value)
    eng.sem_inc(go, 1)


class Order:

    def __init__(self, eng, sem):
        self.eng, self.sem, self.n = eng, sem, 0

    def did(self, ins):
        ins.then_inc(self.sem, 1)
        self.n += 1

    def done(self):
        if self.n:
            self.eng.wait_ge(self.sem, self.n)

    def restart(self):
        if not self.n:
            return
        self.done()
        self.eng.sem_inc(self.sem, -self.n)
        self.n = 0


def steps(eng, body, last=H):
    body(0)
    with eng.Fori(1, last) as i:
        body(i)


def program(nc, A, out):
    ctx = ExitStack()

    def sb(name, shape, dt=F32, c=ctx):
        return c.enter_context(nc.sbuf_tensor(name, shape, dt))

    def ps(name, shape, dt=F32, c=ctx):
        return c.enter_context(nc.psum_tensor(name, shape, dt))

    lent = []

    def sem(name):
        lent.append(nc.alloc_semaphore(name=name))
        return lent[-1]

    def sem2(name, keep=False):
        return [(kept if keep else sem)(f"{name}{u}") for u in range(2)]

    def kept(name):
        return ctx.enter_context(nc.semaphore(name))

    def end_phase():
        for s in lent:
            nc.gpsimd.sem_clear(s)
        nc.all_engine_barrier()
        for s in lent:
            nc.release_semaphore(s)
        lent.clear()

    def dram(name, shape, dt=F32):
        return nc.dram_tensor(name, shape, dt, kind="Internal").ap()

    def flat(ap):
        return ap.rearrange("(p c) -> p c", c=CO)

    def blocks(ap, T=T):
        if len(ap.shape) == 1:
            return ap.rearrange("(b p t) -> b p t", p=P, t=T)
        return ap.rearrange("(b p t) w -> b p t w", p=P, t=T)

    with ctx:
        pos_s = dram("pos_s", [NP], I32)
        pos_d = dram("pos_d", [NP], I32)
        last_s = dram("last_s", [NP], I32)
        last_d = dram("last_d", [NP], I32)
        last_d_f = dram("last_d_f", [NP])
        cnt_s = dram("cnt_s", [NP])
        r_rows = dram("r_rows", [NP, D + 2])
        rec_d = dram("rec_d", [NP, 5])
        key_sh = dram("key_sh", [2, NP + P])
        same_s = dram("same_s", [NP])
        same_d = dram("same_d", [NP])
        cut_d = dram("cut_d", [NP])
        src_d = dram("src_d", [NP], I32)
        wgt_d = dram("wgt_d", [NP])
        coef_d = [dram(f"coef_d{k}", [NP, KS]) for k in range(2)]
        dst_s = dram("dst_s", [NP], I32)
        q_tab = dram("q_tab", [2, NP], I32)
        sum_s = dram("sum_s", [RS, D])
        x1_rows = dram("x1_rows", [NP, D + 1])
        mx_rows = dram("mx_rows", [RS, D])
        y1_rows = dram("y1_rows", [NP, D])
        x2_rows = dram("x2_rows", [NP, D])
        h_tab = [dram(f"h_tab{k}", [RS, D]) for k in range(2)]
        z_rows = dram("z_rows", [RS, D])
        x3_rows = dram("x3_rows", [NP, D])
        y3_rows = dram("y3_rows", [NP, D])
        nscale = dram("nscale", [2, NP])

        ident = sb("ident", [P, P])
        ident16 = sb("ident16", [P, P], F16)
        below = sb("below", [P, P])
        above = sb("above", [P, P])
        iota_i = sb("iota_i", [P, LO], I32)
        diag_i = sb("diag_i", [P, P], I32)
        iota_lo = sb("iota_lo", [P, LO], F16)
        zrow = sb("zrow", [P, 3 * (D + 2)])
        W1a = sb("W1a", [P, D])
        Wcat = sb("Wcat", [P, D])
        W1bT = sb("W1bT", [D, D])
        W1b = sb("W1b", [D, D + 1])
        W2lo = sb("W2lo", [D, D])
        b1bT = sb("b1bT", [D, P])
        W2b = sb("W2b", [D + 1, D])
        root1 = sb("root1", [D + 1, D])
        R2F = sb("R2F", [P, 2 * D])
        F2 = sb("F2", [D + 1, D])
        spl = [sb(f"spl{n}", [P, 3, KS * D]) for n in range(2)]
        net0_bias = sb("net0_bias", [T + 1, T, D])
        b1a_rows = sb("b1a_rows", [1, T, D])
        sb2_row = sb("sb2_row", [1, D])
        ones_row = sb("ones_row", [1, P])
        bv = sb("bv", [1, D])
        mwB = sb("mwB", [P, NL + 1])
        mwl = sb("mwl", [P, 1])

        s_boot = sem("constants_loaded")
        s_zero = sem("zero_rows_stored")
        s_pool = sem("iotas_made")
        s_bv = sem("diagonal_stored")
        s_vo = kept("vector_order")
        s_go = kept("waits_passed")
        s_tr = sem("setup_transposed")
        s_cp = sem("setup_copied")
        s_mm = sem("setup_multiplied")

        nload = [0]
        with nc.Block(no_gpsimd_drain=True) as block, ExitStack() as c:
            pset = ps("pset", [P, 512], F32, c)

            @block.sync
            def _(sp):
                def ld(dst, src):
                    sp.dma_start(dst, src).then_inc(s_boot, 16)
                    nload[0] += 16

                def zero(dst, src):
                    sp.dma_start(dst, src).then_inc(s_zero, 16)
                ld(W1a[:, :], A["W1a"])
                ld(Wcat[0:D, :], A["W2a"][0:D, :])
                ld(W2lo[:, :], A["W2a"][D:2 * D, :])
                ld(W1b[:, 0:D], A["W1b"])
                ld(W1b[:, D:D + 1], A["b1b"].rearrange("(a b) -> a b", b=1))
                ld(W2b[0:D, :], A["W2b"])
                ld(root1[0:D, :], A["root1"])
                ld(R2F[D:P, 0:D], A["root2"])
                ld(R2F[:, D:2 * D], A["final_w"][0:2 * D, :])
                ld(F2[0:D, :], A["final_w"][2 * D:3 * D, :])
                for n in range(2):
                    w = A[f"W{n + 1}"].rearrange("(j i) c o -> (i c) j o", i=KS)
                    for k in range(3):
                        rows = min(P, KS * D - P * k)
                        ld(spl[n][0:rows, k, :].rearrange("p (j o) -> p j o", j=KS), w[P * k:P * k + rows])
                ld(net0_bias[T:T + 1, :, :], A["b2a"].rearrange("(a b n) -> a b n", a=1, b=1).to_broadcast([1, T, D]))
                ld(b1a_rows[:, :, :], A["b1a"].rearrange("(a b n) -> a b n", a=1, b=1).to_broadcast([1, T, D]))
                for row, name in ((sb2_row[:, :], "sb2"), (W2b[D:D + 1, :], "b2b"), (root1[D:D + 1, :], "sb1"),
                                  (F2[D:D + 1, :], "final_b")):
                    ld(row, A[name].rearrange("(a n) -> a n", a=1))
                ld(mwB[:, :], A["mw"].rearrange("(a n) -> a n", a=1).to_broadcast([P, NL + 1]))
                sp.wait_ge(s_cp, 1)
                zero(sum_s[ZROW:ZROW + 1, :], zrow[0:1, 0:D])
                zero(mx_rows[ZROW:ZROW + 1, :], zrow[0:1, 0:D])
                zero(z_rows[ZROW:ZROW + 1, :], zrow[0:1, 0:D])
                for k in range(2):
                    zero(h_tab[k][ZROW:ZROW + 1, :], zrow[0:1, 0:D])
                for k in range(2):
                    zero(key_sh[k:k + 1, 0:1], zrow[0:1, 2 * D:2 * D + 1])
                sp.wait_ge(s_boot, nload[0])
                sp.wait_ge(s_zero, 7 * 16)
                sp.wait_ge(s_cp, 4)
                for k in range(T):
                    sp.dma_start(net0_bias[k:k + 1, k, :], bv[:, :]).then_inc(s_bv, 16)
                sp.wait_ge(s_bv, 16 * T)

            @block.gpsimd
            def _(pool):
                pool.iota(iota_i[:, :], pattern=[[1, LO]], base=0, channel_multiplier=0).then_inc(s_pool, 1)
                pool.iota(diag_i[:, :], pattern=[[1, P]], base=0, channel_multiplier=-1).then_inc(s_pool, 1)

            @block.vector
            def _(dve):
                v = nc.vector
                o = Order(dve, s_vo)
                o.did(v.memset(zrow[:, :], 0.0))
                o.done()
                o.did(v.memset(zrow[:, 2 * D:2 * D + 1], -1.0))
                o.did(v.memset(R2F[0:D, 0:D], 0.0))
                o.did(v.memset(ones_row[:, :], 1.0))
                o.did(v.memset(net0_bias[0:T, :, :], 0.0))
                o.done()
                dve.sem_inc(s_cp, 1)
                dve.wait_ge(s_pool, 2)
                o.did(v.tensor_copy(iota_lo[:, :], iota_i[:, :]))
                o.did(v.tensor_scalar(ident[:, :], diag_i[:, :], 0.0, None, ALU.is_equal))
                o.did(v.tensor_scalar(ident16[:, :], diag_i[:, :], 0.0, None, ALU.is_equal))
                o.did(v.tensor_scalar(below[:, :], diag_i[:, :], 0.0, None, ALU.is_lt))
                o.did(v.tensor_scalar(above[:, :], diag_i[:, :], 0.0, None, ALU.is_gt))
                o.restart()
                dve.sem_inc(s_cp, 1)
                dve.wait_ge(s_tr, 1)
                o.did(v.tensor_copy(W1bT[:, :], pset[0:D, 0:D]))
                o.did(v.tensor_copy(b1bT[:, :], W1b[:, D:D + 1].to_broadcast([D, P])))
                o.restart()
                dve.sem_inc(s_cp, 1)
                dve.wait_ge(s_mm, 1)
                o.did(v.tensor_copy(Wcat[D:P, :], pset[0:D, 64:128]))
                o.did(v.tensor_copy(bv[:, :], pset[0:1, 128:192]))
                o.restart()
                dve.sem_inc(s_cp, 1)

            @block.tensor
            def _(pe):
                pe.wait_ge(s_boot, nload[0])
                pe.wait_ge(s_cp, 2)
                nc.tensor.transpose(pset[0:D, 0:D], W1b[:, 0:D], ident[0:D, 0:D]).then_inc(s_tr, 1)
                pe.wait_ge(s_cp, 3)
                nc.tensor.matmul(pset[0:D, 64:128], W1bT[:, :], W2lo[:, :], start=True, stop=True)
                nc.tensor.matmul(pset[:, 128:192], b1bT[:, :], W2lo[:, :], start=True, stop=True).then_inc(s_mm, 1)

        end_phase()

        def gather(pool, table, idx, dst, s):
            for t in range(idx.shape[1]):
                pool.indirect_dma_start(out=dst[:, t, :], out_offset=None, in_=table,
                                        in_offset=bass.IndirectOffsetOnAxis(ap=idx[:, t:t + 1], axis=0)).then_inc(s, 16)

        def scatter(pool, table, idx, src, s):
            for t in range(T):
                pool.indirect_dma_start(out=table, out_offset=bass.IndirectOffsetOnAxis(ap=idx[:, t:t + 1], axis=0),
                                        in_=src[:, t, :], in_offset=None).then_inc(s, 16)

        def sort_by(name, key_in, pos, last, last_f, count, messages=False):
            with ExitStack() as c:
                def cs(nm, shape, dt=F32):
                    return sb(f"{name}_{nm}", shape, dt, c)

                key_i = cs("key_i", [P, CO], I32)
                dig_i = cs("dig_i", [P, CO], I32)
                key_f = cs("key_f", [P, CO])
                hi_f = cs("hi_f", [P, CO])
                lo_f = cs("lo_f", [P, CO])
                pos_i = cs("pos_i", [P, CO], I32)
                oh_hi = cs("oh_hi", [P, 2 * G, HI], F16)
                oh_lo = cs("oh_lo", [P, 2 * G, LO], F16)
                hist = cs("hist", [HI, LO])
                ends = cs("ends", [HI, LO])
                start = cs("start", [HI, LO])
                base = cs("base", [HI, 1])
                last_t = cs("last_t", [HI, LO])
                last_i = cs("last_i", [HI, LO], I32)
                tab = cs("tab", [HI, 2, LO])
                hiT = cs("hiT", [HI, 2, G, P])
                keyB = cs("keyB", [P, 2, G, P])
                junk = cs("junk", [P, 2, 2 * G, LO])
                rank = cs("rank", [P, 2, UN])
                pC = ps(f"{name}_pC", [HI, LO], F32, c)
                pL = [ps(f"{name}_pL{k}", [P, LO], F32, c) for k in range(2)]
                pH = ps(f"{name}_pH", [HI, 2, G, P], F16, c)
                pK = [ps(f"{name}_pK{k}", [P, G, P], F32, c) for k in range(2)]
                pB = pL[0]

                def ssem(nm):
                    return sem(f"{name}_{nm}")
                s_key, s_dig, s_oh, s_cnt = ssem("key_loaded"), ssem("digits"), ssem("hist_onehots"), ssem("hist_counted")
                s_row, s_base, s_st = ssem("row_totals"), ssem("bases"), ssem("starts")
                s_oh2, s_T, s_bcst, s_tab, s_hT = ssem("onehots"), ssem("transposed"), ssem("key_spread"), ssem("table_copied"), ssem("hiT_copied")
                s_upd, s_look, s_rank, s_eq = ssem("table_updated"), ssem("looked_up"), ssem("ranked"), ssem("compared")
                s_pos, s_st2, s_out = ssem("pos_done"), ssem("last_done"), ssem("stored")
                if messages:
                    di = [sb(f"m_dst{u}", [P, T], I32, c) for u in range(2)]
                    dr = [sb(f"m_dst_row{u}", [P, T], I32, c) for u in range(2)]
                    si = [sb(f"m_src{u}", [P, T], I32, c) for u in range(2)]
                    pi_s = [sb(f"m_pos_s{u}", [P, T], I32, c) for u in range(2)]
                    hb = [sb(f"m_hb{u}", [P, T, 2 * D], F32, c) for u in range(2)]
                    ht = sb("m_ht", [P, 2, T * P], F32, c)
                    rr = [sb(f"m_rr{u}", [P, T, D + 2], F32, c) for u in range(2)]
                    pT = ps("m_pT", [P, G * P], F32, c)
                    pU = ps("m_pU", [P, 8, D], F32, c)
                    m_in1, m_in2 = sem2("m_gather_inputs"), sem2("m_row_inputs")
                    m_g, m_sc = sem2("m_gathered", keep=True), sem2("m_scattered", keep=True)
                    m_T, m_ev, m_mm, m_r = sem("m_transposed"), sem("m_copied"), sem("m_multiplied"), sem("m_rows_ready")
                    dstb, srcb, posb, ea64b = blocks(A["dst"]), blocks(A["src"]), blocks(pos_s), blocks(A["ea64"])

                def spread_of(q):
                    return q // 2, (0 if q % 2 == 0 else G), (G if q % 2 == 0 else T - G)

                with nc.Block(no_gpsimd_drain=True) as block:
                    @block.sync
                    def _(sp):
                        sp.dma_start(key_i[:, :], flat(key_in)).then_inc(s_key, 16)

                        def load1(b, u):
                            sp.dma_start(di[u][:, :], dstb[b]).then_inc(m_in1[u], 16)
                            sp.dma_start(hb[u][:, :, D:2 * D], ea64b[b]).then_inc(m_in1[u], 16)

                        def load2(b, u):
                            sp.dma_start(dr[u][:, :], dstb[b]).then_inc(m_in2[u], 16)
                            sp.dma_start(si[u][:, :], srcb[b]).then_inc(m_in2[u], 16)
                            sp.dma_start(pi_s[u][:, :], posb[b]).then_inc(m_in2[u], 16)

                        def with_messages(sp):
                            def step(i):
                                for u in range(2):
                                    sp.wait_ge(m_T, 2 * (2 * i + u + 1))
                                    load1(2 * i + u + 2, u)
                                    if u == 0:
                                        if not isinstance(i, int):
                                            sp.wait_ge(m_sc[1], T * 16 * i)
                                            load2(2 * i + 1, 1)
                                    else:
                                        sp.wait_ge(m_sc[0], T * 16 * (i + 1))
                                        load2(2 * i + 2, 0)
                            steps(sp, step, H - 1)
                            sp.wait_ge(m_sc[1], T * 16 * (H - 1))
                            load2(2 * H - 1, 1)

                        if messages:
                            for u in range(2):
                                load1(u, u)
                                load2(u, u)
                        sp.wait_ge(s_st2, 1)
                        node = "(h l) -> h l"
                        sp.dma_start(last.rearrange(node, l=LO), last_i[:, :]).then_inc(s_out, 16)
                        n = 16
                        if last_f is not None:
                            sp.dma_start(last_f.rearrange(node, l=LO), last_t[:, :]).then_inc(s_out, 16)
                            n += 16
                        if count is not None:
                            sp.dma_start(count.rearrange(node, l=LO), hist[:, :]).then_inc(s_out, 16)
                            n += 16
                        if messages:
                            with_messages(sp)
                        sp.wait_ge(s_pos, 1)
                        sp.dma_start(flat(pos), pos_i[:, :]).then_inc(s_out, 16)
                        sp.wait_ge(s_out, n + 16)

                    @block.vector
                    def _(dve):
                        v = nc.vector
                        o = Order(dve, s_vo)
                        dve.wait_ge(s_key, 16)
                        o.did(v.tensor_copy(key_f[:, :], key_i[:, :]))
                        o.did(v.tensor_scalar(dig_i[:, :], key_i[:, :], 9, None, ALU.arith_shift_right))
                        o.done()
                        o.did(v.tensor_copy(hi_f[:, :], dig_i[:, :]))
                        o.did(v.scalar_tensor_tensor(out=lo_f[:, :], in0=dig_i[:, :], scalar=-float(LO), in1=key_f[:, :],
                                                     op0=ALU.mult, op1=ALU.add))
                        o.restart()
                        dve.sem_inc(s_dig, 1)

                        def onehots(n, k, s):
                            v.tensor_scalar(oh_hi[:, k, :], iota_lo[:, 0:HI], hi_f[:, bass.ds(n, 1)], None,
                                            ALU.is_equal).then_inc(s, 1)
                            v.tensor_scalar(oh_lo[:, k, :], iota_lo[:, :], lo_f[:, bass.ds(n, 1)], None,
                                            ALU.is_equal).then_inc(s, 1)

                        def hist_step(i):
                            for k in range(UN):
                                n = i * UN + k
                                ge(dve, s_cnt, n - T + 1)
                                onehots(n, k % T, s_oh)
                        steps(dve, hist_step, NU)

                        dve.wait_ge(s_cnt, CO + 1)
                        o.did(v.tensor_copy(hist[:, :], pC[:, :]))
                        o.done()
                        o.did(v.tensor_tensor_scan(ends[:, :], ones[0:HI, :], hist[:, :], 0.0, op0=ALU.mult, op1=ALU.add))
                        o.done()
                        dve.sem_inc(s_row, 1)
                        dve.wait_ge(s_base, 1)
                        o.did(v.tensor_copy(base[:, :], pB[0:HI, 0:1]))
                        o.done()
                        o.did(v.tensor_scalar(ends[:, :], ends[:, :], base[:, :], None, ALU.add))
                        o.done()
                        o.did(v.tensor_tensor(start[:, :], ends[:, :], hist[:, :], ALU.subtract))
                        o.did(v.tensor_scalar(last_t[:, :], ends[:, :], -1.0 - ZROW, None, ALU.add))
                        o.done()
                        o.did(v.tensor_scalar(junk[0:HI, 0, 0, :], hist[:, :], 0.5, None, ALU.is_gt))
                        o.done()
                        o.did(v.tensor_tensor(last_t[:, :], last_t[:, :], junk[0:HI, 0, 0, :], ALU.mult))
                        o.done()
                        o.did(v.tensor_scalar(last_t[:, :], last_t[:, :], float(ZROW), None, ALU.add))
                        o.done()
                        o.did(v.tensor_copy(last_i[:, :], last_t[:, :]))
                        o.did(v.tensor_copy(tab[:, 0, :], start[:, :]))
                        o.restart()
                        dve.sem_inc(s_st, 1)
                        dve.sem_inc(s_st2, 1)

                        def group(i, q):
                            p = q % 2
                            for k in range(GROUPS[q]):
                                j = FIRST[q] + k
                                n = i * UN + j
                                dve.wait_ge(s_T, 2 * (4 * i + q) + 2)
                                v.scalar_tensor_tensor(out=junk[:, 0, p * G + k, 0:(k + 1) * P],
                                                       in0=pK[p][:, 0:k + 1, :].rearrange("p k f -> p (k f)"),
                                                       scalar=key_f[:, bass.ds(n, 1)], in1=before[:, (G - 1 - k) * P:],
                                                       op0=ALU.is_equal, op1=ALU.mult,
                                                       accum_out=rank[:, 0, j:j + 1]).then_inc(s_eq, 1)
                                dve.wait_ge(s_look, n + 1)
                                v.scalar_tensor_tensor(out=junk[:, 1, p * G + k, :], in0=pL[j % 2][:, :], scalar=1.0,
                                                       in1=oh_lo[:, p * G + k, :], op0=ALU.mult, op1=ALU.mult,
                                                       accum_out=rank[:, 1, j:j + 1]).then_inc(s_rank, 1)

                        def group_onehots(i, q):
                            ge(dve, s_upd, 4 * i + q - 1)
                            ge(dve, s_rank, i * UN + FIRST[q - 1])
                            ge(dve, s_eq, i * UN + FIRST[q - 1])
                            for k in range(GROUPS[q]):
                                onehots(i * UN + FIRST[q] + k, (q % 2) * G + k, s_oh2)

                        def sort_step(i, more=True):
                            for q in range(4):
                                if q < 3:
                                    group_onehots(i, q + 1)
                                elif more:
                                    group_onehots(i + 1, 0)
                                group(i, q)
                            dve.wait_ge(s_rank, (i + 1) * UN)
                            dve.wait_ge(s_eq, (i + 1) * UN)
                            o.did(v.tensor_tensor(pos_i[:, bass.ds(i * UN, UN)], rank[:, 0, :], rank[:, 1, :], ALU.add))
                            o.restart()
                        group_onehots(0, 0)
                        steps(dve, sort_step, NU - 1)
                        sort_step(NU - 1, more=False)
                        dve.sem_inc(s_pos, 1)

                    @block.scalar
                    def _(act):
                        a = nc.scalar
                        act.wait_ge(s_dig, 1)

                        def message_part(i, q):
                            u, t0, nt = spread_of(q)
                            if q == 2:
                                hidden(i, 0)
                            if q == 0 and not isinstance(i, int):
                                hidden(i - 1, 1)
                            act.wait_ge(m_T, 4 * i + q + 1)
                            if q % 2 == 0:
                                ge(act, m_mm, 2 * i + u - 1)
                            a.activation(ht[:, u, t0 * P:(t0 + nt) * P], pT[:, 0:nt * P], ACT.Copy).then_inc(m_ev, 1)

                        def hidden(i, u):
                            act.wait_ge(m_in2[u], 3 * 16 * (i + 1))
                            if not (isinstance(i, int) and i == 0):
                                act.wait_ge(m_sc[u], T * 16 * i)
                            a.activation(rr[u][:, :, D:D + 1], dr[u].rearrange("p (t a) -> p t a", a=1), ACT.Copy)
                            a.activation(rr[u][:, :, D + 1:D + 2], si[u].rearrange("p (t a) -> p t a", a=1), ACT.Copy)
                            act.wait_ge(m_mm, 2 * i + u + 1)
                            a.activation(rr[u][:, :, 0:D], pU[:, 0:T, :], ACT.Relu).then_inc(m_r, 1)

                        def sort_step(i):
                            for q in range(4):
                                g, p = 4 * i + q, q % 2
                                n0 = i * UN + FIRST[q]
                                ge(act, s_T, 2 * g - 2)
                                a.activation(keyB[:, p, 0:GROUPS[q], :],
                                             key_f[:, bass.ds(n0, GROUPS[q])].rearrange("p (k a) -> p k a", a=1)
                                             .to_broadcast([P, GROUPS[q], P]), ACT.Copy).then_inc(s_bcst, 1)
                                if messages and not (isinstance(i, int) and q == 0):
                                    message_part(*((i, q - 1) if q else (i - 1, 3)))
                                act.wait_ge(s_T, 2 * g + 2)
                                ge(act, s_look, i * UN + FIRST[q - 1])
                                a.activation(hiT[:, p, 0:GROUPS[q], :], pH[:, p, 0:GROUPS[q], :], ACT.Copy).then_inc(s_hT, 1)
                                act.wait_ge(s_upd, g + 1)
                                ge(act, s_look, n0)
                                a.activation(tab[:, 1 - p, :], pC[:, :], ACT.Copy).then_inc(s_tab, 1)
                        steps(act, sort_step, NU)
                        if messages:
                            message_part(NU - 1, 3)
                            hidden(NU - 1, 1)

                    @block.tensor
                    def _(pe):
                        t = nc.tensor
                        t.matmul(pC[:, :], zero16[:, 0:HI], iota_lo[:, :], start=True, stop=False)

                        def hist_step(i):
                            for k in range(UN):
                                pe.wait_ge(s_oh, 2 * (i * UN + k) + 2)
                                t.matmul(pC[:, :], oh_hi[:, k % T, :], oh_lo[:, k % T, :], start=False,
                                         stop=False).then_inc(s_cnt, 1)
                        steps(pe, hist_step, NU)
                        t.matmul(pC[:, :], zero16[:, 0:HI], iota_lo[:, :], start=False, stop=True).then_inc(s_cnt, 1)
                        pe.wait_ge(s_row, 1)
                        t.matmul(pB[0:HI, 0:1], above[0:HI, 0:HI], ends[:, LO - 1:LO], start=True, stop=True).then_inc(s_base, 1)
                        pe.wait_ge(s_st, 1)

                        def message_columns(i, q):
                            u, t0, nt = spread_of(q)
                            if q % 2 == 0:
                                pe.wait_ge(m_g[u], T * 16 * (i + 1))
                                pe.wait_ge(m_in1[u], 2 * 16 * (i + 1))
                            ge(pe, m_ev, 4 * i + q)
                            pe.sem_inc(s_go, 1)
                            for k in range(nt):
                                x = t.transpose(pT[:, k * P:(k + 1) * P], hb[u][:, t0 + k, :], ident[:, :])
                            x.then_inc(m_T, 1)

                        def message_product(i, u):
                            pe.wait_ge(m_ev, 2 * (2 * i + u + 1))
                            ge(pe, m_r, 2 * i + u)
                            t.matmul(pU[:, 0:T, :].rearrange("p t n -> p (t n)"), ones_row[0:1, :],
                                     b1a_rows.rearrange("a t n -> a (t n)"), start=True, stop=False)
                            for k in range(T):
                                x = t.matmul(pU[:, k, :], ht[:, u, k * P:(k + 1) * P], W1a[:, :], start=False, stop=(k == T - 1))
                            x.then_inc(m_mm, 1)

                        def sort_step(i):
                            for q in range(4):
                                g, p = 4 * i + q, q % 2
                                n0 = i * UN + FIRST[q]
                                pe.wait_ge(s_oh2, 2 * (i * UN + FIRST[q + 1]))
                                ge(pe, s_hT, g - 1)
                                ge(pe, s_eq, i * UN + FIRST[q - 1])
                                for k in range(GROUPS[q]):
                                    x = t.transpose(pH[:, p, k, :], oh_hi[:, p * G + k, :], ident16[:, :])
                                x.then_inc(s_T, 1)
                                pe.wait_ge(s_bcst, g + 1)
                                for k in range(GROUPS[q]):
                                    x = t.transpose(pK[p][:, k, :], keyB[:, p, k, :], ident[:, :])
                                x.then_inc(s_T, 1)
                                ge(pe, s_tab, g)
                                t.matmul(pC[:, :], ident[0:HI, 0:HI], tab[:, p, :], start=True, stop=False)
                                for k in range(GROUPS[q]):
                                    x = t.matmul(pC[:, :], oh_hi[:, p * G + k, :], oh_lo[:, p * G + k, :],
                                                 start=False, stop=(k == GROUPS[q] - 1))
                                x.then_inc(s_upd, 1)
                                pe.wait_ge(s_hT, g + 1)
                                for k in range(GROUPS[q]):
                                    ge(pe, s_rank, n0 + k - 1)
                                    t.matmul(pL[(FIRST[q] + k) % 2][:, :], hiT[:, p, k, :], tab[:, p, :], start=True,
                                             stop=True).then_inc(s_look, 1)
                                if messages:
                                    if q == 2:
                                        message_product(i, 0)
                                    if q == 0 and not isinstance(i, int):
                                        message_product(i - 1, 1)
                                    message_columns(i, q)
                        steps(pe, sort_step, NU)
                        if messages:
                            message_product(NU - 1, 1)

                    if messages:
                        @block.gpsimd
                        def _(pool):
                            def scat(i, u):
                                rsem(pool, m_r, 2 * i + u + 1, s_go)
                                scatter(pool, r_rows[:, :], pi_s[u], rr[u], m_sc[u])

                            def step(i):
                                for u in range(2):
                                    rsem(pool, m_in1[u], 2 * 16 * (i + 1), s_go)
                                    rsem(pool, m_T, 2 * (2 * i + u - 1), s_go)
                                    gather(pool, A["x"][:, :], di[u], hb[u][:, :, 0:D], m_g[u])
                                    if not isinstance(i, int):
                                        scat(i - 1, u)
                            steps(pool, step, H)
                            for u in range(2):
                                scat(H - 1, u)
                            for u in range(2):
                                pool.wait_ge(m_sc[u], T * 16 * H)
            end_phase()

        with ExitStack() as c:
            ones = sb("ones", [P, LO], F32, c)
            zero16 = sb("zero16", [P, P], F16, c)
            before = sb("before", [P, G * P], F32, c)
            with nc.Block(no_gpsimd_drain=True) as block:
                @block.vector
                def _(dve):
                    o = Order(dve, s_vo)
                    o.did(nc.vector.memset(ones[:, :], 1.0))
                    o.did(nc.vector.memset(zero16[:, :], 0.0))
                    o.did(nc.vector.memset(before[:, 0:(G - 1) * P], 1.0))
                    o.did(nc.vector.tensor_copy(before[:, (G - 1) * P:], below[:, :]))
                    o.restart()
            sort_by("bysrc", A["src"], pos_s, last_s, None, cnt_s)
            sort_by("bydst", A["dst"], pos_d, last_d, last_d_f, None, messages=True)

        class Shifted:

            def __init__(self, table, base):
                self.table, self.base = table, base

            def __getitem__(self, b):
                return self.table[b + self.base]

        def cols(ap, w):
            return ap.rearrange("p (t a) -> p t a", a=1).to_broadcast([P, ap.shape[1], w])

        def rsqrt(o, dst, src, scr):
            v = nc.vector
            o.did(v.tensor_scalar(scr.bitcast(I32), src.bitcast(I32), 1, None, ALU.arith_shift_right))
            o.done()
            o.did(v.tensor_scalar(dst.bitcast(I32), scr.bitcast(I32), -1.0, float(RSQRT_SEED), ALU.mult, ALU.add))
            o.did(v.tensor_scalar(src, src, -0.5, None, ALU.mult))
            for _ in range(3):
                o.done()
                o.did(v.tensor_tensor(scr, src, dst, ALU.mult))
                o.done()
                o.did(v.tensor_tensor(scr, scr, dst, ALU.mult))
                o.done()
                o.did(v.scalar_tensor_tensor(out=dst, in0=scr, scalar=1.5, in1=dst, op0=ALU.add, op1=ALU.mult))
            o.done()

        def layernorm_start(o, y, sq, st):
            v = nc.vector
            o.did(v.tensor_reduce(st[:, 0, :], y, AX.X, ALU.add))
            o.done()
            o.did(v.tensor_scalar(st[:, 0, :], st[:, 0, :], -1.0 / D, None, ALU.mult))
            o.done()
            o.did(v.tensor_tensor(y, y, cols(st[:, 0, :], D), ALU.add))
            o.done()
            o.did(v.tensor_tensor(sq, y, y, ALU.mult))
            o.done()
            o.did(v.tensor_reduce(st[:, 1, :], sq, AX.X, ALU.add))

        def layernorm_end(o, y, st, dst):
            v = nc.vector
            o.done()
            o.did(v.tensor_scalar(st[:, 1, :], st[:, 1, :], 1.0 / D, EPS_LN, ALU.mult, ALU.add))
            o.done()
            rsqrt(o, st[:, 2, :], st[:, 1, :], st[:, 3, :])
            return v.tensor_tensor(dst, y, cols(st[:, 2, :], D), ALU.mult)

        def before_h(i, u, h):
            return (i, u, 0) if h == 1 else (*before_b(i, u), 1)

        def before_b(i, u):
            return (i, 0) if u == 1 else (i - 1, 1)

        with ExitStack() as c:
            def ft(nm, w=None, dt=F32):
                return sb(f"fs_{nm}", [P, CO] if w is None else [P, CO, w], dt, c)
            ids, ks, pks, sms, dsti = ft("ids", 2), ft("ks"), ft("pks"), ft("sms"), ft("dsti", None, I32)
            t2, cn, deg, inv, isq = ft("t2"), ft("cn"), ft("deg"), ft("inv"), ft("isq")
            s_ld, s_k, s_kw, s_ld2, s_fin, s_w = (sem("fs_loaded"), sem("fs_keys"), sem("fs_keys_stored"), sem("fs_loaded2"),
                                                  sem("fs_done"), sem("fs_stored"))
            with nc.Block(no_gpsimd_drain=True) as block:
                @block.sync
                def _(sp):
                    sp.dma_start(ids[:, :, :], r_rows[0:NP, D:D + 2].rearrange("(p c) w -> p c w", c=CO)).then_inc(s_ld, 16)
                    sp.dma_start(cn[:, :], flat(cnt_s)).then_inc(s_ld, 16)
                    sp.wait_ge(s_k, 1)
                    sp.dma_start(flat(key_sh[1, 1:NP + 1]), ks[:, :]).then_inc(s_kw, 16)
                    sp.wait_ge(s_kw, 16)
                    sp.dma_start(pks[:, :], flat(key_sh[1, 0:NP])).then_inc(s_ld2, 16)
                    sp.wait_ge(s_fin, 1)
                    stores = ((same_s, sms), (dst_s, dsti), (nscale[0], isq), (nscale[1], inv))
                    for dst, src in stores:
                        sp.dma_start(flat(dst), src[:, :]).then_inc(s_w, 16)
                    sp.wait_ge(s_w, 16 * len(stores))

                @block.vector
                def _(dve):
                    v = nc.vector
                    o = Order(dve, s_vo)
                    dve.wait_ge(s_ld, 32)
                    o.did(v.tensor_copy(ks[:, :], ids[:, :, 1:2].rearrange("p c a -> p (c a)")))
                    o.done()
                    dve.sem_inc(s_k, 1)
                    o.did(v.tensor_copy(dsti[:, :], ids[:, :, 0:1].rearrange("p c a -> p (c a)")))
                    o.did(v.tensor_scalar(deg[:, :], cn[:, :], 1.0, None, ALU.add))
                    o.done()
                    o.did(v.tensor_scalar(t2[:, :], deg[:, :], EPS, None, ALU.add))
                    o.done()
                    o.did(v.reciprocal(inv[:, :], t2[:, :]))
                    o.done()
                    o.did(v.tensor_tensor(deg[:, :], deg[:, :], inv[:, :], ALU.mult))
                    o.done()
                    o.did(v.tensor_scalar(cn[:, :], deg[:, :], 0.0, None, ALU.is_gt))
                    o.did(v.tensor_scalar(deg[:, :], deg[:, :], EPS, None, ALU.add))
                    o.done()
                    rsqrt(o, isq[:, :], deg[:, :], t2[:, :])
                    o.did(v.tensor_tensor(isq[:, :], isq[:, :], cn[:, :], ALU.mult))
                    o.done()
                    o.did(v.tensor_tensor(inv[:, :], isq[:, :], inv[:, :], ALU.mult))
                    dve.wait_ge(s_ld2, 16)
                    o.did(v.tensor_tensor(sms[:, :], ks[:, :], pks[:, :], ALU.is_equal))
                    o.restart()
                    dve.sem_inc(s_fin, 1)

        end_phase()

        def tables_by_destination():
            with ExitStack() as c:
                def ft(nm, w=None, dt=F32):
                    return sb(f"fd_{nm}", [P, CO] if w is None else [P, CO, w], dt, c)
                recs, kd, pd, smd, cut = ft("recs", 5), ft("kd"), ft("pd"), ft("smd"), ft("cut")
                srci, wt, t1, t2 = ft("srci", None, I32), ft("wt"), ft("t1"), ft("t2")
                coef = [ft(f"coef{k}", KS) for k in range(2)]
                s_ld, s_k, s_kw, s_ld2, s_fin, s_w = (sem("fd_loaded"), sem("fd_keys"), sem("fd_keys_stored"),
                                                      sem("fd_loaded2"), sem("fd_done"), sem("fd_stored"))
                with nc.Block(no_gpsimd_drain=True) as block:
                    @block.sync
                    def _(sp):
                        sp.dma_start(recs[:, :, :], rec_d[0:NP, :].rearrange("(p c) w -> p c w", c=CO)).then_inc(s_ld, 16)
                        sp.wait_ge(s_k, 1)
                        sp.dma_start(flat(key_sh[0, 1:NP + 1]), kd[:, :]).then_inc(s_kw, 16)
                        sp.wait_ge(s_kw, 16)
                        sp.dma_start(pd[:, :], flat(key_sh[0, 0:NP])).then_inc(s_ld2, 16)
                        sp.wait_ge(s_fin, 1)
                        stores = ((same_d, smd), (cut_d, cut), (src_d, srci), (q_tab[0], srci), (wgt_d, wt))
                        for dst, src in stores:
                            sp.dma_start(flat(dst), src[:, :]).then_inc(s_w, 16)
                        for k in range(2):
                            sp.dma_start(coef_d[k].rearrange("(p c) w -> p c w", c=CO), coef[k][:, :, :]).then_inc(s_w, 16)
                        sp.wait_ge(s_w, 16 * (len(stores) + 2))

                    @block.vector
                    def _(dve):
                        v = nc.vector
                        o = Order(dve, s_vo)
                        dve.wait_ge(s_ld, 16)

                        def col(tile, k):
                            return tile[:, :, k:k + 1].rearrange("p c a -> p (c a)")
                        o.did(v.tensor_copy(kd[:, :], col(recs, 4)))
                        o.done()
                        dve.sem_inc(s_k, 1)
                        o.did(v.tensor_copy(srci[:, :], col(recs, 0)))
                        o.did(v.tensor_copy(wt[:, :], col(recs, 3)))
                        for d in range(2):
                            for k in range(KS):
                                o.done()
                                o.did(v.tensor_scalar(t1[:, :], col(recs, 1 + d), -float(KS - 1), k + 1.0, ALU.mult, ALU.add))
                                o.did(v.tensor_scalar(t2[:, :], col(recs, 1 + d), float(KS - 1), 1.0 - k, ALU.mult, ALU.add))
                                o.done()
                                o.did(v.tensor_tensor(t1[:, :], t1[:, :], t2[:, :], ALU.min))
                                o.done()
                                o.did(v.tensor_scalar(col(coef[d], k), t1[:, :], 0.0, None, ALU.max))
                        dve.wait_ge(s_ld2, 16)
                        o.did(v.tensor_tensor(smd[:, :], kd[:, :], pd[:, :], ALU.is_equal))
                        o.done()
                        o.did(v.tensor_scalar(cut[:, :], smd[:, :], -1.0, -NEG, ALU.add, ALU.mult))
                        o.restart()
                        dve.sem_inc(s_fin, 1)
            end_phase()

        def edge_pass(name, kind, table, width, index, flags, into, sems, T=T, splw=None, rnd=None, records=False):
            BLK = P * T
            NB = NP // BLK
            H = NB // 2
            i0 = 0 if rnd is None else rnd * H
            conv, rd, plain = kind == "conv", kind == "round", kind == "plain"
            with ExitStack() as c:
                def two(nm, shape, dt=F32):
                    return [sb(f"{name}_{nm}{u}", shape, dt, c) for u in range(2)]
                S = sems
                s_ix, s_fl, s_w, s_g, s_st = S["ix"], S["fl"], S["w"], S["g"], S["st"]
                s_T, s_ev, s_scan, s_bk, s_rows, s_mul = S["T"], S["ev"], S["scan"], S["bk"], S["rows"], S["mul"]
                ix = two("ix", [P, T], I32)
                g = two("g", [P, T, width])
                fl = two("fl", [D, BLK])
                sT = two("sT", [D, BLK]) if not rd else [sb(f"{name}_sT", [D, BLK], F32, c)] * 2
                sO = two("sO", [D, BLK])
                rows = two("rows", [P, T, D])
                pT = ps(f"{name}_pT", [D, -(-T // 4) * 4 * P], F32, c)
                pB = [ps(f"{name}_pB{u}", [P, -(-T // 8) * 8, D], F32, c) for u in range(1 if conv else 2)]
                pB = pB * 2 if conv else pB
                msg = g if kind in ("plain", "sum") else two("msg", [P, T, D])
                if conv:
                    co1, co2 = two("co1_", [P, T, KS]), two("co2_", [P, T, KS])
                    z = two("z", [P, T, KS, D])
                    zT = two("zT", [P, 3, P])
                    cmb = two("cmb", [P, KS, D])
                    qf = two("q", [P, T], I32)
                    pZ = [ps(f"{name}_pZ{u}", [P, 3, P], F32, c) for u in range(2)]
                    pU = [ps(f"{name}_pU{u}", [P, KS, D], F32, c) for u in range(2)]
                    s_qst, s_wx = S["qst"], S["wx"]
                    s_z, s_zT, s_ze, s_pu, s_comb, s_q = S["z"], S["zT"], S["ze"], S["pu"], S["comb"], S["q"]
                if rd:
                    wt_ = two("w", [P, T])
                    sq = two("sq", [P, T, D])
                    st = two("st", [P, 5, T])
                    s_sq, s_nrm, s_th = S["sq"], S["nrm"], S["th"]
                if records:
                    rd_, rs_, rp_ = two("r_dst", [P, T], I32), two("r_src", [P, T], I32), two("r_pos", [P, T], I32)
                    ra, rw, rec = two("r_attr", [P, T, 2]), two("r_weight", [P, T]), two("rec", [P, T, 5])
                    s_ri, s_rsc = sem2("record_inputs"), sem2("records_scattered", keep=True)
                    s_rec = sem("records_ready")
                flb = flags.rearrange("(b a n) -> b a n", a=1, n=BLK)
                write_q = conv and width > D

                def ready_rows(eng, ci, u):
                    if plain:
                        eng.wait_ge(s_ix[u], 16 * (ci + 1))
                    else:
                        eng.wait_ge(s_g[u], T * 16 * (ci + 1))

                with nc.Block(no_gpsimd_drain=True) as block:
                    @block.sync
                    def _(sp):
                        def load_ix(b, u):
                            if plain:
                                sp.dma_start(g[u][:, :, :], blocks(table[0:NP, :], T)[b]).then_inc(s_ix[u], 16)
                            else:
                                sp.dma_start(ix[u][:, :], index[b]).then_inc(s_ix[u], 16)

                        def load_fl(b, u):
                            sp.dma_start(fl[u][:, :], flb[b].to_broadcast([D, BLK])).then_inc(s_fl[u], 16)

                        def load_w(b, u):
                            if conv:
                                sp.dma_start(co2[u][:, :, :], blocks(coef_d[1], T)[b]).then_inc(s_w[u], 16)
                            if rd:
                                sp.dma_start(wt_[u][:, :], blocks(wgt_d, T)[b]).then_inc(s_w[u], 16)

                        def load_wx(b, u):
                            sp.dma_start(co1[u][:, :, :], blocks(coef_d[0], T)[b]).then_inc(s_wx[u], 16)

                        def store(i, u):
                            b = 2 * i + u
                            sp.wait_ge(s_rows, b + 2 * i0 + 1)
                            sp.dma_start(into(b), rows[u][:, :, :]).then_inc(s_st[u], 16)
                        def store_q(b, u):
                            sp.wait_ge(s_q, b + 1)
                            sp.dma_start(blocks(q_tab[1], T)[b], qf[u][:, :]).then_inc(s_qst[u], 16)

                        def load_records(b, u):
                            for dst, src in ((rd_[u][:, :], A["dst"]), (rs_[u][:, :], A["src"]), (rp_[u][:, :], pos_d),
                                             (rw[u][:, :], A["ew"]), (ra[u][:, :, :], A["ea2"])):
                                sp.dma_start(dst, blocks(src, T)[b]).then_inc(s_ri[u], 16)

                        if records:
                            load_records(0, 0)
                            load_records(1, 1)
                        for u in range(2):
                            load_ix(u, u)
                            if conv:
                                load_wx(u, u)
                            load_w(u, u)
                            load_fl(u, u)
                        with sp.Fori(0, H - 1) as i:
                            for u in range(2):
                                b = 2 * i + u
                                bb = b + 2 * i0
                                if plain:
                                    sp.wait_ge(s_T, bb + 1)
                                else:
                                    sp.wait_ge(s_g[u], T * 16 * (i + i0 + 1))
                                load_ix(b + 2, u)
                                if write_q:
                                    store_q(b, u)
                                if conv:
                                    sp.wait_ge(s_z, KS * (b + 1))
                                    load_wx(b + 2, u)
                                if conv or rd:
                                    sp.wait_ge(s_mul, bb + 1)
                                    load_w(b + 2, u)
                                if not conv:
                                    sp.wait_ge(s_scan, bb + 1)
                                    load_fl(b + 2, u)
                                    store(i, u)
                                if records:
                                    sp.wait_ge(s_rsc[u], 16 * T * (i + 1))
                                    load_records(b + 2, u)
                        if write_q:
                            for u in range(2):
                                store_q(2 * (H - 1) + u, u)
                            for u in range(2):
                                sp.wait_ge(s_qst[u], 16 * H)
                        if not conv:
                            store(H - 1, 0)
                            store(H - 1, 1)
                        for u in range(2):
                            sp.wait_ge(s_st[u], 16 * (H + i0))
                        sp.sem_inc(s_go, 1)

                    if records:
                        @block.gpsimd
                        def _(pool):
                            def step(i):
                                for u in range(2):
                                    rsem(pool, s_rec, 2 * i + u + 1, s_go)
                                    scatter(pool, rec_d[:, :], rp_[u], rec[u], s_rsc[u])
                            steps(pool, step, H)
                            for u in range(2):
                                pool.wait_ge(s_rsc[u], 16 * T * H)

                    if not plain:
                        @block.gpsimd
                        def _(pool):
                            def step(i):
                                for u in range(2):
                                    rsem(pool, s_ix[u], 16 * (i + i0 + 1), s_go)
                                    if not isinstance(i, int):
                                        if conv:
                                            rsem(pool, s_z, KS * (2 * i + u - 1), s_go)
                                            if write_q:
                                                rsem(pool, s_q, 2 * i + u - 1, s_go)
                                        else:
                                            rsem(pool, s_mul if rd else s_T, 2 * (i + i0) + u - 1, s_go)
                                    gather(pool, table, ix[u], g[u], s_g[u])
                            steps(pool, step, H)

                    @block.tensor
                    def _(pe):
                        t_ = nc.tensor

                        def to_cols(i, u):
                            b = 2 * (i + i0) + u
                            if kind in ("plain", "sum"):
                                ready_rows(pe, i + i0, u)
                            else:
                                pe.wait_ge(s_mul, b + 1)
                            if not (isinstance(i, int) and u == 0):
                                ge(pe, s_ev, b)
                            pe.sem_inc(s_go, 1)
                            for t in range(T):
                                x = t_.transpose(pT[:, t * P:(t + 1) * P], msg[u][:, t, 0:D], ident[:, :])
                            x.then_inc(s_T, 1)

                        def to_rows(i, u):
                            b = 2 * (i + i0) + u
                            pe.wait_ge(s_scan, b + 1)
                            if conv:
                                ge(pe, s_rows, b)
                            elif not isinstance(i, int):
                                pe.wait_ge(s_rows, b - 1)
                            pe.sem_inc(s_go, 1)
                            v3 = sO[u].rearrange("f (p t) -> f t p", t=T)
                            for t in range(T):
                                x = t_.transpose(pB[u][:, t, :], v3[:, t, :], ident[0:D, 0:D])
                            x.then_inc(s_bk, 1)

                        def spread(i, u, t):
                            n = T * (2 * i + u) + t
                            par = (u + t) % 2
                            if t == 0:
                                pe.wait_ge(s_z, KS * (2 * i + u + 1))
                            ge(pe, s_ze, 2 * (n - 1))
                            zr = z[u].rearrange("p t i o -> p t (i o)")
                            for k in range(3):
                                w = min(P, KS * D - k * P)
                                x = t_.transpose(pZ[par][0:w, k, :], zr[:, t, k * P:k * P + w], ident[:, :])
                            x.then_inc(s_zT, 1)

                        def kernelmul(i, u, t):
                            n = T * (2 * i + u) + t
                            par = (u + t) % 2
                            pe.wait_ge(s_ze, 2 * (n + 1))
                            ge(pe, s_comb, n - 1)
                            for k in range(3):
                                w = min(P, KS * D - k * P)
                                x = t_.matmul(pU[par].rearrange("p j o -> p (j o)"), zT[par][0:w, k, :], splw[0:w, k, :],
                                              start=(k == 0), stop=(k == 2))
                            x.then_inc(s_pu, 1)

                        def step(i):
                            for u in range(2):
                                if conv:
                                    first = isinstance(i, int) and u == 0
                                    for t in range(T):
                                        spread(i, u, t)
                                        if t > 0:
                                            kernelmul(i, u, t - 1)
                                        elif not first:
                                            kernelmul(*before_b(i, u), T - 1)
                                        if t == 2 and not first:
                                            to_cols(*before_b(i, u))
                                        if t == 4 and not isinstance(i, int):
                                            to_rows(i - 1, u)
                                else:
                                    to_cols(i, u)
                                    to_rows(i, u)
                        steps(pe, step, H)
                        if conv:
                            kernelmul(H - 1, 1, T - 1)
                            to_cols(H - 1, 1)
                            to_rows(H - 1, 0)
                            to_rows(H - 1, 1)

                    @block.scalar
                    def _(act):
                        a = nc.scalar

                        def copy_cols(i, u):
                            b = 2 * (i + i0) + u
                            act.wait_ge(s_T, b + 1)
                            if rd:
                                if not (isinstance(i, int) and i == 0 and u == 0):
                                    act.wait_ge(s_scan, b)
                            elif not isinstance(i, int):
                                act.wait_ge(s_scan, b - 1)
                            elif conv:
                                ge(act, s_scan, b - 1)
                            a.activation(sT[u].rearrange("f (p t) -> f t p", t=T),
                                         pT[:, 0:T * P].rearrange("f (t p) -> f t p", t=T), ACT.Copy).then_inc(s_ev, 1)

                        def copy_rows(i, u, more=True):
                            b = 2 * (i + i0) + u
                            act.wait_ge(s_bk, b + 1)
                            ge(act, s_st[u], 16 * i)
                            a.activation(rows[u][:, :, :], pB[u][:, 0:T, :], ACT.Copy).then_inc(s_rows, 1)
                            if conv:
                                act.wait_ge(s_rows, b + 1)
                                act.dma_start(into(2 * i + u), rows[u][:, :, :]).then_inc(s_st[u], 16)
                                if more:
                                    act.wait_ge(s_scan, b + 1)
                                    act.dma_start(fl[u][:, :], flb[b + 2].to_broadcast([D, BLK])).then_inc(s_fl[u], 16)

                        def copy_spread(i, u, t):
                            n = T * (2 * i + u) + t
                            par = (u + t) % 2
                            act.wait_ge(s_zT, n + 1)
                            ge(act, s_pu, n - 1)
                            a.activation(zT[par][:, 0:2, :], pZ[par][:, 0:2, :], ACT.Copy).then_inc(s_ze, 1)
                            a.activation(zT[par][0:D, 2, :], pZ[par][0:D, 2, :], ACT.Copy).then_inc(s_ze, 1)

                        def step(i):
                            for u in range(2):
                                b = 2 * (i + i0) + u
                                if conv:
                                    for t in range(T):
                                        copy_spread(i, u, t)
                                        if t == 2 and not (isinstance(i, int) and u == 0):
                                            copy_cols(*before_b(i, u))
                                        if t == 4 and not isinstance(i, int):
                                            copy_rows(i - 1, u)
                                else:
                                    if records:
                                        act.wait_ge(s_ri[u], 5 * 16 * (i + 1))
                                        ge(act, s_rsc[u], 16 * T * i)
                                        a.activation(rec[u][:, :, 0:1], rs_[u].rearrange("p (t a) -> p t a", a=1), ACT.Copy)
                                        a.activation(rec[u][:, :, 1:3], ra[u][:, :, :], ACT.Copy)
                                        a.activation(rec[u][:, :, 3:4], rw[u].rearrange("p (t a) -> p t a", a=1), ACT.Copy)
                                        a.activation(rec[u][:, :, 4:5], rd_[u].rearrange("p (t a) -> p t a", a=1),
                                                     ACT.Copy).then_inc(s_rec, 1)
                                    copy_cols(i, u)
                                    if rd:
                                        act.wait_ge(s_bk, b + 1)
                                        if not isinstance(i, int):
                                            act.wait_ge(s_nrm, b - 1)
                                        a.activation(sq[u][:, :, :], pB[u][:, 0:T, :], ACT.Square).then_inc(s_sq, 1)
                                        act.wait_ge(s_nrm, b + 1)
                                        a.activation(st[u][:, 3, :], st[u][:, 2, :], ACT.Tanh).then_inc(s_th, 1)
                                    else:
                                        copy_rows(i, u)
                        steps(act, step, H)
                        if conv:
                            copy_cols(H - 1, 1)
                            copy_rows(H - 1, 0, more=False)
                            copy_rows(H - 1, 1, more=False)

                    @block.vector
                    def _(dve):
                        v = nc.vector
                        o = Order(dve, s_vo)

                        def run_over(i, u):
                            b = 2 * (i + i0) + u
                            dve.wait_ge(s_ev, b + 1)
                            dve.wait_ge(s_fl[u], 16 * (i + i0 + 1))
                            if not isinstance(i, int) or conv:
                                ge(dve, s_bk, b - 1)
                            first = isinstance(i, int) and i == 0 and u == 0
                            if not first:
                                dve.wait_ge(s_scan, b)
                            v.tensor_tensor_scan(sO[u][:, :], fl[u][:, :], sT[u][:, :],
                                                 (NEG if conv else 0.0) if first else sO[1 - u][:, BLK - 1:BLK],
                                                 op0=ALU.add if conv else ALU.mult,
                                                 op1=ALU.max if conv else ALU.add).then_inc(s_scan, 1)

                        def scale(i, u, k):
                            if k == 0:
                                ready_rows(dve, i, u)
                                dve.wait_ge(s_wx[u], 16 * (i + 1))
                                ge(dve, s_zT, T * (2 * i + u - 1))
                            v.tensor_tensor(z[u][:, :, k, :], g[u][:, :, 0:D],
                                            co1[u][:, :, k:k + 1].to_broadcast([P, T, D]), ALU.mult).then_inc(s_z, 1)

                        def write_sources(i, u):
                            if write_q:
                                ge(dve, s_qst[u], 16 * i)
                                o.did(v.tensor_copy(qf[u].rearrange("p (t a) -> p t a", a=1), g[u][:, :, D:D + 1]))
                                o.done()
                                dve.sem_inc(s_q, 1)

                        def weigh(i, u, t):
                            n = T * (2 * i + u) + t
                            par = (u + t) % 2
                            if t == 0:
                                dve.wait_ge(s_w[u], 16 * (i + 1))
                            dve.wait_ge(s_pu, n + 1)
                            ge(dve, s_cred, n - 1)
                            v.tensor_tensor(cmb[par][:, :, :], pU[par][:, :, :],
                                            co2[u][:, t, :].rearrange("p (j a) -> p j a", a=1)
                                            .to_broadcast([P, KS, D]), ALU.mult).then_inc(s_comb, 1)

                        def sum_up(i, u, t):
                            n = T * (2 * i + u) + t
                            par = (u + t) % 2
                            dve.wait_ge(s_comb, n + 1)
                            if t == 0:
                                ge(dve, s_T, 2 * i + u - 1)
                            v.tensor_reduce(msg[u][:, t, :], cmb[par].rearrange("p j o -> p o j"), AX.X,
                                            ALU.add).then_inc(s_cred, 1)

                        def conv_block(i, u, scale_next, first=False):
                            for t in range(T):
                                weigh(i, u, t)
                                if t > 0:
                                    sum_up(i, u, t - 1)
                                if t < KS and scale_next is not None:
                                    scale(*scale_next, t)
                                if t == KS and not first:
                                    run_over(*before_b(i, u))
                            if write_q and scale_next is not None:
                                write_sources(*scale_next)
                            sum_up(i, u, T - 1)
                            dve.wait_ge(s_cred, T * (2 * i + u + 1))
                            dve.sem_inc(s_mul, 1)

                        def norm(i, u):
                            b = 2 * (i + i0) + u
                            dve.wait_ge(s_sq, b + 1)
                            o.did(v.tensor_reduce(st[u][:, 0, :], sq[u][:, :, :], AX.X, ALU.add))
                            o.done()
                            rsqrt(o, st[u][:, 1, :], st[u][:, 0, :], st[u][:, 2, :])
                            o.did(v.tensor_tensor(st[u][:, 1, :], st[u][:, 0, :], st[u][:, 1, :], ALU.mult))
                            o.done()
                            v.tensor_scalar(st[u][:, 2, :], st[u][:, 1, :], -2.0, EPS, ALU.mult, ALU.add).then_inc(s_nrm, 1)
                            dve.wait_ge(s_nrm, b + 1)
                            o.did(v.reciprocal(st[u][:, 0, :], st[u][:, 2, :]))
                            o.done()
                            dve.wait_ge(s_th, b + 1)
                            o.did(v.tensor_tensor(st[u][:, 4, :], st[u][:, 0, :], st[u][:, 3, :], ALU.mult))
                            o.done()
                            if not (isinstance(i, int) and i == 0):
                                dve.wait_ge(s_st[u], 16 * (i + i0))
                            v.tensor_tensor(rows[u][:, :, :], pB[u][:, 0:T, :], cols(st[u][:, 4, :], D), ALU.mult).then_inc(s_rows, 1)
                            dve.wait_ge(s_rows, b + 1)
                            zb = Z[:, bass.ds((2 * i + u) * T * D, T * D)]
                            o.did(v.scalar_tensor_tensor(out=zb, in0=rows[u].rearrange("p t w -> p (t w)"), scalar=mwl[:, :],
                                                         in1=zb, op0=ALU.mult, op1=ALU.add))

                        if rd:
                            o.did(v.tensor_copy(mwl[:, :], mwB[:, bass.ds(rnd + 1, 1)]))
                            o.restart()
                        if conv:
                            s_cred = S["cred"]
                            for k in range(KS):
                                scale(0, 0, k)
                            if write_q:
                                write_sources(0, 0)

                        def step(i):
                            for u in range(2):
                                b = 2 * (i + i0) + u
                                first = isinstance(i, int) and u == 0
                                if conv:
                                    conv_block(i, u, (i, 1) if u == 0 else (i + 1, 0), first)
                                else:
                                    if rd:
                                        ready_rows(dve, i + i0, u)
                                        dve.wait_ge(s_w[u], 16 * (i + i0 + 1))
                                        if not isinstance(i, int):
                                            dve.wait_ge(s_T, b - 1)
                                        v.tensor_tensor(msg[u][:, :, :], g[u][:, :, :], cols(wt_[u][:, :], D),
                                                        ALU.mult).then_inc(s_mul, 1)
                                        if not first:
                                            norm(*before_b(i, u))
                                    run_over(i, u)
                            if rd or write_q:
                                o.restart()
                        if conv:
                            steps(dve, step, H - 1)
                            conv_block(H - 1, 0, (H - 1, 1))
                            conv_block(H - 1, 1, None)
                            run_over(H - 1, 1)
                            if write_q:
                                o.restart()
                        else:
                            steps(dve, step, H)
                            if rd:
                                norm(H - 1, 1)
                                o.restart()

        def edge_semaphores(name, kind):
            S = {k: sem2(f"{name}_{k}_") for k in ("ix", "fl", "w", "st")}
            S["g"] = sem2(f"{name}_g_", keep=True)
            S.update({k: sem(f"{name}_{k}") for k in ("T", "ev", "scan", "bk", "rows", "mul")})
            if kind == "conv":
                S.update({k: sem(f"{name}_{k}") for k in ("z", "zT", "ze", "pu", "comb", "q", "cred")})
                S["qst"], S["wx"] = sem2(f"{name}_qst_"), sem2(f"{name}_wx_")
            if kind == "round":
                S.update({k: sem(f"{name}_{k}") for k in ("sq", "nrm", "th")})
            return S
        def node_pass(name, table, index, loads, into):
            mats = name in ("net0", "conv1", "conv2")
            second = name in ("net0", "conv2")
            BLKN = P * TN
            NBN = NP // BLKN
            HN = NBN // 2
            with ExitStack() as c:
                def two(nm, shape, dt=F32):
                    return [sb(f"n_{name}_{nm}{u}", shape, dt, c) for u in range(2)]
                s_ix, s_in, s_late, s_st = [sem2(f"n_{name}_{x}") for x in ("index", "inputs", "late_inputs", "stored")]
                s_g = sem2(f"n_{name}_gathered", keep=True)
                s_one = sem(f"n_{name}_ones")
                s_mean, s_T1, s_e1, s_m1, s_used, s_read1, s_r, s_T2, s_e2, s_m2, s_y, s_fin = [
                    sem(f"n_{name}_{x}") for x in ("means", "transposed1", "copied1", "multiplied1", "rows_used", "product1_used",
                                                   "relu", "transposed2", "copied2", "multiplied2", "summed", "finished")]
                ix = two("ix", [P, TN], I32)
                ga = two("ga", [P, TN, D])
                buf = {"o": two("o", [P, TN, D + 1 if name == "net0" else D])}
                widths = {"hb": 2 * D, "xr": D, "yr": D}
                early = [x for x in loads if x[0] not in ("y", "ldf")]
                late = [x for x in loads if x[0] in ("y", "ldf")]
                for k in sorted({x[0] for x in loads} - {"y"}):
                    buf[k] = two(k, [P, TN, widths[k]] if k in widths else [P, TN])
                if name == "z":
                    buf["o2"] = two("o2", [P, TN, D])
                y = buf["y"] = two("y", [P, TN, D])
                sq = sb(f"n_{name}_sq", [P, TN, D], F32, c)
                st = sb(f"n_{name}_st", [P, 4, TN], F32, c)
                mean = sb(f"n_{name}_mean", [P, 2, TN], F32, c)
                k1 = 2 * D if name != "conv1" else D
                n1 = 2 * D if name == "conv2" else D
                if mats:
                    if name == "net0":
                        has = two("has", [P, 2, T + 1])
                        hasT = sb(f"n_{name}_hasT", [T + 1, 2, P], F32, c)
                    k1b = k1 + 1 if name == "conv1" else k1
                    x1T = sb(f"n_{name}_x1T", [k1b, 2, T * P], F32, c)
                    bufs = 1 if second else 2
                    pT = [ps(f"n_{name}_pT{h}", [P, 8 * P], F32, c) for h in range(bufs)] * (3 - bufs)
                    pU = [ps(f"n_{name}_pU{h}", [P, 8, n1], F32, c) for h in range(bufs)] * (3 - bufs)
                    w1, w2 = {"net0": (Wcat, W2b), "conv1": (root1, None), "conv2": (R2F, F2)}[name]
                    t2 = [sb(f"n_{name}_t2_{h}", [P, T, D], F32, c) for h in range(2)]
                if second:
                    x2T = sb(f"n_{name}_x2T", [D + 1, 2, T * P], F32, c)
                    pT2 = ps(f"n_{name}_pT2", [D, 8 * P], F32, c)
                    pU2 = [ps(f"n_{name}_pU2_{h}", [P, 8, D], F32, c) for h in range(2)]
                if name == "conv2":
                    t1 = [sb(f"n_{name}_t1_{h}", [P, T, D], F32, c) for h in range(2)]

                def half(h):
                    return slice(h * T, (h + 1) * T)

                with nc.Block(no_gpsimd_drain=True) as block:
                    @block.sync
                    def _(sp):
                        def load_in(b, u, which, s):
                            for k, src, cut in which:
                                dst = buf[k][u]
                                dst = dst[:, :] if len(dst.shape) == 2 else dst[:, :, cut or slice(0, D)]
                                sp.dma_start(dst, src(b)).then_inc(s[u], 16)

                        def store(b, u):
                            sp.wait_ge(s_fin, b + 1)
                            for k, dst in into:
                                sp.dma_start(dst(b), buf[k][u][:, :, :]).then_inc(s_st[u], 16)
                        for u in range(2):
                            sp.dma_start(ix[u][:, :], index[u]).then_inc(s_ix[u], 16)
                            load_in(u, u, early, s_in)
                            load_in(u, u, late, s_late)
                        with sp.Fori(0, HN - 1) as i:
                            for u in range(2):
                                b = 2 * i + u
                                if second:
                                    sp.wait_ge(s_m1, 2 * (b + 1))
                                    if name == "conv2":
                                        sp.wait_ge(s_read1, 2 * (b + 1))
                                    load_in(b + 2, u, early, s_in)
                                    store(b, u)
                                    load_in(b + 2, u, late, s_late)
                                else:
                                    sp.wait_ge(s_g[u], TN * 16 * (i + 1))
                                    sp.dma_start(ix[u][:, :], index[b + 2]).then_inc(s_ix[u], 16)
                                    store(b, u)
                                    load_in(b + 2, u, early, s_in)
                        for u in range(2):
                            store(2 * (HN - 1) + u, u)
                        for u in range(2):
                            sp.wait_ge(s_st[u], 16 * len(into) * HN)

                    @block.gpsimd
                    def _(pool):
                        def step(i):
                            for u in range(2):
                                rsem(pool, s_ix[u], 16 * (i + 1), s_go)
                                rsem(pool, s_used, 2 * i + u - 1, s_go)
                                gather(pool, table, ix[u], ga[u], s_g[u])
                        steps(pool, step, HN)

                    if mats:
                        @block.tensor
                        def _(pe):
                            t_ = nc.tensor
                            pe.wait_ge(s_one, 1)

                            def first(i, u, h):
                                n = 2 * (2 * i + u) + h
                                if h == 0:
                                    pe.wait_ge(s_in[u], 16 * len(early) * (i + 1))
                                    if name == "net0":
                                        pe.wait_ge(s_mean, 2 * i + u + 1)
                                ge(pe, s_e1, n if second else n - 1)
                                pe.sem_inc(s_go, 1)
                                src = buf["hb"][u] if "hb" in buf else buf["xr"][u]
                                if name == "net0":
                                    t_.transpose(pT[h][0:T + 1, T * P:(T + 1) * P], has[u][:, h, :], ident[:, :])
                                for t in range(T):
                                    x = t_.transpose(pT[h][0:k1, t * P:(t + 1) * P], src[:, h * T + t, 0:k1], ident[:, :])
                                x.then_inc(s_T1, 1)

                            def product1(i, u, h):
                                n = 2 * (2 * i + u) + h
                                pe.wait_ge(s_e1, n + 1)
                                if second:
                                    ge(pe, s_r if name == "net0" else s_read1, n)
                                else:
                                    ge(pe, s_read1, n - 1)
                                if name == "net0":
                                    t_.matmul(pU[h][:, 0:T, :].rearrange("p t n -> p (t n)"), hasT[:, h, :],
                                              net0_bias.rearrange("a t n -> a (t n)"), start=True, stop=False)
                                    for t in range(T):
                                        x = t_.matmul(pU[h][:, t, :], x1T[:, h, t * P:(t + 1) * P], w1[:, :], start=False,
                                                      stop=(t == T - 1))
                                else:
                                    for t in range(T):
                                        x = t_.matmul(pU[h][:, t, :], x1T[:, h, t * P:(t + 1) * P], w1[:, :], start=True,
                                                      stop=name == "conv1")
                                        if name == "conv2":
                                            x = t_.matmul(pU[h][:, t, 0:D], ones_row[0:1, :], sb2_row[:, :], start=False,
                                                          stop=True)
                                x.then_inc(s_m1, 1)

                            def columns2(i, u, h):
                                n = 2 * (2 * i + u) + h
                                pe.wait_ge(s_r, n + 1)
                                ge(pe, s_e2, n)
                                pe.sem_inc(s_go, 1)
                                for t in range(T):
                                    x = t_.transpose(pT2[:, t * P:(t + 1) * P], t2[h][:, t, :], ident[:, :])
                                x.then_inc(s_T2, 1)

                            def product2(i, u, h):
                                n = 2 * (2 * i + u) + h
                                pe.wait_ge(s_e2, n + 1)
                                ge(pe, s_y, n - 1)
                                for t in range(T):
                                    x = t_.matmul(pU2[h][:, t, :], x2T[:, h, t * P:(t + 1) * P], w2[:, :],
                                                  start=True, stop=True)
                                x.then_inc(s_m2, 1)

                            def step(i):
                                for u in range(2):
                                    if not second:
                                        first(i, u, 0)
                                        first(i, u, 1)
                                        product1(i, u, 0)
                                        product1(i, u, 1)
                                        continue
                                    for h in range(2):
                                        start = isinstance(i, int) and u == 0 and h == 0
                                        first(i, u, h)
                                        if not start:
                                            columns2(*before_h(i, u, h))
                                        product1(i, u, h)
                                        if not start:
                                            product2(*before_h(i, u, h))
                            steps(pe, step, HN)
                            if second:
                                columns2(HN - 1, 1, 1)
                                product2(HN - 1, 1, 1)

                        @block.scalar
                        def _(act):
                            a = nc.scalar

                            def copy1(i, u, h):
                                n = 2 * (2 * i + u) + h
                                act.wait_ge(s_T1, n + 1)
                                ge(act, s_m1, n - 1)
                                if name == "net0":
                                    a.activation(hasT[:, h, :], pT[h][0:T + 1, T * P:(T + 1) * P], ACT.Copy)
                                a.activation(x1T[0:k1, h, :], pT[h][0:k1, 0:T * P], ACT.Copy).then_inc(s_e1, 1)

                            def hidden(i, u, h):
                                n = 2 * (2 * i + u) + h
                                act.wait_ge(s_m1 if name == "net0" else s_read1, n + 1)
                                ge(act, s_T2, n - 1)
                                a.activation(t2[h][:, :, :], pU[h][:, 0:T, 0:D] if name == "net0" else t1[h][:, :, :],
                                             ACT.Relu).then_inc(s_r, 1)

                            def copy2(i, u, h):
                                n = 2 * (2 * i + u) + h
                                act.wait_ge(s_T2, n + 1)
                                ge(act, s_m2, n - 1)
                                a.activation(x2T[0:D, h, :], pT2[:, 0:T * P], ACT.Copy).then_inc(s_e2, 1)

                            def step(i, more=True):
                                for u in range(2):
                                    if not second:
                                        copy1(i, u, 0)
                                        copy1(i, u, 1)
                                        for h in range(2):
                                            act.wait_ge(s_read1, 2 * (2 * i + u) + h + 1)
                                        ge(act, s_st[u], 16 * len(into) * i)
                                        a.activation(buf["o"][u][:, :, :], y[u][:, :, :], ACT.Relu).then_inc(s_fin, 1)
                                        continue
                                    if more:
                                        act.wait_ge(s_g[u], TN * 16 * (i + 1))
                                        act.dma_start(ix[u][:, :], index[2 * i + u + 2]).then_inc(s_ix[u], 16)
                                    for h in range(2):
                                        copy1(i, u, h)
                                        if not (isinstance(i, int) and i == 0 and u == 0 and h == 0):
                                            copy2(*before_h(i, u, h))
                                        hidden(i, u, h)
                            if second:
                                steps(act, step, HN - 1)
                                step(HN - 1, more=False)
                                copy2(HN - 1, 1, 1)
                            else:
                                steps(act, step, HN)

                    @block.vector
                    def _(dve):
                        v = nc.vector
                        o = Order(dve, s_vo)
                        if mats:
                            o.did(v.memset((x2T if second else x1T)[D:D + 1, :, :], 1.0))
                            if name == "net0":
                                for u in range(2):
                                    o.did(v.memset(has[u][:, :, T:T + 1], 1.0))
                            o.restart()
                            dve.sem_inc(s_one, 1)

                        def arrived(i, u):
                            dve.wait_ge(s_g[u], TN * 16 * (i + 1))
                            dve.wait_ge(s_in[u], 16 * len(early) * (i + 1))

                        def means(i, u):
                            arrived(i, u)
                            cn = buf["cnt"][u]
                            o.done()
                            o.did(v.tensor_scalar(mean[:, 0, :], cn[:, :], 1.0, None, ALU.max))
                            o.done()
                            o.did(v.tensor_scalar(has[u][:, :, 0:T], cn.rearrange("p (h t) -> p h t", h=2), 1.0, None, ALU.min))
                            o.did(v.reciprocal(mean[:, 1, :], mean[:, 0, :]))
                            o.done()
                            v.tensor_tensor(buf["hb"][u][:, :, D:2 * D], ga[u][:, :, :], cols(mean[:, 1, :], D),
                                            ALU.mult).then_inc(s_mean, 1)
                            dve.wait_ge(s_mean, 2 * i + u + 1)
                            dve.sem_inc(s_used, 1)

                        def use1(i, u, h):
                            n = 2 * (2 * i + u) + h
                            if h == 0:
                                arrived(i, u)
                            dve.wait_ge(s_m1, n + 1)
                            if name == "conv1":
                                if h == 0:
                                    ge(dve, s_fin, 2 * i + u - 1)
                                v.tensor_tensor(y[u][:, half(h), :], ga[u][:, half(h), :], pU[h][:, 0:T, 0:D],
                                                ALU.add).then_inc(s_read1, 1)
                                dve.wait_ge(s_read1, n + 1)
                            else:
                                ge(dve, s_r, n - 1)
                                o.did(v.tensor_tensor(y[u][:, half(h), :], buf["hb"][u][:, half(h), 0:D], pU[h][:, 0:T, D:2 * D],
                                                      ALU.add))
                                v.tensor_tensor(t1[h][:, :, :], ga[u][:, half(h), :], pU[h][:, 0:T, 0:D],
                                                ALU.add).then_inc(s_read1, 1)
                                dve.wait_ge(s_read1, n + 1)
                            if h == 1:
                                dve.sem_inc(s_used, 1)

                        def use2(i, u, h):
                            n = 2 * (2 * i + u) + h
                            dve.wait_ge(s_m2, n + 1)
                            if late and h == 0:
                                dve.wait_ge(s_late[u], 16 * len(late) * (i + 1))
                            o.done()
                            v.tensor_tensor(y[u][:, half(h), :], y[u][:, half(h), :], pU2[h][:, 0:T, :],
                                            ALU.add).then_inc(s_y, 1)

                        def combine(i, u):
                            yy, xr, g_ = y[u][:, :, :], buf["xr"][u], ga[u]
                            arrived(i, u)
                            if name == "z":
                                o.did(v.scalar_tensor_tensor(out=y[u].rearrange("p t w -> p (t w)"),
                                                             in0=xr.rearrange("p t w -> p (t w)"), scalar=mwB[:, 0:1],
                                                             in1=g_.rearrange("p t w -> p (t w)"), op0=ALU.mult, op1=ALU.add))
                            else:
                                o.did(v.tensor_tensor(yy, g_[:, :, :], buf["yr"][u][:, :, :], ALU.add))
                                o.done()
                                o.did(v.tensor_tensor(yy, yy, cols(buf["sc"][u][:, :], D), ALU.mult))
                            o.done()
                            dve.sem_inc(s_used, 1)
                            o.did(v.tensor_tensor(yy, yy, xr[:, :, :], ALU.add))

                        def norm_start(i, u):
                            if second:
                                dve.wait_ge(s_y, 2 * (2 * i + u + 1))
                            o.done()
                            layernorm_start(o, y[u][:, :, :], sq[:, :, :], st)

                        def norm_end(i, u):
                            if not (isinstance(i, int) and i == 0):
                                dve.wait_ge(s_st[u], 16 * len(into) * i)
                            o.did(layernorm_end(o, y[u][:, :, :], st, buf["o"][u][:, :, 0:D]))
                            if name == "net0":
                                o.did(v.tensor_copy(buf["o"][u][:, :, D:D + 1], buf["ldf"][u].rearrange("p (t a) -> p t a", a=1)))
                            o.done()
                            if name == "z":
                                o.did(v.tensor_tensor(buf["o2"][u][:, :, :], buf["o"][u][:, :, :], cols(buf["sc"][u][:, :], D),
                                                      ALU.mult))
                                o.done()
                            dve.sem_inc(s_fin, 1)

                        def step(i, more=True):
                            for u in range(2):
                                first = isinstance(i, int) and i == 0 and u == 0
                                if name == "net0":
                                    if u == 0:
                                        means(i, 1)
                                    elif more:
                                        means(i + 1, 0)
                                    if not first:
                                        use2(*before_h(i, u, 0))
                                        norm_start(*before_b(i, u))
                                        norm_end(*before_b(i, u))
                                    use2(i, u, 0)
                                if name == "conv2":
                                    use1(i, u, 0)
                                    if not first:
                                        use2(*before_h(i, u, 0))
                                        norm_start(*before_b(i, u))
                                    use1(i, u, 1)
                                    if not first:
                                        norm_end(*before_b(i, u))
                                    use2(i, u, 0)
                                if name == "conv1":
                                    use1(i, u, 0)
                                    use1(i, u, 1)
                                if not mats:
                                    combine(i, u)
                                    norm_start(i, u)
                                    norm_end(i, u)
                            o.restart()
                        if second:
                            if name == "net0":
                                means(0, 0)
                            steps(dve, step, HN - 1)
                            step(HN - 1, more=False)
                            use2(HN - 1, 1, 1)
                            norm_start(HN - 1, 1)
                            norm_end(HN - 1, 1)
                            o.restart()
                        else:
                            steps(dve, step, HN)
            end_phase()

        idx_src_d, idx_dst_s = blocks(src_d), blocks(dst_s)
        edge_pass("sum0", "plain", r_rows, D + 2, None, same_s, lambda b: blocks(sum_s[0:NP, :])[b],
                  edge_semaphores("sum0", "plain"), records=True)
        end_phase()
        tables_by_destination()
        node_pass("net0", sum_s[:, :], blocks(last_s, TN),
                  [("hb", lambda b: blocks(A["x"], TN)[b], slice(0, D)), ("cnt", lambda b: blocks(cnt_s, TN)[b], None),
                   ("y", lambda b: blocks(A["x"], TN)[b], None), ("ldf", lambda b: blocks(last_d_f, TN)[b], None)],
                  [("o", lambda b: blocks(x1_rows, TN)[b])])
        edge_pass("conv1", "conv", x1_rows[:, :], D + 1, idx_src_d, cut_d, lambda b: blocks(mx_rows[0:NP, :])[b],
                  edge_semaphores("conv1", "conv"), splw=spl[0])
        end_phase()
        node_pass("conv1", mx_rows[:, :], blocks(last_d, TN), [("xr", lambda b: blocks(x1_rows, TN)[b][:, :, 0:D], slice(0, D))],
                  [("o", lambda b: blocks(y1_rows, TN)[b])])
        edge_pass("conv2", "conv", y1_rows[:, :], D, idx_src_d, cut_d, lambda b: blocks(mx_rows[0:NP, :])[b],
                  edge_semaphores("conv2", "conv"), splw=spl[1])
        end_phase()
        node_pass("conv2", mx_rows[:, :], blocks(last_d, TN),
                  [("hb", lambda b: blocks(x1_rows, TN)[b][:, :, 0:D], slice(0, D)), ("hb", lambda b: blocks(y1_rows, TN)[b], slice(D, 2 * D))],
                  [("o", lambda b: blocks(h_tab[0][0:NP, :], TN)[b]), ("o", lambda b: blocks(x2_rows, TN)[b])])

        with ExitStack() as c:
            Z = sb("Z", [P, CO * D], F32, c)
            s_zz = sem("z_stored")
            with nc.Block(no_gpsimd_drain=True) as block:
                @block.vector
                def _(dve):
                    o = Order(dve, s_vo)
                    o.did(nc.vector.memset(Z[:, :], 0.0))
                    o.restart()

            q_blocks = blocks(q_tab.rearrange("k n -> (k n)"), TR)
            round_sems = edge_semaphores("round", "round")
            with nc.Fori(0, NL // 2) as pair:
                for half in range(2):
                    r = pair * 2 + half
                    later = (pair + NL - 1) // NL if half == 0 else 1
                    edge_pass(f"round{half}", "round", h_tab[half][:, :], D, Shifted(q_blocks, later * (NP // (P * TR))),
                              same_d, lambda b: blocks(h_tab[1 - half][0:NP, :], TR)[b], round_sems, T=TR, rnd=r)
            with nc.Block(no_gpsimd_drain=True) as block:
                @block.sync
                def _(sp):
                    sp.dma_start(z_rows[0:NP, :].rearrange("(b p t) w -> p b (t w)", p=P, t=TR),
                                 Z[:, :].rearrange("p (b n) -> p b n", n=TR * D)).then_inc(s_zz, 16)
                    sp.wait_ge(s_zz, 16)
        end_phase()
        node_pass("z", z_rows[:, :], blocks(last_d, TN),
                  [("xr", lambda b: blocks(x2_rows, TN)[b], slice(0, D)), ("sc", lambda b: blocks(nscale[0], TN)[b], None)],
                  [("o", lambda b: blocks(x3_rows, TN)[b]), ("o2", lambda b: blocks(y3_rows, TN)[b])])
        edge_pass("sum3", "sum", y3_rows[:, :], D, idx_dst_s, same_s, lambda b: blocks(sum_s[0:NP, :])[b],
                  edge_semaphores("sum3", "sum"))
        end_phase()
        node_pass("out", sum_s[:, :], blocks(last_s, TN),
                  [("xr", lambda b: blocks(x3_rows, TN)[b], slice(0, D)), ("yr", lambda b: blocks(y3_rows, TN)[b], slice(0, D)),
                   ("sc", lambda b: blocks(nscale[1], TN)[b], None)],
                  [("o", lambda b: blocks(out, TN)[b])])


_INS = {'x': 'x', 'src': 'src', 'dst': 'dst', 'edge_attr_2': 'ea2', 'edge_attr_64': 'ea64', 'edge_weight': 'ew',
        'L0_gnn_W1a': 'W1a', 'L0_gnn_b1a': 'b1a', 'L0_gnn_W1b': 'W1b', 'L0_gnn_b1b': 'b1b', 'L0_gnn_W2a': 'W2a',
        'L0_gnn_b2a': 'b2a', 'L0_gnn_W2b': 'W2b', 'L0_gnn_b2b': 'b2b', 'L1_gnn_W1': 'W1', 'L1_gnn_root1': 'root1',
        'L1_gnn_b1': 'sb1', 'L1_gnn_W2': 'W2', 'L1_gnn_root2': 'root2', 'L1_gnn_b2': 'sb2',
        'L1_gnn_final_w': 'final_w', 'L1_gnn_final_b': 'final_b', 'L2_gnn_manifold_weights': 'mw'}


def kernel(**inputs):
    import numpy as _np
    import concourse.bacc as _bacc
    from concourse import mybir as _mybir
    from concourse.bass_utils import run_bass_kernel_spmd as _run

    nc = _bacc.Bacc("TRN2", target_bir_lowering=False, num_devices=1)
    arrays, args = {}, {}
    for name, short in _INS.items():
        a = _np.ascontiguousarray(inputs[name])
        if a.shape[0] == N:
            pad = _np.full((NP,) + a.shape[1:], N if a.dtype.kind in "iu" else 0, a.dtype)
            pad[:N] = a
            a = pad
        arrays[f"in_{short}"] = a
        args[short] = nc.dram_tensor(f"in_{short}", a.shape, _mybir.dt.from_np(a.dtype), kind="ExternalInput").ap()
    out = nc.dram_tensor("out_0", (NP, D), F32, kind="ExternalOutput").ap()
    program(nc, args, out)
    r = _run(nc, [arrays], core_ids=[0])
    return r.results[0]["out_0"][:N]
```
